# Optimizing a Trainium2 kernel written in Bass

```python
import numpy as np
import jax
import jax.numpy as jnp

def _softmax(x, axis=-1):
    return jax.nn.softmax(x, axis=axis)

def _gelu(x):
    return jax.nn.gelu(x, approximate=True)

def _silu(x):
    return jax.nn.silu(x)

def _sigmoid(x):
    return jax.nn.sigmoid(x)

def _layernorm(x, axis=-1, eps=1e-05):
    m = jnp.mean(x, axis=axis, keepdims=True)
    v = jnp.var(x, axis=axis, keepdims=True)
    return (x - m) / jnp.sqrt(v + eps)

def _scatter_add(tgt, idx, src, axis=0):
    return tgt.at[idx].add(src)

def _segment_sum(src, seg, n):
    return jax.ops.segment_sum(src, seg, n)
kernel_name = 'mk_audio_tower_d1_tok_audfeat256_r4_925321'

def setup_inputs(seed: int=0):
    np.random.seed(seed)
    _w = jnp.asarray

    def _rec_inputs():
        import jax
        import jax.numpy as jnp
        _rk = jax.random.key(seed)
        x = -7.10856e-05 + 0.999911 * jax.random.normal(jax.random.fold_in(_rk, 1), (128, 64, 750), jnp.float32)
        return x
    x = _rec_inputs()

    def _L0_tok_setup():
        import jax, jax.numpy as jnp
        import numpy as np
        KERNEL_SIZE = 8
        key = jax.random.key(seed)
        k1, k2 = jax.random.split(key)
        B, F, T = (16, 64, 4096)
        x = jax.random.normal(k1, (B, F, T), dtype=jnp.float32)
        w = jax.random.normal(k2, (1, F), dtype=jnp.float32) * 0.05
        b = jnp.zeros((1,), dtype=jnp.float32)
        return {'x': x, 'w': w, 'b': b}
    _L0_tok_all = _L0_tok_setup()
    _L0_tok_in = {k: v for k, v in _L0_tok_all.items() if k in ('w', 'b')}
    del _L0_tok_all

    def _L0_attn_setup():
        import jax, jax.numpy as jnp
        import numpy as np
        B, N, C, H = (4, 256, 64, 8)
        HD = C // H
        BN_EPS = 1e-05
        key = jax.random.key(seed)
        ks = jax.random.split(key, 6)

        def w(k, shape, sc=0.02):
            return jax.random.normal(k, shape, jnp.float32) * sc
        return {'x': jax.random.normal(ks[0], (B, N, C), jnp.float32), 'w_qkv': w(ks[1], (3 * C, C)), 'b_qkv': jnp.zeros((3 * C,), jnp.float32), 'w_proj': w(ks[2], (C, C)), 'b_proj': jnp.zeros((C,), jnp.float32), 'scale': jnp.float32(HD ** (-0.5)), 'riem_scale': jnp.float32(HD ** (-0.5)), 'grassman_scale': jnp.float32(HD ** (-0.5)), 'bn_gamma': jnp.ones((3 * H,), jnp.float32), 'bn_beta': jnp.zeros((3 * H,), jnp.float32), 'bn_mean': jnp.zeros((3 * H,), jnp.float32), 'bn_var': jnp.ones((3 * H,), jnp.float32), 'conv_w': w(ks[3], (H, 3 * H)), 'conv_b': jnp.zeros((H,), jnp.float32)}
    _L0_attn_all = _L0_attn_setup()
    _L0_attn_in = {k: v for k, v in _L0_attn_all.items() if k in ('w_qkv', 'b_qkv', 'w_proj', 'b_proj', 'scale', 'riem_scale', 'grassman_scale', 'bn_gamma', 'bn_beta', 'bn_mean', 'bn_var', 'conv_w', 'conv_b')}
    del _L0_attn_all

    def _L0_ffn_setup():
        import jax, jax.numpy as jnp
        import numpy as np
        B, T, IN_DIM = (64, 64, 64)
        HID, OUT_DIM = (128, 64)
        N_LAYERS, N_EXPERTS, N_SHARED = (2, 16, 1)
        key = jax.random.key(seed)
        ks = jax.random.split(key, 10)
        s = 0.02
        x = jax.random.normal(ks[0], (B, T, IN_DIM), dtype=jnp.float32)
        route_id = jax.random.randint(ks[1], (B,), 0, N_EXPERTS)
        Wi = jax.random.normal(ks[2], (HID, IN_DIM), dtype=jnp.float32) * s
        bi = jnp.zeros((HID,), dtype=jnp.float32)
        Wr = jax.random.normal(ks[3], (N_LAYERS, N_EXPERTS, HID, HID), dtype=jnp.float32) * s
        br = jax.random.normal(ks[4], (N_LAYERS, N_EXPERTS, HID), dtype=jnp.float32) * s
        Ws = jax.random.normal(ks[5], (N_LAYERS, N_SHARED, HID, HID), dtype=jnp.float32) * s
        bs = jax.random.normal(ks[6], (N_LAYERS, N_SHARED, HID), dtype=jnp.float32) * s
        Wo = jax.random.normal(ks[7], (OUT_DIM, HID), dtype=jnp.float32) * s
        bo = jnp.zeros((OUT_DIM,), dtype=jnp.float32)
        return {'x': x, 'route_id': route_id, 'Wi': Wi, 'bi': bi, 'Wr': Wr, 'br': br, 'Ws': Ws, 'bs': bs, 'Wo': Wo, 'bo': bo}
    _L0_ffn_all = _L0_ffn_setup()
    _L0_ffn_in = {k: v for k, v in _L0_ffn_all.items() if k in ('route_id', 'Wi', 'bi', 'Wr', 'br', 'Ws', 'bs', 'Wo', 'bo')}
    del _L0_ffn_all
    return {'x': x, 'L0_tok_w': _L0_tok_in['w'], 'L0_tok_b': _L0_tok_in['b'], 'L0_attn_w_qkv': _L0_attn_in['w_qkv'], 'L0_attn_b_qkv': _L0_attn_in['b_qkv'], 'L0_attn_w_proj': _L0_attn_in['w_proj'], 'L0_attn_b_proj': _L0_attn_in['b_proj'], 'L0_attn_scale': _L0_attn_in['scale'], 'L0_attn_riem_scale': _L0_attn_in['riem_scale'], 'L0_attn_grassman_scale': _L0_attn_in['grassman_scale'], 'L0_attn_bn_gamma': _L0_attn_in['bn_gamma'], 'L0_attn_bn_beta': _L0_attn_in['bn_beta'], 'L0_attn_bn_mean': _L0_attn_in['bn_mean'], 'L0_attn_bn_var': _L0_attn_in['bn_var'], 'L0_attn_conv_w': _L0_attn_in['conv_w'], 'L0_attn_conv_b': _L0_attn_in['conv_b'], 'L0_ffn_route_id': _L0_ffn_in['route_id'], 'L0_ffn_Wi': _L0_ffn_in['Wi'], 'L0_ffn_bi': _L0_ffn_in['bi'], 'L0_ffn_Wr': _L0_ffn_in['Wr'], 'L0_ffn_br': _L0_ffn_in['br'], 'L0_ffn_Ws': _L0_ffn_in['Ws'], 'L0_ffn_bs': _L0_ffn_in['bs'], 'L0_ffn_Wo': _L0_ffn_in['Wo'], 'L0_ffn_bo': _L0_ffn_in['bo']}

def reference(x, L0_tok_w, L0_tok_b, L0_attn_w_qkv, L0_attn_b_qkv, L0_attn_w_proj, L0_attn_b_proj, L0_attn_scale, L0_attn_riem_scale, L0_attn_grassman_scale, L0_attn_bn_gamma, L0_attn_bn_beta, L0_attn_bn_mean, L0_attn_bn_var, L0_attn_conv_w, L0_attn_conv_b, L0_ffn_route_id, L0_ffn_Wi, L0_ffn_bi, L0_ffn_Wr, L0_ffn_br, L0_ffn_Ws, L0_ffn_bs, L0_ffn_Wo, L0_ffn_bo):
    import jax
    import jax.numpy as jnp

    def _L0_tok_ref(x, w, b):
        import jax, jax.numpy as jnp
        import numpy as np
        KERNEL_SIZE = 8
        k = KERNEL_SIZE
        B, F, T = x.shape
        pad = -T % k
        if pad:
            x = jnp.pad(x, ((0, 0), (0, 0), (0, pad)))
            T += pad
        nw = T // k
        xp = x.reshape(B, F, nw, k).transpose(0, 2, 3, 1)
        scores = jnp.einsum('bwkf,of->bwko', xp, w) + b
        weights = jax.nn.softmax(scores, axis=2)
        pooled = jnp.sum(xp * weights, axis=2)
        return pooled

    def _L0_attn_ref(x, w_qkv, b_qkv, w_proj, b_proj, scale, riem_scale, grassman_scale, bn_gamma, bn_beta, bn_mean, bn_var, conv_w, conv_b):
        import jax, jax.numpy as jnp
        import numpy as np
        B, N, C, H = (4, 256, 64, 8)
        HD = C // H
        BN_EPS = 1e-05
        b, n, c = x.shape
        h, hd = (H, c // H)
        qkv = (x @ w_qkv.T + b_qkv).reshape(b, n, 3, h, hd).transpose(2, 0, 3, 1, 4)
        q, k, v = (qkv[0], qkv[1], qkv[2])
        qgr, _ = jnp.linalg.qr(q)
        kgr, _ = jnp.linalg.qr(k)
        attn_grass = jnp.einsum('bhnd,bhmd->bhnm', qgr, kgr) ** 2 * grassman_scale
        dots = jnp.einsum('bhnd,bhmd->bhnm', q, k)
        attn_eucl = dots * scale
        attn_riem = dots ** 2 * riem_scale
        a = jnp.concatenate([attn_eucl, attn_riem, attn_grass], axis=1)
        inv = (bn_gamma * jax.lax.rsqrt(bn_var + BN_EPS))[:, None, None]
        a = (a - bn_mean[:, None, None]) * inv + bn_beta[:, None, None]
        a = jnp.einsum('oc,bcnm->bonm', conv_w, a) + conv_b[None, :, None, None]
        a = jax.nn.softmax(a, axis=-1)
        out = jnp.einsum('bhnm,bhmd->bhnd', a, v)
        out = out.transpose(0, 2, 1, 3).reshape(b, n, c)
        return out @ w_proj.T + b_proj

    def _L0_ffn_ref(x, route_id, Wi, bi, Wr, br, Ws, bs, Wo, bo):
        import jax, jax.numpy as jnp
        import numpy as np
        B, T, IN_DIM = (64, 64, 64)
        HID, OUT_DIM = (128, 64)
        N_LAYERS, N_EXPERTS, N_SHARED = (2, 16, 1)
        flat = x.reshape(-1, x.shape[-1])
        n_tok = flat.shape[0]
        route = jnp.repeat(route_id, n_tok // route_id.shape[0])
        h = jax.nn.relu(flat @ Wi.T + bi)
        n_layers, n_experts = (Wr.shape[0], Wr.shape[1])
        for l in range(n_layers):
            shared = (jnp.einsum('nd,shd->snh', h, Ws[l]) + bs[l][:, None, :]).mean(axis=0)
            routed = jnp.zeros_like(h)
            for e in range(n_experts):
                ye = h @ Wr[l, e].T + br[l, e]
                routed = routed + jnp.where((route == e)[:, None], ye, 0.0)
            h = jax.nn.relu(shared + routed + h)
        out = h @ Wo.T + bo
        return out.reshape(*x.shape[:-1], out.shape[-1])
    h = _L0_tok_ref(x, L0_tok_w, L0_tok_b)
    h = h + _L0_attn_ref(_layernorm(h, axis=-1), L0_attn_w_qkv, L0_attn_b_qkv, L0_attn_w_proj, L0_attn_b_proj, L0_attn_scale, L0_attn_riem_scale, L0_attn_grassman_scale, L0_attn_bn_gamma, L0_attn_bn_beta, L0_attn_bn_mean, L0_attn_bn_var, L0_attn_conv_w, L0_attn_conv_b)
    h = h + _L0_ffn_ref(_layernorm(h, axis=-1), L0_ffn_route_id, L0_ffn_Wi, L0_ffn_bi, L0_ffn_Wr, L0_ffn_br, L0_ffn_Ws, L0_ffn_bs, L0_ffn_Wo, L0_ffn_bo)
    return h

_drawn_inputs = setup_inputs


def setup_inputs(seed=0):
    import zlib

    import numpy as np

    out = dict(_drawn_inputs(seed))
    spreads = {'L0_attn_b_qkv': (0.0, 0.1),
     'L0_attn_b_proj': (0.0, 0.1),
     'L0_attn_bn_gamma': (1.0, 0.6),
     'L0_attn_bn_beta': (0.0, 0.8),
     'L0_attn_bn_mean': (0.0, 0.8),
     'L0_attn_bn_var': (1.0, 0.6),
     'L0_attn_conv_b': (0.0, 0.8),
     'L0_ffn_bi': (0.0, 0.1),
     'L0_ffn_bo': (0.0, 0.1)}
    factors = {'L0_attn_w_qkv': 5.185,
     'L0_attn_conv_w': 8.0,
     'L0_ffn_Wr': 2.834,
     'L0_ffn_br': 4.769,
     'L0_ffn_Ws': 2.849,
     'L0_ffn_bs': 4.372}
    for name, (base, spread) in spreads.items():
        noise = np.random.default_rng([zlib.crc32(name.encode()), seed]).standard_normal(out[name].shape)
        drawn = base * np.exp(spread * noise) if base else spread * noise
        out[name] = jnp.asarray(drawn.astype(out[name].dtype))
    for name, factor in factors.items():
        out[name] = (out[name] * factor).astype(out[name].dtype)
    return out
```

```python
from contextlib import ExitStack

import numpy as np
import concourse.bass as bass
import concourse.mybir as mybir

F32 = mybir.dt.float32
BF16 = mybir.dt.bfloat16
I32 = mybir.dt.int32
ALU = mybir.AluOpType
ACT = mybir.ActivationFunctionType
AX = mybir.AxisListType

B, C, T = 128, 64, 750
WIN = 8
N = (T + WIN - 1) // WIN
NP = 96
TP = N * WIN
H, D = 8, 8
PAIRS = B // 2
NT, NTAU = 6, 12
HID, EXP, LAYERS = 128, 16, 2
GP = 16
NG = PAIRS // GP
CP = 4
NCH = PAIRS // CP
HALF = TP // 2
LN_EPS = 1e-5
BN_EPS = 1e-5


def raw(ap, offset, pattern):
    return bass.AP(ap.tensor, offset, pattern)


def constants(nc, sb, p, k):
    sem = nc.semaphore
    with ExitStack() as ctx:
        param_in = ctx.enter_context(sem("param_in"))
        pool_step = ctx.enter_context(sem("pool_step"))
        dve_step = ctx.enter_context(sem("dve_step"))
        act_step = ctx.enter_context(sem("act_step"))
        pe_step = ctx.enter_context(sem("pe_step"))
        upper = ctx.enter_context(nc.sbuf_tensor("upper", [128, 1], F32))
        mask4 = ctx.enter_context(nc.sbuf_tensor("mask4", [128, 4], F32))
        bn_rows = ctx.enter_context(nc.sbuf_tensor("bn_rows", [128, 4, 24], F32))
        conv_rows = ctx.enter_context(nc.sbuf_tensor("conv_rows", [128, 24], F32))
        bn_col = ctx.enter_context(nc.sbuf_tensor("bn_col", [128, 2, 2], F32))
        scale_col = ctx.enter_context(nc.sbuf_tensor("scale_col", [128, 3], F32))
        conv2 = ctx.enter_context(nc.sbuf_tensor("conv2", [128, 8], F32))
        w_in = ctx.enter_context(nc.sbuf_tensor("w_in", [128, 6, 64], F32))
        wr_in = ctx.enter_context(nc.sbuf_tensor("wr_in", [128, 34, 128], F32))
        wi_in = ctx.enter_context(nc.sbuf_tensor("wi_in", [128, 64], F32))
        wo_in = ctx.enter_context(nc.sbuf_tensor("wo_in", [64, 128], F32))
        bias_in = ctx.enter_context(nc.sbuf_tensor("bias_in", [36, 128], F32))
        route_f = ctx.enter_context(nc.sbuf_tensor("route_f", [1, 5, PAIRS], F32))
        tokw = ctx.enter_context(nc.sbuf_tensor("tokw", [128, 1], F32))
        shared_t = ctx.enter_context(nc.sbuf_tensor("shared_t", [128, 2, 128], F32))
        ps_t = ctx.enter_context(nc.psum_tensor("ps_t", [128, 4, 512], F32))
        block = ctx.enter_context(nc.Block())
        LOADS = []
        marks = {}

        @block.sync
        def _(sp):
            def load(dst, src):
                sp.dma_start(dst, src).then_inc(param_in, 16)
                LOADS.append(1)

            w, wp = p["w_qkv"], p["w_proj"]
            for b in range(2):
                load(tokw[64 * b:64 * b + 64, :], raw(p["tok_w"], 0, [[1, 64], [1, 1]]))
                for s in range(3):
                    load(w_in[64 * b:64 * b + 64, s, :], raw(w, s * 4096, [[64, 64], [1, 64]]))
                    load(k["qkv_bias"][64 * b:64 * b + 64, s:s + 1], raw(p["b_qkv"], 64 * s, [[1, 64], [1, 1]]))
                load(w_in[64 * b:64 * b + 64, 3, :], raw(wp, 0, [[64, 64], [1, 64]]))
                load(k["proj_bias"][64 * b:64 * b + 64, :], raw(p["b_proj"], 0, [[1, 64], [1, 1]]))
                load(k["bias_row"][:, b, :], raw(p["b_qkv"], 0, [[0, 96], [1, 192]]))
                load(k["bo_row"][:, b, :], raw(p["bo"], 0, [[0, N], [1, 64]]))
            load(k["tok_bias"][:], raw(p["tok_b"], 0, [[0, 32], [1, 1]]))
            for q in range(16):
                load(bn_col[8 * q:8 * q + 8, 0, 0:1], raw(p["bn_gamma"], q % 8, [[0, 8], [1, 1]]))
                load(bn_col[8 * q:8 * q + 8, 0, 1:2], raw(p["bn_var"], q % 8, [[0, 8], [1, 1]]))
                load(bn_col[8 * q:8 * q + 8, 1, 0:1], raw(p["bn_gamma"], 8 + q, [[0, 8], [1, 1]]))
                load(bn_col[8 * q:8 * q + 8, 1, 1:2], raw(p["bn_var"], 8 + q, [[0, 8], [1, 1]]))
                load(k["conv1"][8 * q:8 * q + 8, :], raw(p["conv_wt"], 8 * (q % 8), [[0, 8], [1, 8]]))
                load(conv2[8 * q:8 * q + 8, :], raw(p["conv_wt"], 8 * (8 + q), [[0, 8], [1, 8]]))
                load(conv_rows[8 * q:8 * q + 8, :], raw(p["conv_w"], 24 * (q % 8), [[0, 8], [1, 24]]))
                load(k["conv_const"][8 * q:8 * q + 8, :], raw(p["conv_b"], q % 8, [[0, 8], [1, 1]]))
            for n, name in enumerate(("bn_gamma", "bn_beta", "bn_mean", "bn_var")):
                load(bn_rows[:, n, :], raw(p[name], 0, [[0, 128], [1, 24]]))
            load(scale_col[:, 0:1], raw(p["scale"], 0, [[0, 128], [1, 1]]))
            load(scale_col[0:64, 1:2], raw(p["riem_scale"], 0, [[0, 64], [1, 1]]))
            load(scale_col[64:128, 1:2], raw(p["grassman_scale"], 0, [[0, 64], [1, 1]]))
            load(wr_in[:, 0:32, :], raw(p["Wr"], 0, [[128, 128], [16384, 32], [1, 128]]))
            load(wr_in[:, 32:34, :], raw(p["Ws"], 0, [[128, 128], [16384, 2], [1, 128]]))
            load(wi_in[:, :], p["Wi"])
            load(wo_in[:, :], p["Wo"])
            load(bias_in[0:32, :], raw(p["br"], 0, [[128, 32], [1, 128]]))
            load(bias_in[32:34, :], raw(p["bs"], 0, [[128, 2], [1, 128]]))
            load(bias_in[34:35, :], raw(p["bi"], 0, [[128, 1], [1, 128]]))
            load(k["route_in"][:, :], p["route_id"])
            sp.wait_ge(param_in, 16 * len(LOADS))

        n_loads = len(LOADS)

        @block.gpsimd
        def _(pool):
            done = 0

            def step(ins):
                nonlocal done
                done += 1
                ins.then_inc(pool_step, 1)
                pool.wait_ge(pool_step, done)

            def diagonal(view, base, pattern, mult):
                step(pool.affine_select(out=view, in_=view, compare_op=ALU.not_equal, fill=1.0, base=base,
                                        pattern=pattern, channel_multiplier=mult))

            for name in ("ident", "score_w", "delta_q", "mean_w", "w_bd", "w_tok", "wi_bd", "pair_sel"):
                step(pool.memset(k[name][:], 0.0))
            step(pool.memset(k["mask16"][:], 1.0))
            step(pool.memset(k["ln_eps"][:], LN_EPS))
            step(pool.memset(upper[0:64, :], 0.0))
            step(pool.memset(upper[64:128, :], 1.0))
            diagonal(k["ident"][:], 0, [[-1, 128]], 1)
            for b in range(2):
                q = slice(64 * b, 64 * b + 64)
                diagonal(k["score_w"][q], -b, [[-2, GP], [1, 32]], 0)
                step(pool.memset(k["mean_w"][q, q], 1.0 / C))
            m = k["mask16"][:]
            step(pool.affine_select(out=m, in_=m, compare_op=ALU.is_ge, fill=0.0, base=0,
                                    pattern=[[-8, 16]], channel_multiplier=1))
            step(pool.affine_select(out=m, in_=m, compare_op=ALU.is_ge, fill=0.0, base=7,
                                    pattern=[[8, 16]], channel_multiplier=-1))
            diagonal(k["delta_q"][:], 0, [[-8, 16], [-1, 8]], 1)
            for part in range(3):
                diagonal(k["pair_sel"][32 * part:32 * part + 32], 0, [[-2, GP], [-1, 2], [0, 64]], 1)
            marks["pool"] = done

        @block.scalar
        def _(act):
            act.wait_ge(dve_step, 2)
            act.activation(bn_rows[:, 3, :], bn_rows[:, 3, :], ACT.Sqrt).then_inc(act_step, 1)
            act.activation(bn_col[:, :, 1], bn_col[:, :, 1], ACT.Sqrt).then_inc(act_step, 1)

        @block.vector
        def _(dve):
            done = 0

            def step(ins):
                nonlocal done
                done += 1
                ins.then_inc(dve_step, 1)
                dve.wait_ge(dve_step, done)

            dve.wait_ge(param_in, 16 * n_loads)
            step(dve.tensor_scalar(bn_rows[:, 3, :], bn_rows[:, 3, :], BN_EPS, None, ALU.add))
            step(dve.tensor_scalar(bn_col[:, :, 1], bn_col[:, :, 1], BN_EPS, None, ALU.add))
            dve.wait_ge(act_step, 2)
            step(dve.reciprocal(bn_rows[:, 3, :], bn_rows[:, 3, :]))
            step(dve.reciprocal(bn_col[:, :, 1], bn_col[:, :, 1]))
            step(dve.tensor_tensor(bn_rows[:, 0, :], bn_rows[:, 0, :], bn_rows[:, 3, :], ALU.mult))
            step(dve.tensor_tensor(bn_col[:, :, 0], bn_col[:, :, 0], bn_col[:, :, 1], ALU.mult))
            step(dve.tensor_tensor(bn_rows[:, 2, :], bn_rows[:, 2, :], bn_rows[:, 0, :], ALU.mult))
            step(dve.tensor_tensor(bn_rows[:, 1, :], bn_rows[:, 1, :], bn_rows[:, 2, :], ALU.subtract))
            step(dve.tensor_tensor(conv_rows[:], conv_rows[:], bn_rows[:, 1, :], ALU.mult))
            step(dve.tensor_reduce(scale_col[:, 2:3], conv_rows[:], AX.X, ALU.add))
            step(dve.tensor_tensor(k["conv_const"][:], k["conv_const"][:], scale_col[:, 2:3], ALU.add))
            step(dve.tensor_scalar(k["conv1"][:], k["conv1"][:], bn_col[:, 0, 0:1], scale_col[:, 0:1], ALU.mult, ALU.mult))
            step(dve.tensor_scalar(conv2[:], conv2[:], bn_col[:, 1, 0:1], scale_col[:, 1:2], ALU.mult, ALU.mult))
            dve.wait_ge(pool_step, marks["pool"])
            step(dve.tensor_reduce(k["delta"][:], k["delta_q"][:].rearrange("p q m -> p m q"), AX.X, ALU.add))
            step(dve.tensor_tensor(k["hmask"][:], k["mask16"][:, 0:8], k["mask16"][:, 8:16], ALU.add))
            step(dve.tensor_reduce(mask4[:], k["mask16"][:].rearrange("p (j g) -> p g j", g=4), AX.X, ALU.add))
            for g in range(4):
                step(dve.tensor_scalar(k["ident_g"][:, g, :], k["ident"][:], mask4[:, g:g + 1], None, ALU.mult))
            step(dve.tensor_tensor(k["mix_w"][:].rearrange("p (o m) -> p o m", o=8),
                                   conv2[:].unsqueeze(2).broadcast_to([128, 8, 8]),
                                   k["delta"][:].unsqueeze(1).broadcast_to([128, 8, 8]), ALU.mult))
            step(dve.tensor_scalar(k["score_w"][:], k["score_w"][:], tokw[:, 0:1], None, ALU.mult))
            step(dve.tensor_tensor(upper[:], upper[:], k["delta"][:, 7:8], ALU.mult))
            step(dve.tensor_scalar(upper[:], upper[:], -1.0, 1.0, ALU.mult, ALU.add))
            for t in range(NT):
                if t < 4:
                    step(dve.tensor_copy(k["vmask"][:, t, :], k["hmask"][:]))
                else:
                    step(dve.tensor_scalar(k["vmask"][:, t, :], k["hmask"][:], upper[:, 0:1], None, ALU.mult))
            for n, t in enumerate((0, 4)):
                step(dve.tensor_copy(k["den_w"][:, n, :].rearrange("p (o d) -> p o d", o=8),
                                     k["vmask"][:, t, :].unsqueeze(2).broadcast_to([128, 8, 8])))
            dve.wait_ge(pe_step, 1)
            for b in range(2):
                q = slice(64 * b, 64 * b + 64)
                for s in range(4):
                    step(dve.tensor_copy(k["w_bd"][q, s, q], ps_t[q, 0, s * 128 + 64 * b:s * 128 + 64 * b + 64]))
            marks["weights out"] = done
            dve.wait_ge(pe_step, 2)
            for b in range(2):
                q = slice(64 * b, 64 * b + 64)
                for s in range(3):
                    step(dve.tensor_copy(k["w_tok"][q, b, 64 * s:64 * s + 64], k["w_bd"][q, s, q]))
                step(dve.tensor_copy(k["wi_bd"][q, b, :], ps_t[q, 1, 0:128]))
            step(dve.tensor_copy(k["wo_t"][:], ps_t[:, 1, 128:192]))
            step(dve.tensor_copy(k["ffn_bias"][:, 0:35], ps_t[:, 1, 192:227]))
            for l in range(LAYERS):
                dve.wait_ge(pe_step, 3)
                step(dve.tensor_tensor(shared_t[:, l, :], ps_t[:, 2, l * 128:l * 128 + 128], k["ident"][:], ALU.add))
                step(dve.tensor_copy(k["ffn_w"][:, EXP, l, 0:HID], shared_t[:, l, :]))
            marks["shared out"] = done
            for n in range(8):
                dve.wait_ge(pe_step, 4 + n)
                for q in range(4):
                    l, e = divmod(4 * n + q, EXP)
                    step(dve.tensor_tensor(k["ffn_w"][:, e, l, 0:HID], ps_t[:, 3 if n % 2 else 0, q * 128:q * 128 + 128],
                                           shared_t[:, l, :], ALU.add))
            for l in range(LAYERS):
                step(dve.tensor_copy(k["ffn_w"][:, EXP, l, HID:HID + 1], k["ffn_bias"][:, 32 + l:33 + l]))
                step(dve.tensor_scalar(k["ffn_w"][:, 0:EXP, l, HID], k["ffn_bias"][:, 16 * l:16 * l + 16],
                                       k["ffn_bias"][:, 32 + l:33 + l], None, ALU.add))
            step(dve.tensor_copy(route_f[:, 0, :], k["route_in"][:, :]))
            step(dve.tensor_scalar(route_f[:, 1, :], route_f[:, 0, :], 0.0, None, ALU.is_ge))
            step(dve.tensor_scalar(route_f[:, 2, :], route_f[:, 0, :], float(EXP), None, ALU.is_lt))
            step(dve.tensor_tensor(route_f[:, 1, :], route_f[:, 1, :], route_f[:, 2, :], ALU.mult))
            step(dve.tensor_scalar(route_f[:, 3, :], route_f[:, 0, :], 0.0, float(EXP), ALU.max, ALU.min))
            step(dve.tensor_scalar(route_f[:, 3, :], route_f[:, 3, :], -float(EXP), None, ALU.add))
            step(dve.tensor_tensor(route_f[:, 3, :], route_f[:, 3, :], route_f[:, 1, :], ALU.mult))
            step(dve.tensor_scalar(k["route"][:, :], route_f[:, 3, :], float(EXP), None, ALU.add))

        @block.tensor
        def _(pe):
            pe.wait_ge(param_in, 16 * n_loads)
            pe.wait_ge(pool_step, marks["pool"])
            for s in range(4):
                mm = pe.transpose(ps_t[0:64, 0, s * 128:s * 128 + 128], w_in[:, s, :], k["ident"][:])
            mm = pe.transpose(ps_t[0:64, 1, 0:128], wi_in[:, :], k["ident"][:])
            for s in range(4):
                mm = pe.matmul(ps_t[64:128, 0, s * 128:s * 128 + 128], w_in[:, s, :], k["ident"][:], start=True, stop=True)
            mm.then_inc(pe_step, 1)
            pe.matmul(ps_t[64:128, 1, 0:128], wi_in[:, :], k["ident"][:], start=True, stop=True)
            pe.transpose(ps_t[:, 1, 128:192], wo_in[:, :], k["ident"][0:64, 0:64])
            pe.transpose(ps_t[:, 1, 192:227], bias_in[0:35, :], k["ident"][0:35, 0:35]).then_inc(pe_step, 1)
            for l in range(LAYERS):
                mm = pe.transpose(ps_t[:, 2, l * 128:l * 128 + 128], wr_in[:, 32 + l, :], k["ident"][:])
            mm.then_inc(pe_step, 1)
            for n in range(8):
                if n == 0:
                    pe.wait_ge(dve_step, marks["weights out"])
                if n >= 2:
                    pe.wait_ge(dve_step, marks["shared out"] + 4 * (n - 1))
                for q in range(4):
                    mm = pe.transpose(ps_t[:, 3 if n % 2 else 0, q * 128:q * 128 + 128], wr_in[:, 4 * n + q, :], k["ident"][:])
                mm.then_inc(pe_step, 1)



def pool_windows(nc, x, tokens, k):
    sem = nc.semaphore
    rows = x.rearrange("b f t -> (b f) t").rearrange("(n p) t -> p n t", p=128)
    with ExitStack() as ctx:
        x_in = [ctx.enter_context(sem(f"x_in{a}")) for a in range(2)]
        x_used = ctx.enter_context(sem("x_used"))
        pad_zero = ctx.enter_context(sem("pad_zero"))
        scores_done = ctx.enter_context(sem("scores_done"))
        scores_out = ctx.enter_context(sem("scores_out"))
        shifted = ctx.enter_context(sem("shifted"))
        exps = ctx.enter_context(sem("exps"))
        dve_step = ctx.enter_context(sem("dve_step"))
        weights_done = ctx.enter_context(sem("weights_done"))
        spread_done = ctx.enter_context(sem("spread_done"))
        spread_used = ctx.enter_context(sem("spread_used"))
        prod_done = ctx.enter_context(sem("prod_done"))
        x_g = ctx.enter_context(nc.sbuf_tensor("x_g", [128, 2, GP, TP], F32))
        soft = ctx.enter_context(nc.sbuf_tensor("soft", [32, N, WIN], F32))
        rest = ctx.enter_context(nc.sbuf_tensor("rest", [32, TP], F32))
        stat = ctx.enter_context(nc.sbuf_tensor("stat", [32, 2, N], F32))
        parts = ctx.enter_context(nc.sbuf_tensor("parts", [96, TP], BF16))
        prod = ctx.enter_context(nc.sbuf_tensor("prod", [128, 2, TP], F32))
        ps_score = ctx.enter_context(nc.psum_tensor("ps_score", [32, 2, 512], F32))
        ps_spread = ctx.enter_context(nc.psum_tensor("ps_spread", [128, 4, 512], F32))
        block = ctx.enter_context(nc.Block())
        LOADS_G = GP // 4

        @block.sync
        def _(sp):
            with sp.Fori(0, (NG) // 2) as twice:
                g = twice * 2
                for a in range(2):
                    sp.wait_ge(x_used, (g + a + 1) * 1)
                    for q in range(LOADS_G):
                        sp.dma_start(x_g[:, a, 4 * q:4 * q + 4, 0:T],
                                     rows[:, bass.ds((g + a) * GP + 4 * q, 4), :]).then_inc(x_in[a], 16)

        @block.tensor
        def _(pe):
            with pe.Fori(0, (NG) // 2) as twice:
                g = twice * 2
                for a in range(2):
                    pe.wait_ge(x_in[a], (twice + 1) * 16 * LOADS_G)
                    pe.wait_ge(pad_zero, 1)
                    pe.wait_ge(scores_out, g + a + 1)
                    for half in range(2):
                        for n in range(GP):
                            mm = pe.matmul(ps_score[:, half, 0:HALF], k["score_w"][:, n, :],
                                           x_g[:, a, n, half * HALF:half * HALF + HALF],
                                           start=(n == 0), stop=(n == GP - 1))
                    mm.then_inc(scores_done, 1)
                    pe.wait_ge(weights_done, g + a + 1)
                    for n in range(GP):
                        pe.wait_ge(spread_used, (g + a) * GP + n + 1)
                        for half in range(2):
                            mm = pe.matmul(ps_spread[:, 2 * (n % 2) + half, 0:HALF], k["pair_sel"][:, n, :],
                                           parts[:, half * HALF:half * HALF + HALF], start=True, stop=True)
                        mm.then_inc(spread_done, 1)

        @block.scalar
        def _(act):
            act.sem_inc(scores_out, 1)
            with act.Fori(0, NG) as g:
                act.wait_ge(scores_done, g + 1)
                act.wait_ge(weights_done, g)
                act.activation(soft[:].rearrange("p w k -> p (w k)").rearrange("p (a t) -> p a t", a=2),
                               ps_score[:, :, 0:HALF], ACT.Identity, bias=k["tok_bias"][:, 0:1]).then_inc(scores_out, 1)
                act.wait_ge(shifted, g + 1)
                act.activation(soft[:], soft[:], ACT.Exp).then_inc(exps, 1)

        @block.vector
        def _(dve):
            dve.memset(x_g[:, :, :, T:TP], 0.0).then_inc(pad_zero, 1)
            dve.sem_inc(x_used, 2)
            dve.sem_inc(spread_used, 2)
            with dve.Fori(0, (NG) // 2) as twice:
                g = twice * 2
                for a in range(2):
                    i = g + a

                    def step(n, ins):
                        ins.then_inc(dve_step, 1)
                        dve.wait_ge(dve_step, i * 8 + n)

                    def over(view):
                        return view.unsqueeze(2).broadcast_to([32, N, WIN])

                    dve.wait_ge(scores_out, i + 2)
                    step(1, dve.tensor_reduce(stat[:, 0, :], soft[:], AX.X, ALU.max))
                    dve.tensor_tensor(soft[:], soft[:], over(stat[:, 0, :]), ALU.subtract).then_inc(shifted, 1)
                    dve.wait_ge(exps, i + 1)
                    step(2, dve.tensor_reduce(stat[:, 0, :], soft[:], AX.X, ALU.add))
                    step(3, dve.reciprocal(stat[:, 1, :], stat[:, 0, :]))
                    dve.wait_ge(spread_done, i * GP)
                    step(4, dve.tensor_tensor(soft[:], soft[:], over(stat[:, 1, :]), ALU.mult))
                    flat = soft[:].rearrange("p w k -> p (w k)")
                    step(5, dve.tensor_copy(parts[0:32, :], flat))
                    step(6, dve.tensor_tensor(rest[:], flat, parts[0:32, :], ALU.subtract))
                    step(7, dve.tensor_copy(parts[32:64, :], rest[:]))
                    step(8, dve.tensor_tensor(flat, rest[:], parts[32:64, :], ALU.subtract))
                    dve.tensor_copy(parts[64:96, :], flat).then_inc(weights_done, 1)
                    for n in range(GP):
                        dve.wait_ge(spread_done, i * GP + n + 1)
                        ins = dve.tensor_tensor(prod[:, n % 2, :].rearrange("p (a t) -> p a t", a=2),
                                                x_g[:, a, n, :].rearrange("p (a t) -> p a t", a=2),
                                                ps_spread[:, 2 * (n % 2):2 * (n % 2) + 2, 0:HALF], ALU.mult)
                        ins.then_inc(spread_used, 1)
                        dve.wait_ge(spread_used, i * GP + n + 3)
                        ins = dve.tensor_reduce(tokens[:, bass.ds(i * GP + n, 1), 0:N],
                                                prod[:, n % 2, :].rearrange("p (w k) -> p w k", k=WIN), AX.X, ALU.add)
                        ins.then_inc(prod_done, 1)
                    ins = dve.sem_inc(x_used, 1)


def span(c, n):
    return slice(c * n, c * n + n) if isinstance(c, int) else bass.ds(c * n, n)


def two_stages(eng, count, first, second):
    first(0, 0, 0)
    with eng.Fori(0, count // 2 - 1) as n:
        first(2 * n + 1, 1, n)
        second(2 * n, 0, n)
        first(2 * n + 2, 0, n + 1)
        second(2 * n + 1, 1, n)
    first(count - 1, 1, count // 2 - 1)
    second(count - 2, 0, count // 2 - 1)
    second(count - 1, 1, count // 2 - 1)


def project(nc, tokens, q_cm, k_cm, gram, v_dram, top_dram, k):
    sem = nc.semaphore
    with ExitStack() as ctx:
        pads = ctx.enter_context(sem("pads"))
        mean_done = ctx.enter_context(sem("mean_done"))
        centered = ctx.enter_context(sem("centered"))
        squared = ctx.enter_context(sem("squared"))
        var_done = ctx.enter_context(sem("var_done"))
        std_done = ctx.enter_context(sem("std_done"))
        rstd_done = ctx.enter_context(sem("rstd_done"))
        xn_done = ctx.enter_context(sem("xn_done"))
        qk_done = ctx.enter_context(sem("qk_done"))
        qk_out = ctx.enter_context(sem("qk_out"))
        tok_done = ctx.enter_context(sem("tok_done"))
        tok_out = ctx.enter_context(sem("tok_out"))
        gram_done = ctx.enter_context(sem("gram_done"))
        gram_out = ctx.enter_context(sem("gram_out"))
        stored = [ctx.enter_context(sem(f"stored{a}")) for a in range(2)]
        xc = ctx.enter_context(nc.sbuf_tensor("xc", [128, 2, CP, NP], F32))
        sq = ctx.enter_context(nc.sbuf_tensor("sq_ln", [128, 2, CP, NP], F32))
        rstd = ctx.enter_context(nc.sbuf_tensor("rstd", [128, 2, CP, NP], F32))
        xn = ctx.enter_context(nc.sbuf_tensor("xn", [128, 2, CP, NP], F32))
        tok = ctx.enter_context(nc.sbuf_tensor("tok", [96, 2, CP, 2, 192], F32))
        ps_mean = ctx.enter_context(nc.psum_tensor("ps_mean", [128, 512], F32))
        ps_var = ctx.enter_context(nc.psum_tensor("ps_var", [128, 512], F32))
        ps_qk = ctx.enter_context(nc.psum_tensor("ps_qk", [128, 2, 512], F32))
        ps_tok = ctx.enter_context(nc.psum_tensor("ps_tok", [96, 2, 512], F32))
        ps_gram = ctx.enter_context(nc.psum_tensor("ps_gram", [128, 512], F32))
        block = ctx.enter_context(nc.Block())
        W = CP * NP

        def flat(view):
            return view.rearrange("p r m -> p (r m)")

        @block.sync
        def _(sp):
            def store(c, a):
                sp.wait_ge(tok_out, CP * (c + 1))
                sp.dma_start(v_dram[bass.ds(c * 2 * CP, 2 * CP)].rearrange("b m f -> m b f"),
                             tok[:, a].rearrange("p r b f -> p (r b) f")[:, :, 128:192]).then_inc(stored[a], 16)
                sp.dma_start(top_dram[bass.ds(c * 2 * CP, 2 * CP)].rearrange("b m f -> m b f"),
                             tok[0:8, a].rearrange("p r b f -> p (r b) f")[:, :, 0:128]).then_inc(stored[a], 16)

            with sp.Fori(0, (NCH) // 2) as twice:
                c = twice * 2
                store(c, 0)
                store(c + 1, 1)
            for a in range(2):
                sp.wait_ge(stored[a], 32 * NCH // 2)

        @block.tensor
        def _(pe):
            def norm(c, a, n):
                pe.wait_ge(pads, c + 1)
                pe.wait_ge(centered, c)
                pe.matmul(ps_mean[:, 0:W], k["mean_w"][:], tokens[:, span(c, CP), :], start=True, stop=True).then_inc(mean_done, 1)
                pe.wait_ge(squared, c + 1)
                pe.wait_ge(std_done, c)
                pe.matmul(ps_var[:, 0:W], k["mean_w"][:], flat(sq[:, a]), start=True, stop=True).then_inc(var_done, 1)

            def products(c, a, n):
                pe.wait_ge(xn_done, c + 1)
                pe.wait_ge(qk_out, 2 * c)
                for s in range(2):
                    pe.matmul(ps_qk[:, s, 0:W], k["w_bd"][:, s, :], flat(xn[:, a]), start=True, stop=True).then_inc(qk_done, 1)
                for r in range(CP):
                    pe.wait_ge(tok_out, CP * c + max(r - 1, 0))
                    pe.matmul(ps_tok[:, r % 2, 0:384], xn[:, a, r, :], k["w_tok"][:].rearrange("p b f -> p (b f)"),
                              start=True, stop=True).then_inc(tok_done, 1)
                pe.wait_ge(gram_out, c)
                pe.wait_ge(tok_out, CP * (c + 1))
                for r in range(CP):
                    for b in range(2):
                        for j in range(4):
                            rows = tok[0:N, a, r, b, 32 * j:32 * j + 32]
                            mm = pe.matmul(ps_gram[32 * j:32 * j + 32, 64 * r + 32 * b:64 * r + 32 * b + 32], rows, rows,
                                           start=True, stop=True)
                mm.then_inc(gram_done, 1)

            two_stages(pe, NCH, norm, products)

        @block.scalar
        def _(act):
            def norm(c, a, n):
                act.wait_ge(centered, c + 1)
                act.wait_ge(var_done, c)
                act.activation(sq[:, a], xc[:, a], ACT.Square).then_inc(squared, 1)
                act.wait_ge(var_done, c + 1)
                act.wait_ge(xn_done, c)
                act.activation(flat(rstd[:, a]), ps_var[:, 0:W], ACT.Sqrt, bias=k["ln_eps"][:, 0:1]).then_inc(std_done, 1)

            def products(c, a, n):
                at = span(c, CP)
                for s, out in enumerate((q_cm, k_cm)):
                    act.wait_ge(qk_done, 2 * c + s + 1)
                    act.activation(out[:, at, :], ps_qk[:, s, 0:W].rearrange("p (r m) -> p r m", r=CP), ACT.Identity,
                                   bias=k["qkv_bias"][:, s:s + 1]).then_inc(qk_out, 1)
                at = span(c, 2 * CP)
                act.wait_ge(gram_done, c + 1)
                act.activation(gram[:, at, :], ps_gram[:, 0:256].rearrange("p (b e) -> p b e", e=32), ACT.Copy).then_inc(gram_out, 1)

            two_stages(act, NCH, norm, products)

        @block.vector
        def _(dve):
            def norm(c, a, n):
                at = span(c, CP)
                dve.tensor_copy(tokens[:, at, N:NP], tokens[:, at, N - 2:N]).then_inc(pads, 1)
                dve.wait_ge(mean_done, c + 1)
                dve.tensor_tensor(xc[:, a], tokens[:, at, :], ps_mean[:, 0:W].rearrange("p (r m) -> p r m", r=CP),
                                  ALU.subtract).then_inc(centered, 1)
                dve.wait_ge(std_done, c + 1)
                dve.reciprocal(rstd[:, a], rstd[:, a]).then_inc(rstd_done, 1)
                dve.wait_ge(rstd_done, c + 1)
                if not (isinstance(c, int) and c == 0):
                    dve.wait_ge(tok_done, CP * (c - 1))
                dve.tensor_tensor(xn[:, a], xc[:, a], rstd[:, a], ALU.mult).then_inc(xn_done, 1)

            def products(c, a, n):
                dve.wait_ge(stored[a], 32 * n)
                dve.wait_ge(gram_done, c)
                for r in range(CP):
                    dve.wait_ge(tok_done, CP * c + r + 1)
                    dve.tensor_tensor(tok[:, a, r].rearrange("p b f -> p (b f)"), ps_tok[:, r % 2, 0:384],
                                      k["bias_row"][:].rearrange("p b f -> p (b f)"), ALU.add).then_inc(tok_out, 1)

            two_stages(dve, NCH, norm, products)


def orthogonalise(nc, gram, m_t, top_dram, k):
    sem = nc.semaphore
    KH = 2 * H
    with ExitStack() as ctx:
        top_in = ctx.enter_context(sem("top_in"))
        aug_zero = ctx.enter_context(sem("aug_zero"))
        turned = ctx.enter_context(sem("turned"))
        dve_step = ctx.enter_context(sem("dve_step"))
        roots = ctx.enter_context(sem("roots"))
        m_turned = ctx.enter_context(sem("m_turned"))
        aug = ctx.enter_context(nc.sbuf_tensor("aug", [128, KH, D, 2 * D], F32))
        top = ctx.enter_context(nc.sbuf_tensor("top", [128, D, KH, D], F32))
        rows = ctx.enter_context(nc.sbuf_tensor("head_rows", [128, KH, D, D], F32))
        prods = ctx.enter_context(nc.sbuf_tensor("prods", [128, KH, D, D], F32))
        piv = ctx.enter_context(nc.sbuf_tensor("piv", [128, KH], F32))
        inv_piv = ctx.enter_context(nc.sbuf_tensor("inv_piv", [128, KH], F32))
        fac = ctx.enter_context(nc.sbuf_tensor("fac", [128, KH, D], F32))
        diag = ctx.enter_context(nc.sbuf_tensor("diag", [128, KH, D], F32))
        rs = ctx.enter_context(nc.sbuf_tensor("rs", [128, KH, D], F32))
        newton = ctx.enter_context(nc.sbuf_tensor("newton", [128, KH, D], F32))
        sign = ctx.enter_context(nc.sbuf_tensor("sign", [128, KH, D], F32))
        wq = ctx.enter_context(nc.sbuf_tensor("wq", [128, H, D, D], F32))
        m_sum = ctx.enter_context(nc.sbuf_tensor("m_sum", [128, D, 2, H, D], F32))
        ps_turn = ctx.enter_context(nc.psum_tensor("ps_turn", [128, 8, 512], F32))
        block = ctx.enter_context(nc.Block())
        marks = {}

        @block.sync
        def _(sp):
            sp.dma_start(top[:].rearrange("p n k d -> p (n k d)"), top_dram.rearrange("b m f -> b (m f)")).then_inc(top_in, 16)

        @block.gpsimd
        def _(pool):
            pool.memset(aug[:], 0.0).then_inc(aug_zero, 1)
            pool.wait_ge(aug_zero, 1)
            for i in range(D):
                pool.memset(aug[:, :, i, D + i], 1.0).then_inc(aug_zero, 1)

        @block.scalar
        def _(act):
            act.wait_ge(dve_step, DIAG_STEP)
            act.activation(rs[:], diag[:], ACT.Sqrt).then_inc(roots, 1)

        @block.vector
        def _(dve):
            done = 0

            def step(ins):
                nonlocal done
                done += 1
                ins.then_inc(dve_step, 1)
                dve.wait_ge(dve_step, done)

            def tt(out, a, b, op):
                step(dve.tensor_tensor(out, a, b, op))

            dve.wait_ge(aug_zero, 1 + D)
            for n in range(2):
                dve.wait_ge(turned, n + 1)
                step(dve.tensor_copy(aug[:].rearrange("p k i c -> p (k i) c")[:, :, 4 * n:4 * n + 4].rearrange("p a e -> p e a"),
                                     ps_turn[:, n, :].rearrange("p (e a) -> p e a", e=4)))
            for j in range(D - 1):
                left = D - 1 - j
                step(dve.reciprocal(inv_piv[:], aug[:, :, j, j]))
                tt(fac[:, :, 0:left], aug[:, :, j + 1:D, j], inv_piv[:].unsqueeze(2).broadcast_to([128, KH, left]), ALU.mult)
                tt(prods[:, :, 0:left, :], fac[:, :, 0:left].unsqueeze(3).broadcast_to([128, KH, left, D]),
                   aug[:, :, j, j + 1:j + 1 + D].unsqueeze(2).broadcast_to([128, KH, left, D]), ALU.mult)
                tt(aug[:, :, j + 1:D, j + 1:j + 1 + D], aug[:, :, j + 1:D, j + 1:j + 1 + D], prods[:, :, 0:left, :], ALU.subtract)
            step(dve.tensor_copy(diag[:], aug[:].rearrange("p k i c -> p k (i c)")[:, :, 0:D * 2 * D:2 * D + 1]))
            assert done == DIAG_STEP
            dve.wait_ge(roots, 1)
            step(dve.reciprocal(rs[:], rs[:]))
            tt(newton[:], rs[:], rs[:], ALU.mult)
            tt(newton[:], newton[:], diag[:], ALU.mult)
            step(dve.tensor_scalar(newton[:], newton[:], -0.5, 1.5, ALU.mult, ALU.add))
            tt(rs[:], rs[:], newton[:], ALU.mult)
            dve.wait_ge(top_in, 16)
            for d in range(D):
                cols = D - d
                out = rows if d == 0 else prods
                tt(out[:, :, :, 0:cols] if d else out[:], top[:, :, :, d].rearrange("p n k -> p k n").unsqueeze(3).broadcast_to([128, KH, D, cols]),
                   aug[:, :, d:D, D + d].unsqueeze(2).broadcast_to([128, KH, D, cols]), ALU.mult)
                if d:
                    tt(rows[:, :, :, d:D], rows[:, :, :, d:D], prods[:, :, :, 0:cols], ALU.add)
            tt(rows[:], rows[:], rs[:].unsqueeze(2).broadcast_to([128, KH, D, D]), ALU.mult)
            for j in range(D):
                left = D - 1 - j
                step(dve.tensor_scalar(sign[:, :, j], rows[:, :, j, j], 0.0, -2.0, ALU.is_ge, ALU.mult))
                step(dve.tensor_scalar(sign[:, :, j], sign[:, :, j], 1.0, None, ALU.add))
                if not left:
                    break
                tt(piv[:], rows[:, :, j, j], sign[:, :, j], ALU.subtract)
                step(dve.reciprocal(inv_piv[:], piv[:]))
                tt(fac[:, :, 0:left], rows[:, :, j + 1:D, j], inv_piv[:].unsqueeze(2).broadcast_to([128, KH, left]), ALU.mult)
                tt(prods[:, :, 0:left, 0:left], fac[:, :, 0:left].unsqueeze(3).broadcast_to([128, KH, left, left]),
                   rows[:, :, j, j + 1:D].unsqueeze(2).broadcast_to([128, KH, left, left]), ALU.mult)
                tt(rows[:, :, j + 1:D, j + 1:D], rows[:, :, j + 1:D, j + 1:D], prods[:, :, 0:left, 0:left], ALU.subtract)
            tt(sign[:], sign[:], rs[:], ALU.mult)
            tt(sign[:, 0:H, :], sign[:, 0:H, :], sign[:, H:KH, :], ALU.mult)
            tt(wq[:], aug[:, 0:H, :, D:2 * D], sign[:, 0:H, :].unsqueeze(3).broadcast_to([128, H, D, D]), ALU.mult)
            m_view = m_sum[:, :, 0].rearrange("p d h e -> p h d e")
            for j in range(D - 1, -1, -1):
                n = j + 1
                out = m_view if j == D - 1 else prods[:, 0:H, 0:n, 0:n]
                tt(out, wq[:, :, j, 0:n].unsqueeze(3).broadcast_to([128, H, n, n]),
                   aug[:, H:KH, j, D:D + n].unsqueeze(2).broadcast_to([128, H, n, n]), ALU.mult)
                if j < D - 1:
                    tt(m_view[:, :, 0:n, 0:n], m_view[:, :, 0:n, 0:n], prods[:, 0:H, 0:n, 0:n], ALU.add)
            step(dve.tensor_copy(m_sum[:, :, 1].rearrange("p d h e -> p d (h e)"), m_sum[:, :, 0].rearrange("p d h e -> p d (h e)")))
            marks["m"] = done
            for n in range(2):
                dve.wait_ge(m_turned, n + 1)
                for b in range(2):
                    q = slice(64 * b, 64 * b + 64)
                    step(dve.tensor_copy(m_t[q, :, 4 * n:4 * n + 4].rearrange("p i d -> p d i"),
                                         ps_turn[q, 2 + n, :].rearrange("p (d i b) -> p d i b", d=4, b=2)[:, :, :, b]))

        @block.tensor
        def _(pe):
            for e in range(D):
                for g in range(4):
                    mm = pe.matmul(ps_turn[:, e // 4, 128 * (e % 4):128 * (e % 4) + 128], gram[:, :, 8 * g + e], k["ident_g"][:, g, :],
                                   start=(g == 0), stop=(g == 3))
                if e % 4 == 3:
                    mm.then_inc(turned, 1)
            pe.wait_ge(dve_step, marks["m"])
            for d in range(D):
                mm = pe.transpose(ps_turn[:, 2 + d // 4, 128 * (d % 4):128 * (d % 4) + 128],
                                  m_sum[:, d].rearrange("p b h e -> p (b h e)"), k["ident"][:])
                if d % 4 == 3:
                    mm.then_inc(m_turned, 1)


DIAG_STEP = 2 + 4 * (D - 1) + 1


def attend(nc, q_cm, k_cm, m_t, o_cm, v_dram, k):
    sem = nc.semaphore
    N2 = 2 * N
    with ExitStack() as ctx:
        names = ("q_zero q_ready m_ready keys_ready turned_ready v_ready kt_done kt_out dots_done squared mixed keys_used "
                 "max_done max_turned max_ready max_spread max_out sub_done exp_done sum_done av_done inv_done out_done blk_zero r_done")
        s = {n: ctx.enter_context(sem(n)) for n in names.split()}
        v_in = [ctx.enter_context(sem(f"v_in{a}")) for a in range(2)]

        def sb(name, shape):
            return ctx.enter_context(nc.sbuf_tensor(name, shape, F32))

        m_blk = sb("m_blk", [128, 2, 16, D])
        k_blk = sb("k_blk", [128, 2, NTAU, 2, H, 8])
        k_mix = sb("k_mix", [128, 2, NT, 2, H, 8])
        v_rep = sb("v_rep", [128, 2, 2, NT * C])
        v_blk = sb("v_blk", [128, 2, 2, NT, C])
        k_turn = sb("k_turn", [128, 2, NP])
        q_z = sb("q_z", [128, 2, N2])
        sq = sb("sq", [128, 6, 2 * N2])
        top = sb("row_max", [128, N2])
        top16 = sb("row_max16", [N, 2, 2, H])
        top_e = sb("row_max_e", [N, 2, H, 8])
        shift = sb("shift", [128, N2])
        prob = sb("prob", [128, NT, N2])
        sums = sb("sums", [128, 2, N2])
        inv = sb("inv", [128, N])
        ps_dot = ctx.enter_context(nc.psum_tensor("ps_dot", [128, 2, 512], F32))
        ps_a = ctx.enter_context(nc.psum_tensor("ps_a", [128, 3, 512], F32))
        ps_x = ctx.enter_context(nc.psum_tensor("ps_x", [128, 512], F32))
        ps_b = ctx.enter_context(nc.psum_tensor("ps_b", [128, 512], F32))
        ps_o = ctx.enter_context(nc.psum_tensor("ps_o", [128, 512], F32))
        block = ctx.enter_context(nc.Block())

        def steps(eng, step):
            step(0, 0, False, True)
            with eng.Fori(0, (PAIRS - 2) // 2) as twice:
                c = twice * 2
                step(c + 1, 1, True, True)
                step(c + 2, 0, True, True)
            step(PAIRS - 1, 1, True, False)

        @block.sync
        def _(sp):
            def load(i, a):
                if not isinstance(i, int):
                    sp.wait_ge(s["v_ready"], i - 1)
                for b in range(2):
                    src = v_dram[span(2 * i + b, 1)].rearrange("b (mj mi t) f -> mi mj (b t f)", mi=2, t=NT)
                    for mi in range(2):
                        sp.dma_start(v_rep[64 * mi:64 * mi + 64, a, b, :], src[mi].unsqueeze(0).broadcast_to([8, 8, NT * C])).then_inc(v_in[a], 16)

            load(0, 0)
            load(1, 1)
            with sp.Fori(1, (PAIRS) // 2) as twice:
                i = twice * 2
                load(i, 0)
                load(i + 1, 1)

        @block.gpsimd
        def _(pool):
            def build(i, a, n):
                pool.tensor_tensor(m_blk[:, a], m_t[:, span(i, 1), :].broadcast_to([128, 16, D]),
                                   k["mask16"][:].unsqueeze(2).broadcast_to([128, 16, D]), ALU.mult).then_inc(s["m_ready"], 1)
                if not (isinstance(i, int) and i < 2):
                    pool.wait_ge(s["keys_used"], i - 1)
                key = k_cm[:, span(i, 1), :].rearrange("p i (mj tau) -> p (i tau) mj", tau=NTAU)
                heads = k["hmask"][:].unsqueeze(1).unsqueeze(3)

                def blocked(kind, view):
                    return pool.tensor_tensor(k_blk[:, a, :, kind], view.unsqueeze(2).broadcast_to([128, NTAU, H, 8]),
                                              heads.broadcast_to([128, NTAU, H, 8]), ALU.mult)

                blocked(0, key).then_inc(s["keys_ready"], 1)
                for mi in range(2):
                    pool.tensor_tensor(k_mix[:, a, :, mi], key[:, NT * mi:NT * mi + NT].unsqueeze(2).broadcast_to([128, NT, H, 8]),
                                       k["conv1"][:].unsqueeze(1).unsqueeze(3).broadcast_to([128, NT, H, 8]), ALU.mult).then_inc(s["keys_ready"], 1)
                pool.wait_ge(v_in[a], 64 * (n + 1))
                if not (isinstance(i, int) and i < 2):
                    pool.wait_ge(s["av_done"], i - 1)
                for b in range(2):
                    mm = pool.tensor_tensor(v_blk[:, a, b].rearrange("p t (o d) -> p (t o) d", o=H),
                                            v_rep[:, a, b].rearrange("p (t o d) -> p (t o) d", o=H, t=NT),
                                            k["vmask"][:].rearrange("p t o -> p (t o)").unsqueeze(2).broadcast_to([128, NT * H, D]), ALU.mult)
                mm.then_inc(s["v_ready"], 1)
                pool.wait_ge(s["kt_out"], i + 1)
                blocked(1, k_turn[:, a].rearrange("p (mj tau) -> p tau mj", tau=NTAU)).then_inc(s["turned_ready"], 1)

            build(0, 0, 0)
            build(1, 1, 0)
            with pool.Fori(1, (PAIRS) // 2) as twice:
                i = twice * 2
                build(i, 0, twice)
                build(i + 1, 1, twice)

        @block.tensor
        def _(pe):
            def turn_keys(i, a):
                pe.wait_ge(s["m_ready"], i + 1)
                pe.wait_ge(s["kt_out"], i)
                pe.matmul(ps_x[:, 256:256 + NP], m_blk[:, a].rearrange("p q d -> p (q d)"), k_cm[:, span(i, 1), :],
                          start=True, stop=True).then_inc(s["kt_done"], 1)

            def soft(prev, a, part):
                if part == 0:
                    pe.wait_ge(s["max_done"], prev + 1)
                    for b in range(2):
                        mm = pe.transpose(ps_x[0:N, 128 * b:128 * b + 128], top[:, N * b:N * b + N], k["ident"][:])
                    mm.then_inc(s["max_turned"], 1)
                if part == 1:
                    pe.wait_ge(s["max_ready"], prev + 1)
                    for mi in range(2):
                        for b in range(2):
                            mm = pe.matmul(ps_b[64 * mi:64 * mi + 64, N * b:N * b + N], top_e[:, b].rearrange("p o m -> p (o m)"),
                                           k["ident"][0:N, 0:N], start=True, stop=True)
                    mm.then_inc(s["max_spread"], 1)
                if part == 2:
                    pe.wait_ge(s["exp_done"], prev + 1)
                    pe.wait_ge(s["v_ready"], prev + 1)
                    pe.wait_ge(s["out_done"], prev)
                    for t in range(NT):
                        for b in range(2):
                            pe.matmul(ps_o[64 * b:64 * b + 64, 0:N], v_blk[:, a, b, t, :], prob[:, t, N * b:N * b + N],
                                      start=(t == 0), stop=(t == NT - 1))
                    pe.wait_ge(s["sum_done"], prev + 1)
                    for n in range(2):
                        for b in range(2):
                            mm = pe.matmul(ps_o[64 * b:64 * b + 64, NP:NP + N], k["den_w"][:, n, :], sums[:, n, N * b:N * b + N],
                                           start=(n == 0), stop=(n == 1))
                    mm.then_inc(s["av_done"], 1)

            def step(i, a, has_prev, has_next):
                prev = i - 1
                pe.wait_ge(s["q_ready"], i + 1)
                pe.wait_ge(s["keys_ready"], 3 * (i + 1))
                pe.wait_ge(s["turned_ready"], i + 1)
                for g in range(6):
                    j, mi = divmod(g, 2)
                    if has_prev or g >= 2:
                        pe.wait_ge(s["squared"], 6 * i + g - 1)
                    for t in (2 * j, 2 * j + 1):
                        mm = pe.matmul(ps_dot[:, g % 2, N2 * (t % 2):N2 * (t % 2) + N2],
                                       k_blk[:, a, mi * NT + t].rearrange("p k h m -> p (k h m)"), q_z[:, a, :], start=True, stop=True)
                    mm.then_inc(s["dots_done"], 1)
                    if has_prev and g == 0:
                        soft(prev, 1 - a, 0)
                    if has_prev and g == 2:
                        soft(prev, 1 - a, 1)
                    if has_next and g == 3:
                        turn_keys(i + 1, 1 - a)
                if has_prev:
                    pe.wait_ge(s["sub_done"], prev + 1)
                for j in range(3):
                    for t in (2 * j, 2 * j + 1):
                        mm = pe.matmul(ps_a[:, j, N2 * (t % 2):N2 * (t % 2) + N2], k_mix[:, a, t].rearrange("p q o m -> p (q o m)"),
                                       q_z[:, a, :], start=(t % 2 == 0), stop=False, skip_group_check=True)
                    if j == 2:
                        mm.then_inc(s["keys_used"], 1)
                    for mi in range(2):
                        pe.wait_ge(s["squared"], 6 * i + 2 * j + mi + 1)
                        mm = pe.matmul(ps_a[64 * mi:64 * mi + 64, j, 0:2 * N2], k["mix_w"][:], sq[:, 2 * j + mi, :],
                                       start=False, stop=True, skip_group_check=True)
                mm.then_inc(s["mixed"], 1)
                if has_prev:
                    soft(prev, 1 - a, 2)

            turn_keys(0, 0)
            steps(pe, step)
            soft(PAIRS - 1, 1, 0)
            soft(PAIRS - 1, 1, 1)
            soft(PAIRS - 1, 1, 2)

        @block.scalar
        def _(act):
            def turned_out(i, a):
                act.wait_ge(s["kt_done"], i + 1)
                if not (isinstance(i, int) and i < 2):
                    act.wait_ge(s["turned_ready"], i - 1)
                act.activation(k_turn[:, a, :], ps_x[:, 256:256 + NP], ACT.Copy).then_inc(s["kt_out"], 1)

            def shift_out(prev):
                act.wait_ge(s["max_spread"], prev + 1)
                act.wait_ge(s["sub_done"], prev)
                act.activation(shift[:], ps_b[:, 0:N2], ACT.Identity, bias=k["conv_const"][:, 0:1]).then_inc(s["max_out"], 1)

            def exps(prev):
                act.wait_ge(s["sub_done"], prev + 1)
                act.activation(prob[:], prob[:], ACT.Exp, bias=k["conv_const"][:, 0:1]).then_inc(s["exp_done"], 1)

            def step(i, a, has_prev, has_next):
                for g in range(6):
                    if has_prev and g == 0:
                        act.wait_ge(s["mixed"], i)
                    act.wait_ge(s["dots_done"], 6 * i + g + 1)
                    act.activation(sq[:, g, :], ps_dot[:, g % 2, 0:2 * N2], ACT.Square).then_inc(s["squared"], 1)
                    if has_prev and g == 2:
                        shift_out(i - 1)
                    if has_next and g == 3:
                        turned_out(i + 1, 1 - a)
                if has_prev:
                    exps(i - 1)

            turned_out(0, 0)
            steps(act, step)
            shift_out(PAIRS - 1)
            exps(PAIRS - 1)

        @block.vector
        def _(dve):
            def queries(i, a):
                if not (isinstance(i, int) and i < 2):
                    dve.wait_ge(s["keys_used"], i - 1)
                for b in range(2):
                    q = slice(64 * b, 64 * b + 64)
                    cp = dve.tensor_copy(q_z[q, a, N * b:N * b + N], q_cm[q, span(i, 1), 0:N])
                cp.then_inc(s["q_ready"], 1)

            def maxima(prev):
                dve.wait_ge(s["mixed"], prev + 1)
                dve.wait_ge(s["max_turned"], prev)
                dve.tensor_reduce(top[:], ps_a[:, :, 0:2 * N2].rearrange("p j (t n) -> p n j t", t=2), AX.XY, ALU.max).then_inc(s["max_done"], 1)
                dve.wait_ge(s["max_turned"], prev + 1)
                dve.tensor_reduce(top16[:].rearrange("p b m o -> p (b m o)"), ps_x[0:N, 0:256].rearrange("p (q m) -> p q m", m=8),
                                  AX.X, ALU.max).then_inc(s["r_done"], 1)
                dve.wait_ge(s["r_done"], prev + 1)
                dve.wait_ge(s["max_spread"], prev)
                dve.tensor_tensor(top_e[:], top16[:, :, 0].unsqueeze(3).broadcast_to([N, 2, H, 8]),
                                  top16[:, :, 1].unsqueeze(3).broadcast_to([N, 2, H, 8]), ALU.max).then_inc(s["max_ready"], 1)

            def output(i):
                dve.wait_ge(s["av_done"], i + 1)
                dve.reciprocal(inv[:], ps_o[:, NP:NP + N]).then_inc(s["inv_done"], 1)
                dve.wait_ge(s["inv_done"], i + 1)
                dve.tensor_tensor(o_cm[:, span(i, 1), 0:N].rearrange("p i n -> p (i n)"), ps_o[:, 0:N], inv[:], ALU.mult).then_inc(s["out_done"], 1)

            def shifted(prev, first=False):
                dve.wait_ge(s["max_out"], prev + 1)
                dve.wait_ge(s["av_done"], prev)
                dve.tensor_tensor(prob[:].rearrange("p (j t) n -> p j t n", t=2), ps_a[:, :, 0:2 * N2].rearrange("p j (t n) -> p j t n", t=2),
                                  shift[:].unsqueeze(1).unsqueeze(1).broadcast_to([128, 3, 2, N2]), ALU.subtract).then_inc(s["sub_done"], 1)

            def sums_of(prev):
                dve.wait_ge(s["exp_done"], prev + 1)
                dve.tensor_reduce(sums[:, 0, :], prob[:, 0:4, :].rearrange("p t n -> p n t"), AX.X, ALU.add)
                dve.tensor_tensor(sums[:, 1, :], prob[:, 4, :], prob[:, 5, :], ALU.add).then_inc(s["sum_done"], 1)

            def step(i, a, has_prev, has_next):
                if has_prev:
                    maxima(i - 1)
                if has_next:
                    queries(i + 1, 1 - a)
                if has_prev:
                    shifted(i - 1)
                    if has_prev == "two":
                        output(i - 2)
                    sums_of(i - 1)

            dve.memset(q_z[:], 0.0).then_inc(s["q_zero"], 1)
            dve.wait_ge(s["q_zero"], 1)
            queries(0, 0)
            step(0, 0, False, True)
            step(1, 1, True, True)
            with dve.Fori(1, (PAIRS) // 2 - 1) as twice:
                i = twice * 2
                step(i, 0, "two", True)
                step(i + 1, 1, "two", True)
            step(PAIRS - 2, 0, "two", True)
            step(PAIRS - 1, 1, "two", False)
            maxima(PAIRS - 1)
            shifted(PAIRS - 1)
            output(PAIRS - 2)
            sums_of(PAIRS - 1)
            output(PAIRS - 1)


def feed_forward(nc, tokens, o_cm, out, k):
    sem = nc.semaphore
    with ExitStack() as ctx:
        names = ("proj_done h1_done mean_done centered squared var_done std_done rstd_done xn_done hid_done hid_out sel_done "
                 "lay_done lay_out out_done row_out")
        s = {n: ctx.enter_context(sem("f_" + n)) for n in names.split()}
        stored = [ctx.enter_context(sem(f"out_stored{a}")) for a in range(2)]

        def sb(name, shape):
            return ctx.enter_context(nc.sbuf_tensor(name, shape, F32))

        h1 = sb("h1", [128, 2, CP, N])
        xc = sb("f_xc", [128, 2, CP, N])
        sq = sb("f_sq", [128, 2, CP, N])
        rstd = sb("f_rstd", [128, 2, CP, N])
        xn = sb("f_xn", [128, 2, CP, N])
        hid = sb("hid", [128, 3, CP, 2, N])
        w_sel = sb("w_sel", [128, 2, CP, LAYERS, HID + 1])
        rows = sb("rows", [N, 2, CP, 2 * C])
        ps = ctx.enter_context(nc.psum_tensor("ps_f", [128, 8, 512], F32))
        block = ctx.enter_context(nc.Block())
        W = CP * N

        def flat(view):
            return view.rearrange("p r m -> p (r m)")

        @block.sync
        def _(sp):
            def store(c, a):
                sp.wait_ge(s["row_out"], CP * (c + 1))
                sp.dma_start(out[span(c, 2 * CP)].rearrange("b n f -> n b f"),
                             rows[:, a].rearrange("n r (b f) -> n (r b) f", b=2)).then_inc(stored[a], 16)

            with sp.Fori(0, (NCH) // 2) as twice:
                c = twice * 2
                store(c, 0)
                store(c + 1, 1)
            for a in range(2):
                sp.wait_ge(stored[a], 16 * NCH // 2)

        @block.gpsimd
        def _(pool):
            def select(c, a):
                if not (isinstance(c, int) and c < 2):
                    pool.wait_ge(s["lay_out"], 2 * CP * (c - 1))
                for r in range(CP):
                    e = pool.value_load(k["route"][0:1, span(c * CP + r, 1)], min_val=0, max_val=EXP)
                    pool.tensor_copy(w_sel[:, a, r].rearrange("p l f -> p (l f)"),
                                     k["ffn_w"][:, bass.ds(e, 1)].rearrange("p e l f -> p (e l f)")).then_inc(s["sel_done"], 1)

            select(0, 0)
            select(1, 1)
            with pool.Fori(1, (NCH) // 2) as twice:
                c = twice * 2
                select(c, 0)
                select(c + 1, 1)

        @block.tensor
        def _(pe):
            def norm(c, a, n):
                pe.wait_ge(s["h1_done"], c)
                pe.matmul(ps[:, 0, 0:W], k["w_bd"][:, 3, :], o_cm[:, span(c, CP), 0:N], start=True, stop=True).then_inc(s["proj_done"], 1)
                pe.wait_ge(s["h1_done"], c + 1)
                pe.wait_ge(s["centered"], c)
                pe.matmul(ps[:, 1, 0:W], k["mean_w"][:], flat(h1[:, a]), start=True, stop=True).then_inc(s["mean_done"], 1)
                pe.wait_ge(s["squared"], c + 1)
                pe.wait_ge(s["std_done"], c)
                pe.matmul(ps[:, 2, 0:W], k["mean_w"][:], flat(sq[:, a]), start=True, stop=True).then_inc(s["var_done"], 1)

            def layers(c, a, n):
                pe.wait_ge(s["xn_done"], c + 1)
                for b in range(2):
                    pe.wait_ge(s["hid_out"], 2 * c + b)
                    pe.matmul(ps[:, 3, 0:W], k["wi_bd"][:, b, :], flat(xn[:, a]), start=True, stop=True).then_inc(s["hid_done"], 1)
                pe.wait_ge(s["hid_out"], 2 * c + 2)
                for l in range(LAYERS):
                    for r in range(CP):
                        u = l * CP + r
                        pe.wait_ge(s["sel_done"], CP * c + r + 1)
                        pe.wait_ge(s["lay_out"], 2 * CP * c + (u - 1 if u else 0))
                        if l:
                            pe.wait_ge(s["lay_out"], 2 * CP * c + r + 1)
                        pe.matmul(ps[:, 4 + u % 2, 0:2 * N], w_sel[:, a, r, l, 0:HID], hid[:, l, r].rearrange("p b n -> p (b n)"),
                                  start=True, stop=True).then_inc(s["lay_done"], 1)
                for r in range(CP):
                    pe.wait_ge(s["lay_out"], 2 * CP * c + CP + r + 1)
                    pe.wait_ge(s["row_out"], CP * c + max(r - 1, 0))
                    o = ps[0:N, 6 + r % 2, 0:2 * C]
                    pe.matmul(o, h1[:, a, r, :], k["ident"][:], start=True, stop=False, skip_group_check=True)
                    for b in range(2):
                        mm = pe.matmul(o[:, C * b:C * b + C], hid[:, 2, r, b, :], k["wo_t"][:], start=False, stop=True, skip_group_check=True)
                    mm.then_inc(s["out_done"], 1)

            two_stages(pe, NCH, norm, layers)

        @block.scalar
        def _(act):
            def norm(c, a, n):
                act.wait_ge(s["centered"], c + 1)
                act.wait_ge(s["var_done"], c)
                act.activation(sq[:, a], xc[:, a], ACT.Square).then_inc(s["squared"], 1)
                act.wait_ge(s["var_done"], c + 1)
                act.wait_ge(s["xn_done"], c)
                act.activation(flat(rstd[:, a]), ps[:, 2, 0:W], ACT.Sqrt, bias=k["ln_eps"][:, 0:1]).then_inc(s["std_done"], 1)

            def layers(c, a, n):
                for b in range(2):
                    act.wait_ge(s["hid_done"], 2 * c + b + 1)
                    act.wait_ge(s["lay_done"], 2 * CP * c)
                    act.activation(hid[:, 0, :, b, :], ps[:, 3, 0:W].rearrange("p (r n) -> p r n", r=CP), ACT.Relu,
                                   bias=k["ffn_bias"][:, 34:35]).then_inc(s["hid_out"], 1)
                for l in range(LAYERS):
                    for r in range(CP):
                        u = l * CP + r
                        act.wait_ge(s["lay_done"], 2 * CP * c + u + 1)
                        act.wait_ge(s["out_done"], CP * c)
                        act.activation(hid[:, l + 1, r].rearrange("p b n -> p (b n)"), ps[:, 4 + u % 2, 0:2 * N], ACT.Relu,
                                       bias=w_sel[:, a, r, l, HID:HID + 1]).then_inc(s["lay_out"], 1)

            two_stages(act, NCH, norm, layers)

        @block.vector
        def _(dve):
            def norm(c, a, n):
                dve.wait_ge(s["proj_done"], c + 1)
                if not (isinstance(c, int) and c < 2):
                    dve.wait_ge(s["out_done"], CP * (c - 1))
                dve.scalar_tensor_tensor(out=h1[:, a], in0=ps[:, 0, 0:W].rearrange("p (r n) -> p r n", r=CP), scalar=k["proj_bias"][:, 0:1],
                                         in1=tokens[:, span(c, CP), 0:N], op0=ALU.add, op1=ALU.add).then_inc(s["h1_done"], 1)
                dve.wait_ge(s["mean_done"], c + 1)
                dve.wait_ge(s["h1_done"], c + 1)
                dve.tensor_tensor(flat(xc[:, a]), flat(h1[:, a]), ps[:, 1, 0:W], ALU.subtract).then_inc(s["centered"], 1)
                dve.wait_ge(s["std_done"], c + 1)
                dve.reciprocal(rstd[:, a], rstd[:, a]).then_inc(s["rstd_done"], 1)
                dve.wait_ge(s["rstd_done"], c + 1)
                if not (isinstance(c, int) and c < 2):
                    dve.wait_ge(s["hid_done"], 2 * (c - 1))
                dve.tensor_tensor(xn[:, a], xc[:, a], rstd[:, a], ALU.mult).then_inc(s["xn_done"], 1)

            def layers(c, a, n):
                dve.wait_ge(stored[a], 16 * n)
                for r in range(CP):
                    dve.wait_ge(s["out_done"], CP * c + r + 1)
                    dve.tensor_tensor(rows[:, a, r, :], ps[0:N, 6 + r % 2, 0:2 * C], k["bo_row"][:].rearrange("p b f -> p (b f)"),
                                      ALU.add).then_inc(s["row_out"], 1)

            two_stages(dve, NCH, norm, layers)


def audio_layer(nc, p, out, debug=None):
    with ExitStack() as ctx:
        def sb(name, shape, dt=F32):
            return ctx.enter_context(nc.sbuf_tensor(name, shape, dt))

        k = {
            "ident": sb("ident", [128, 128]), "ident_g": sb("ident_g", [128, 4, 128]),
            "score_w": sb("score_w", [128, GP, 32]), "pair_sel": sb("pair_sel", [96, GP, 128], BF16),
            "mean_w": sb("mean_w", [128, 128]), "w_bd": sb("w_bd", [128, 4, 128]), "w_tok": sb("w_tok", [128, 2, 192]),
            "wi_bd": sb("wi_bd", [128, 2, HID]), "wo_t": sb("wo_t", [128, C]), "mask16": sb("mask16", [128, 16]),
            "delta_q": sb("delta_q", [128, 16, 8]), "delta": sb("delta", [128, 8]), "hmask": sb("hmask", [128, 8]),
            "conv1": sb("conv1", [128, 8]), "mix_w": sb("mix_w", [128, 64]), "conv_const": sb("conv_const", [128, 1]),
            "vmask": sb("vmask", [128, NT, H]), "den_w": sb("den_w", [128, 2, 64]), "tok_bias": sb("tok_bias", [32, 1]),
            "qkv_bias": sb("qkv_bias", [128, 3]), "proj_bias": sb("proj_bias", [128, 1]), "ln_eps": sb("ln_eps", [128, 1]),
            "bias_row": sb("bias_row", [96, 2, 192]), "bo_row": sb("bo_row", [N, 2, C]),
            "ffn_w": sb("ffn_w", [128, EXP + 1, LAYERS, HID + 1]), "ffn_bias": sb("ffn_bias", [128, 35]),
            "route_in": sb("route_in", [1, PAIRS], I32), "route": sb("route", [1, PAIRS], I32),
        }
        tokens = sb("tokens", [128, PAIRS, NP])
        v_dram = nc.dram_tensor("v_rows", (B, NP, C), F32).ap()
        top_dram = nc.dram_tensor("top_rows", (B, D, 2 * C), F32).ap()

        constants(nc, sb, p, k)
        pool_windows(nc, p["x"], tokens, k)
        with nc.sbuf_tensor("q_cm", [128, PAIRS, NP], F32) as q_cm, nc.sbuf_tensor("k_cm", [128, PAIRS, NP], F32) as k_cm, \
                nc.sbuf_tensor("m_t", [128, PAIRS, D], F32) as m_t:
            with nc.sbuf_tensor("gram", [128, B, 32], F32) as gram:
                project(nc, tokens, q_cm, k_cm, gram, v_dram, top_dram, k)
                orthogonalise(nc, gram, m_t, top_dram, k)
            attend(nc, q_cm, k_cm, m_t, q_cm, v_dram, k)
            feed_forward(nc, tokens, q_cm, out, k)


_PARAMS = {
    "tok_w": "L0_tok_w", "tok_b": "L0_tok_b", "w_qkv": "L0_attn_w_qkv", "b_qkv": "L0_attn_b_qkv", "w_proj": "L0_attn_w_proj",
    "b_proj": "L0_attn_b_proj", "scale": "L0_attn_scale", "riem_scale": "L0_attn_riem_scale",
    "grassman_scale": "L0_attn_grassman_scale", "bn_gamma": "L0_attn_bn_gamma", "bn_beta": "L0_attn_bn_beta",
    "bn_mean": "L0_attn_bn_mean", "bn_var": "L0_attn_bn_var", "conv_w": "L0_attn_conv_w", "conv_b": "L0_attn_conv_b",
    "route_id": "L0_ffn_route_id", "Wi": "L0_ffn_Wi", "bi": "L0_ffn_bi", "Wr": "L0_ffn_Wr", "br": "L0_ffn_br",
    "Ws": "L0_ffn_Ws", "bs": "L0_ffn_bs", "Wo": "L0_ffn_Wo", "bo": "L0_ffn_bo", "x": "x",
    "conv_wt": "conv_wt",
}
_SHAPES = {"scale": (1, 1), "riem_scale": (1, 1), "grassman_scale": (1, 1), "route_id": (1, PAIRS)}


def kernel(**inputs):
    import numpy as _np
    import concourse.bacc as _bacc
    from concourse import mybir as _mybir
    from concourse.bass_utils import run_bass_kernel_spmd as _run

    nc = _bacc.Bacc("TRN2", target_bir_lowering=False, num_devices=1)
    arrays, p = {}, {}
    inputs["conv_wt"] = inputs["L0_attn_conv_w"].T
    for name, given in _PARAMS.items():
        a = _np.ascontiguousarray(inputs[given])
        a = a.reshape(_SHAPES.get(name, a.shape))
        arrays[f"in_{name}_dram"] = a
        p[name] = nc.dram_tensor(f"in_{name}_dram", a.shape, _mybir.dt.from_np(a.dtype), kind="ExternalInput").ap()
    out = nc.dram_tensor("out_0_dram", (B, N, C), F32, kind="ExternalOutput").ap()
    audio_layer(nc, p, out)
    r = _run(nc, [arrays], core_ids=[0])
    return r.results[0]["out_0_dram"]
```

```python
from contextlib import ExitStack

import numpy as np
import concourse.bass as bass
import concourse.mybir as mybir

F32 = mybir.dt.float32
BF16 = mybir.dt.bfloat16
I32 = mybir.dt.int32
ALU = mybir.AluOpType
ACT = mybir.ActivationFunctionType
AX = mybir.AxisListType

B, C, T = 128, 64, 750
WIN = 8
N = (T + WIN - 1) // WIN
NP = 96
TP = N * WIN
H, D = 8, 8
PAIRS = B // 2
NT, NTAU = 6, 12
HID, EXP, LAYERS = 128, 16, 2
GP = 16
NG = PAIRS // GP
CP = 4
NCH = PAIRS // CP
HALF = TP // 2
LN_EPS = 1e-5
BN_EPS = 1e-5


def raw(ap, offset, pattern):
    return bass.AP(ap.tensor, offset, pattern)


def constants(nc, p, x_g, x_in, k):
    sem = nc.semaphore
    with ExitStack() as ctx:
        param_in = ctx.enter_context(sem("param_in"))
        pool_step = ctx.enter_context(sem("pool_step"))
        dve_step = ctx.enter_context(sem("dve_step"))
        act_step = ctx.enter_context(sem("act_step"))
        pe_step = ctx.enter_context(sem("pe_step"))
        upper = ctx.enter_context(nc.sbuf_tensor("upper", [128, 1], F32))
        mask4 = ctx.enter_context(nc.sbuf_tensor("mask4", [128, 4], F32))
        bn_rows = ctx.enter_context(nc.sbuf_tensor("bn_rows", [128, 4, 24], F32))
        dot_sum = ctx.enter_context(nc.sbuf_tensor("dot_sum", [128, 1], F32))
        w_in = ctx.enter_context(nc.sbuf_tensor("w_in", [128, 4, 64], F32))
        wr_in = ctx.enter_context(nc.sbuf_tensor("wr_in", [128, 34, 128], F32))
        wi_in = ctx.enter_context(nc.sbuf_tensor("wi_in", [128, 64], F32))
        wo_in = ctx.enter_context(nc.sbuf_tensor("wo_in", [64, 128], F32))
        bias_in = ctx.enter_context(nc.sbuf_tensor("bias_in", [35, 128], F32))
        cols = k["cols"]
        tokw, conv2, conv_rows = cols[:, 5:6], cols[:, 24:32], cols[:, 32:56]
        bn_col = cols[:, 8:12].rearrange("p (n v) -> p n v", n=2)
        route_f = ctx.enter_context(nc.sbuf_tensor("route_f", [1, 5, PAIRS], F32))
        shared_t = ctx.enter_context(nc.sbuf_tensor("shared_t", [128, 2, 128], F32))
        ps_t = ctx.enter_context(nc.psum_tensor("ps_t", [128, 4, 512], F32))
        block = ctx.enter_context(nc.Block())
        LOADS = []
        marks = {}

        @block.sync
        def _(sp):
            def load(dst, src):
                sp.dma_start(dst, src).then_inc(param_in, 16)
                LOADS.append(1)

            load(cols[:], p["columns"])
            load(w_in[:], p["square"])
            load(k["bias_row"][:].rearrange("n b f -> n (b f)"), raw(p["rows"], 0, [[0, NP], [1, 2 * 3 * C]]))
            load(k["bo_row"][:].rearrange("n b f -> n (b f)"), raw(p["rows"], 2 * 3 * C, [[0, N], [1, 2 * C]]))
            load(bn_rows[:].rearrange("p n f -> p (n f)"), raw(p["rows"], 2 * 4 * C, [[0, 128], [1, 4 * 3 * H]]))
            load(wi_in[:, :], p["Wi"])
            load(wo_in[:, :], p["Wo"])
            load(bias_in[:, :], p["biases"])
            load(k["route_in"][:, :], p["route_id"])
            load(wr_in[:, 32:34, :], raw(p["Ws"], 0, [[128, 128], [16384, 2], [1, 128]]))
            load(wr_in[:, 0:32, :], raw(p["Wr"], 0, [[128, 128], [16384, 32], [1, 128]]))
            sp.wait_ge(param_in, 16 * len(LOADS))

        n_loads = len(LOADS)

        @block.gpsimd
        def _(pool):
            done = 0

            def step(ins):
                nonlocal done
                done += 1
                ins.then_inc(pool_step, 1)
                pool.wait_ge(pool_step, done)

            def diagonal(view, base, pattern, mult):
                step(pool.affine_select(out=view, in_=view, compare_op=ALU.not_equal, fill=1.0, base=base,
                                        pattern=pattern, channel_multiplier=mult))

            for name in ("ident", "score_w", "delta_q", "mean_w", "w_bd", "w_tok", "wi_bd", "pair_sel"):
                step(pool.memset(k[name][:], 0.0))
            step(pool.memset(k["mask16"][:], 1.0))
            step(pool.memset(k["ln_eps"][:], LN_EPS))
            step(pool.memset(upper[0:64, :], 0.0))
            step(pool.memset(upper[64:128, :], 1.0))
            diagonal(k["ident"][:], 0, [[-1, 128]], 1)
            for b in range(2):
                q = slice(64 * b, 64 * b + 64)
                diagonal(k["score_w"][q], -b, [[-2, GP], [1, 32]], 0)
                step(pool.memset(k["mean_w"][q, q], 1.0 / C))
            m = k["mask16"][:]
            step(pool.affine_select(out=m, in_=m, compare_op=ALU.is_ge, fill=0.0, base=0,
                                    pattern=[[-8, 16]], channel_multiplier=1))
            step(pool.affine_select(out=m, in_=m, compare_op=ALU.is_ge, fill=0.0, base=7,
                                    pattern=[[8, 16]], channel_multiplier=-1))
            diagonal(k["delta_q"][:], 0, [[-8, 16], [-1, 8]], 1)
            for part in range(3):
                diagonal(k["pair_sel"][32 * part:32 * part + 32], 0, [[-2, GP], [-1, 2], [0, 64]], 1)
            marks["pool"] = done

        @block.scalar
        def _(act):
            for g in range(2):
                load_group(act, p["x"], x_g, x_in, g, g)
            act.wait_ge(dve_step, 2)
            act.activation(bn_rows[:, 3, :], bn_rows[:, 3, :], ACT.Sqrt).then_inc(act_step, 1)
            act.activation(bn_col[:, :, 1], bn_col[:, :, 1], ACT.Sqrt).then_inc(act_step, 1)

        @block.vector
        def _(dve):
            done = 0

            def step(ins):
                nonlocal done
                done += 1
                ins.then_inc(dve_step, 1)
                dve.wait_ge(dve_step, done)

            dve.wait_ge(param_in, 16 * n_loads)
            step(dve.tensor_scalar(bn_rows[:, 3, :], bn_rows[:, 3, :], BN_EPS, None, ALU.add))
            step(dve.tensor_scalar(bn_col[:, :, 1], bn_col[:, :, 1], BN_EPS, None, ALU.add))
            dve.wait_ge(act_step, 2)
            step(dve.reciprocal(bn_rows[:, 3, :], bn_rows[:, 3, :]))
            step(dve.reciprocal(bn_col[:, :, 1], bn_col[:, :, 1]))
            step(dve.tensor_tensor(bn_rows[:, 0, :], bn_rows[:, 0, :], bn_rows[:, 3, :], ALU.mult))
            step(dve.tensor_tensor(bn_col[:, :, 0], bn_col[:, :, 0], bn_col[:, :, 1], ALU.mult))
            step(dve.tensor_tensor(bn_rows[:, 2, :], bn_rows[:, 2, :], bn_rows[:, 0, :], ALU.mult))
            step(dve.tensor_tensor(bn_rows[:, 1, :], bn_rows[:, 1, :], bn_rows[:, 2, :], ALU.subtract))
            step(dve.tensor_tensor(conv_rows, conv_rows, bn_rows[:, 1, :], ALU.mult))
            step(dve.tensor_reduce(dot_sum[:], conv_rows, AX.X, ALU.add))
            step(dve.tensor_tensor(k["conv_const"], k["conv_const"], dot_sum[:], ALU.add))
            step(dve.tensor_scalar(k["conv1"], k["conv1"], bn_col[:, 0, 0:1], cols[:, 6:7], ALU.mult, ALU.mult))
            step(dve.tensor_scalar(conv2, conv2, bn_col[:, 1, 0:1], cols[:, 7:8], ALU.mult, ALU.mult))
            dve.wait_ge(pool_step, marks["pool"])
            step(dve.tensor_reduce(k["delta"][:], k["delta_q"][:].rearrange("p q m -> p m q"), AX.X, ALU.add))
            step(dve.tensor_tensor(k["hmask"][:], k["mask16"][:, 0:8], k["mask16"][:, 8:16], ALU.add))
            step(dve.tensor_reduce(mask4[:], k["mask16"][:].rearrange("p (j g) -> p g j", g=4), AX.X, ALU.add))
            for g in range(4):
                step(dve.tensor_scalar(k["ident_g"][:, g, :], k["ident"][:], mask4[:, g:g + 1], None, ALU.mult))
            step(dve.tensor_tensor(k["mix_w"][:].rearrange("p (o m) -> p o m", o=8),
                                   conv2.unsqueeze(2).broadcast_to([128, 8, 8]),
                                   k["delta"][:].unsqueeze(1).broadcast_to([128, 8, 8]), ALU.mult))
            step(dve.tensor_scalar(k["score_w"][:], k["score_w"][:], tokw, None, ALU.mult))
            step(dve.tensor_tensor(upper[:], upper[:], k["delta"][:, 7:8], ALU.mult))
            step(dve.tensor_scalar(upper[:], upper[:], -1.0, 1.0, ALU.mult, ALU.add))
            for t in range(NT):
                if t < 4:
                    step(dve.tensor_copy(k["vmask"][:, t, :], k["hmask"][:]))
                else:
                    step(dve.tensor_scalar(k["vmask"][:, t, :], k["hmask"][:], upper[:, 0:1], None, ALU.mult))
            for n, t in enumerate((0, 4)):
                step(dve.tensor_copy(k["den_w"][:, n, :].rearrange("p (o d) -> p o d", o=8),
                                     k["vmask"][:, t, :].unsqueeze(2).broadcast_to([128, 8, 8])))
            dve.wait_ge(pe_step, 1)
            for b in range(2):
                q = slice(64 * b, 64 * b + 64)
                for s in range(4):
                    step(dve.tensor_copy(k["w_bd"][q, s, q], ps_t[q, 0, s * 128 + 64 * b:s * 128 + 64 * b + 64]))
            marks["weights out"] = done
            dve.wait_ge(pe_step, 2)
            for b in range(2):
                q = slice(64 * b, 64 * b + 64)
                for s in range(3):
                    step(dve.tensor_copy(k["w_tok"][q, b, 64 * s:64 * s + 64], k["w_bd"][q, s, q]))
                step(dve.tensor_copy(k["wi_bd"][q, b, :], ps_t[q, 1, 0:128]))
            step(dve.tensor_copy(k["wo_t"][:], ps_t[:, 1, 128:192]))
            step(dve.tensor_copy(k["ffn_bias"][:, 0:35], ps_t[:, 1, 192:227]))
            for l in range(LAYERS):
                dve.wait_ge(pe_step, 3)
                step(dve.tensor_tensor(shared_t[:, l, :], ps_t[:, 2, l * 128:l * 128 + 128], k["ident"][:], ALU.add))
                step(dve.tensor_copy(k["ffn_w"][:, EXP, l, 0:HID], shared_t[:, l, :]))
            marks["shared out"] = done
            for n in range(8):
                dve.wait_ge(pe_step, 4 + n)
                for q in range(4):
                    l, e = divmod(4 * n + q, EXP)
                    step(dve.tensor_tensor(k["ffn_w"][:, e, l, 0:HID], ps_t[:, 3 if n % 2 else 0, q * 128:q * 128 + 128],
                                           shared_t[:, l, :], ALU.add))
            for l in range(LAYERS):
                step(dve.tensor_copy(k["ffn_w"][:, EXP, l, HID:HID + 1], k["ffn_bias"][:, 32 + l:33 + l]))
                step(dve.tensor_scalar(k["ffn_w"][:, 0:EXP, l, HID], k["ffn_bias"][:, 16 * l:16 * l + 16],
                                       k["ffn_bias"][:, 32 + l:33 + l], None, ALU.add))
            step(dve.tensor_copy(route_f[:, 0, :], k["route_in"][:, :]))
            step(dve.tensor_scalar(route_f[:, 1, :], route_f[:, 0, :], 0.0, None, ALU.is_ge))
            step(dve.tensor_scalar(route_f[:, 2, :], route_f[:, 0, :], float(EXP), None, ALU.is_lt))
            step(dve.tensor_tensor(route_f[:, 1, :], route_f[:, 1, :], route_f[:, 2, :], ALU.mult))
            step(dve.tensor_scalar(route_f[:, 3, :], route_f[:, 0, :], 0.0, float(EXP), ALU.max, ALU.min))
            step(dve.tensor_scalar(route_f[:, 3, :], route_f[:, 3, :], -float(EXP), None, ALU.add))
            step(dve.tensor_tensor(route_f[:, 3, :], route_f[:, 3, :], route_f[:, 1, :], ALU.mult))
            step(dve.tensor_scalar(k["route"][:, :], route_f[:, 3, :], float(EXP), None, ALU.add))

        @block.tensor
        def _(pe):
            pe.wait_ge(param_in, 16 * n_loads)
            pe.wait_ge(pool_step, marks["pool"])
            for s in range(4):
                mm = pe.transpose(ps_t[0:64, 0, s * 128:s * 128 + 128], w_in[:, s, :], k["ident"][:])
            mm = pe.transpose(ps_t[0:64, 1, 0:128], wi_in[:, :], k["ident"][:])
            for s in range(4):
                mm = pe.matmul(ps_t[64:128, 0, s * 128:s * 128 + 128], w_in[:, s, :], k["ident"][:], start=True, stop=True)
            mm.then_inc(pe_step, 1)
            pe.matmul(ps_t[64:128, 1, 0:128], wi_in[:, :], k["ident"][:], start=True, stop=True)
            pe.transpose(ps_t[:, 1, 128:192], wo_in[:, :], k["ident"][0:64, 0:64])
            pe.transpose(ps_t[:, 1, 192:227], bias_in[0:35, :], k["ident"][0:35, 0:35]).then_inc(pe_step, 1)
            for l in range(LAYERS):
                mm = pe.transpose(ps_t[:, 2, l * 128:l * 128 + 128], wr_in[:, 32 + l, :], k["ident"][:])
            mm.then_inc(pe_step, 1)
            for n in range(8):
                if n == 0:
                    pe.wait_ge(dve_step, marks["weights out"])
                if n >= 2:
                    pe.wait_ge(dve_step, marks["shared out"] + 4 * (n - 1))
                for q in range(4):
                    mm = pe.transpose(ps_t[:, 3 if n % 2 else 0, q * 128:q * 128 + 128], wr_in[:, 4 * n + q, :], k["ident"][:])
                mm.then_inc(pe_step, 1)



GROUP_LOADS = GP // 4


def load_group(eng, x, x_g, x_in, g, a, used=None):
    rows = x.rearrange("b f t -> (b f) t").rearrange("(n p) t -> p n t", p=128)
    for q in range(GROUP_LOADS):
        at = g * GP + 4 * q
        if used is not None:
            eng.wait_ge(used, (g - 2) * GROUP_LOADS + q + 1)
        eng.dma_start(x_g[:, a, 4 * q:4 * q + 4, 0:T],
                      rows[:, slice(at, at + 4) if isinstance(g, int) else bass.ds(at, 4), :]).then_inc(x_in[a][q], 16)


def pool_windows(nc, x, x_g, x_in, tokens, k):
    sem = nc.semaphore
    with ExitStack() as ctx:
        x_used = ctx.enter_context(sem("x_used"))
        pad_zero = ctx.enter_context(sem("pad_zero"))
        scores_done = ctx.enter_context(sem("scores_done"))
        scores_out = ctx.enter_context(sem("scores_out"))
        shifted = ctx.enter_context(sem("shifted"))
        exps = ctx.enter_context(sem("exps"))
        dve_step = ctx.enter_context(sem("dve_step"))
        weights_done = ctx.enter_context(sem("weights_done"))
        spread_done = ctx.enter_context(sem("spread_done"))
        spread_used = ctx.enter_context(sem("spread_used"))
        soft = ctx.enter_context(nc.sbuf_tensor("soft", [32, N, WIN], F32))
        rest = ctx.enter_context(nc.sbuf_tensor("rest", [32, TP], F32))
        stat = ctx.enter_context(nc.sbuf_tensor("stat", [32, 2, N], F32))
        parts = ctx.enter_context(nc.sbuf_tensor("parts", [96, TP], BF16))
        prod = ctx.enter_context(nc.sbuf_tensor("prod", [128, 2, TP], F32))
        ps_score = ctx.enter_context(nc.psum_tensor("ps_score", [32, 2, 512], F32))
        ps_spread = ctx.enter_context(nc.psum_tensor("ps_spread", [128, 4, 512], F32))
        block = ctx.enter_context(nc.Block())
        @block.sync
        def _(sp):
            with sp.Fori(1, NG // 2) as n:
                for a in range(2):
                    load_group(sp, x, x_g, x_in, 2 * n + a, a, x_used)

        def groups(eng, group):
            with eng.Fori(0, NG // 2 - 1) as n:
                group(2 * n, 0, n, True)
                group(2 * n + 1, 1, n, True)
            group(NG - 2, 0, NG // 2 - 1, True)
            group(NG - 1, 1, NG // 2 - 1, False)

        @block.tensor
        def _(pe):
            def score(a, n, turn):
                if n % 4 == 0:
                    pe.wait_ge(x_in[a][n // 4], 16 * (turn + 1))
                for half in range(2):
                    mm = pe.matmul(ps_score[:, half, 0:HALF], k["score_w"][:, n, :], x_g[:, a, n, half * HALF:half * HALF + HALF],
                                   start=(n == 0), stop=(n == GP - 1))
                return mm

            def group(g, a, twin, has_next):
                if has_next:
                    pe.wait_ge(scores_out, g + 1)
                pe.wait_ge(weights_done, g + 1)
                for n in range(GP):
                    pe.wait_ge(spread_used, g * GP + n + 1)
                    for half in range(2):
                        mm = pe.matmul(ps_spread[:, 2 * (n % 2) + half, 0:HALF], k["pair_sel"][:, n, :],
                                       parts[:, half * HALF:half * HALF + HALF], start=True, stop=True)
                    mm.then_inc(spread_done, 1)
                    if has_next:
                        mm = score(1 - a, n, twin + a)
                if has_next:
                    mm.then_inc(scores_done, 1)

            pe.wait_ge(pad_zero, 1)
            for n in range(GP):
                mm = score(0, n, 0)
            mm.then_inc(scores_done, 1)
            groups(pe, group)

        @block.scalar
        def _(act):
            with act.Fori(0, NG) as g:
                act.wait_ge(scores_done, g + 1)
                act.wait_ge(weights_done, g)
                act.activation(soft[:].rearrange("p w k -> p (w k)").rearrange("p (a t) -> p a t", a=2),
                               ps_score[:, :, 0:HALF], ACT.Identity, bias=k["tok_bias"]).then_inc(scores_out, 1)
                act.wait_ge(shifted, g + 1)
                act.activation(soft[:], soft[:], ACT.Exp).then_inc(exps, 1)

        @block.vector
        def _(dve):
            def softmax(i):
                def step(n, ins):
                    ins.then_inc(dve_step, 1)
                    dve.wait_ge(dve_step, i * 8 + n)

                def over(view):
                    return view.unsqueeze(2).broadcast_to([32, N, WIN])

                dve.wait_ge(scores_out, i + 1)
                step(1, dve.tensor_reduce(stat[:, 0, :], soft[:], AX.X, ALU.max))
                dve.tensor_tensor(soft[:], soft[:], over(stat[:, 0, :]), ALU.subtract).then_inc(shifted, 1)
                dve.wait_ge(exps, i + 1)
                step(2, dve.tensor_reduce(stat[:, 0, :], soft[:], AX.X, ALU.add))
                step(3, dve.reciprocal(stat[:, 1, :], stat[:, 0, :]))
                step(4, dve.tensor_tensor(soft[:], soft[:], over(stat[:, 1, :]), ALU.mult))
                flat = soft[:].rearrange("p w k -> p (w k)")
                dve.wait_ge(spread_done, i * GP)
                step(5, dve.tensor_copy(parts[0:32, :], flat))
                step(6, dve.tensor_tensor(rest[:], flat, parts[0:32, :], ALU.subtract))
                step(7, dve.tensor_copy(parts[32:64, :], rest[:]))
                step(8, dve.tensor_tensor(flat, rest[:], parts[32:64, :], ALU.subtract))
                dve.tensor_copy(parts[64:96, :], flat).then_inc(weights_done, 1)

            def group(g, a, twin, has_next):
                for n in range(GP):
                    dve.wait_ge(spread_done, g * GP + n + 1)
                    dve.tensor_tensor(prod[:, n % 2, :].rearrange("p (a t) -> p a t", a=2),
                                      x_g[:, a, n, :].rearrange("p (a t) -> p a t", a=2),
                                      ps_spread[:, 2 * (n % 2):2 * (n % 2) + 2, 0:HALF], ALU.mult).then_inc(spread_used, 1)
                    dve.wait_ge(spread_used, g * GP + n + 3)
                    at = slice(g * GP + n, g * GP + n + 1) if isinstance(g, int) else bass.ds(g * GP + n, 1)
                    dve.tensor_reduce(tokens[:, at, 0:N], prod[:, n % 2, :].rearrange("p (w k) -> p w k", k=WIN), AX.X, ALU.add)
                    if n % 4 == 3:
                        dve.sem_inc(x_used, 1)
                if has_next:
                    softmax(g + 1)

            dve.memset(x_g[:, :, :, T:TP], 0.0).then_inc(pad_zero, 1)
            dve.sem_inc(spread_used, 2)
            softmax(0)
            groups(dve, group)


def span(c, n):
    return slice(c * n, c * n + n) if isinstance(c, int) else bass.ds(c * n, n)


def two_stages(eng, count, first, second, order):
    def both(c, a, n):
        for stage, part in order:
            if stage:
                second(part, c, a, n)
            else:
                first(part, c + 1, 1 - a, n + a)

    def alone(stage, which, c, a, n):
        for s, part in order:
            if s == which:
                stage(part, c, a, n)

    alone(first, 0, 0, 0, 0)
    with eng.Fori(0, count // 2 - 1) as n:
        both(2 * n, 0, n)
        both(2 * n + 1, 1, n)
    both(count - 2, 0, count // 2 - 1)
    alone(second, 1, count - 1, 1, count // 2 - 1)


def project(nc, tokens, q_cm, k_cm, gram, v_dram, top_dram, k):
    sem = nc.semaphore
    with ExitStack() as ctx:
        pads = ctx.enter_context(sem("pads"))
        mean_done = ctx.enter_context(sem("mean_done"))
        centered = ctx.enter_context(sem("centered"))
        squared = ctx.enter_context(sem("squared"))
        var_done = ctx.enter_context(sem("var_done"))
        std_done = ctx.enter_context(sem("std_done"))
        rstd_done = ctx.enter_context(sem("rstd_done"))
        xn_done = ctx.enter_context(sem("xn_done"))
        qk_done = ctx.enter_context(sem("qk_done"))
        qk_out = ctx.enter_context(sem("qk_out"))
        tok_done = ctx.enter_context(sem("tok_done"))
        tok_out = ctx.enter_context(sem("tok_out"))
        gram_done = ctx.enter_context(sem("gram_done"))
        gram_out = ctx.enter_context(sem("gram_out"))
        stored = [ctx.enter_context(sem(f"stored{a}")) for a in range(2)]
        xc = ctx.enter_context(nc.sbuf_tensor("xc", [128, 2, CP, NP], F32))
        sq = ctx.enter_context(nc.sbuf_tensor("sq_ln", [128, 2, CP, NP], F32))
        rstd = ctx.enter_context(nc.sbuf_tensor("rstd", [128, 2, CP, NP], F32))
        xn = ctx.enter_context(nc.sbuf_tensor("xn", [128, 2, CP, NP], F32))
        tok = ctx.enter_context(nc.sbuf_tensor("tok", [96, 2, CP, 2, 192], F32))
        ps_mean = ctx.enter_context(nc.psum_tensor("ps_mean", [128, 512], F32))
        ps_var = ctx.enter_context(nc.psum_tensor("ps_var", [128, 512], F32))
        ps_qk = ctx.enter_context(nc.psum_tensor("ps_qk", [128, 2, 512], F32))
        ps_tok = ctx.enter_context(nc.psum_tensor("ps_tok", [96, 2, 512], F32))
        ps_gram = ctx.enter_context(nc.psum_tensor("ps_gram", [128, 512], F32))
        block = ctx.enter_context(nc.Block())
        W = CP * NP

        def flat(view):
            return view.rearrange("p r m -> p (r m)")

        @block.sync
        def _(sp):
            def store(c, a):
                sp.wait_ge(tok_out, CP * (c + 1))
                sp.dma_start(v_dram[bass.ds(c * 2 * CP, 2 * CP)].rearrange("b m f -> m b f"),
                             tok[:, a].rearrange("p r b f -> p (r b) f")[:, :, 128:192]).then_inc(stored[a], 16)
                sp.dma_start(top_dram[bass.ds(c * 2 * CP, 2 * CP)].rearrange("b m f -> m b f"),
                             tok[0:8, a].rearrange("p r b f -> p (r b) f")[:, :, 0:128]).then_inc(stored[a], 16)

            with sp.Fori(0, (NCH) // 2) as twice:
                c = twice * 2
                store(c, 0)
                store(c + 1, 1)
            for a in range(2):
                sp.wait_ge(stored[a], 32 * NCH // 2)

        @block.tensor
        def _(pe):
            def norm(part, c, a, n):
                if part == 0:
                    pe.wait_ge(pads, 1)
                    pe.wait_ge(centered, c)
                    pe.matmul(ps_mean[:, 0:W], k["mean_w"][:], tokens[:, span(c, CP), :], start=True, stop=True).then_inc(mean_done, 1)
                if part == 1:
                    pe.wait_ge(squared, c + 1)
                    pe.wait_ge(std_done, c)
                    pe.matmul(ps_var[:, 0:W], k["mean_w"][:], flat(sq[:, a]), start=True, stop=True).then_inc(var_done, 1)

            def products(part, c, a, n):
                if part == 0:
                    pe.wait_ge(xn_done, c + 1)
                    pe.wait_ge(qk_out, 2 * c)
                    for s in range(2):
                        pe.matmul(ps_qk[:, s, 0:W], k["w_bd"][:, s, :], flat(xn[:, a]), start=True, stop=True).then_inc(qk_done, 1)
                for r in ((0, 1), (2, 3))[part]:
                    pe.wait_ge(tok_out, CP * c + max(r - 1, 0))
                    pe.matmul(ps_tok[:, r % 2, 0:384], xn[:, a, r, :], k["w_tok"][:].rearrange("p b f -> p (b f)"),
                              start=True, stop=True).then_inc(tok_done, 1)
                if part == 1:
                    pe.wait_ge(gram_out, c)
                    pe.wait_ge(tok_out, CP * (c + 1))
                    for r in range(CP):
                        for b in range(2):
                            for j in range(4):
                                rows = tok[0:N, a, r, b, 32 * j:32 * j + 32]
                                mm = pe.matmul(ps_gram[32 * j:32 * j + 32, 64 * r + 32 * b:64 * r + 32 * b + 32], rows, rows,
                                               start=True, stop=True)
                    mm.then_inc(gram_done, 1)

            two_stages(pe, NCH, norm, products, [(0, 0), (1, 0), (0, 1), (1, 1)])

        @block.scalar
        def _(act):
            def norm(part, c, a, n):
                if part == 0:
                    act.wait_ge(centered, c + 1)
                    act.wait_ge(var_done, c)
                    act.activation(sq[:, a], xc[:, a], ACT.Square).then_inc(squared, 1)
                if part == 1:
                    act.wait_ge(var_done, c + 1)
                    act.wait_ge(xn_done, c)
                    act.activation(flat(rstd[:, a]), ps_var[:, 0:W], ACT.Sqrt, bias=k["ln_eps"][:, 0:1]).then_inc(std_done, 1)

            def products(part, c, a, n):
                if part == 0:
                    for s, out in enumerate((q_cm, k_cm)):
                        act.wait_ge(qk_done, 2 * c + s + 1)
                        act.activation(out[:, span(c, CP), :], ps_qk[:, s, 0:W].rearrange("p (r m) -> p r m", r=CP), ACT.Identity,
                                       bias=k["qkv_bias"][:, s:s + 1]).then_inc(qk_out, 1)
                if part == 1:
                    act.wait_ge(gram_done, c + 1)
                    act.activation(gram[:, span(c, 2 * CP), :], ps_gram[:, 0:256].rearrange("p (b e) -> p b e", e=32), ACT.Copy).then_inc(gram_out, 1)

            two_stages(act, NCH, norm, products, [(0, 0), (1, 0), (0, 1), (1, 1)])

        @block.vector
        def _(dve):
            def norm(part, c, a, n):
                at = span(c, CP)
                if part == 0:
                    dve.wait_ge(mean_done, c + 1)
                    dve.tensor_tensor(xc[:, a], tokens[:, at, :], ps_mean[:, 0:W].rearrange("p (r m) -> p r m", r=CP),
                                      ALU.subtract).then_inc(centered, 1)
                if part == 1:
                    dve.wait_ge(std_done, c + 1)
                    dve.reciprocal(rstd[:, a], rstd[:, a]).then_inc(rstd_done, 1)
                    dve.wait_ge(rstd_done, c + 1)
                    if not (isinstance(c, int) and c == 0):
                        dve.wait_ge(tok_done, CP * (c - 1))
                    dve.tensor_tensor(xn[:, a], xc[:, a], rstd[:, a], ALU.mult).then_inc(xn_done, 1)

            def products(part, c, a, n):
                if part == 0:
                    dve.wait_ge(stored[a], 32 * n)
                    dve.wait_ge(gram_done, c)
                for r in ((0, 1), (2, 3))[part]:
                    dve.wait_ge(tok_done, CP * c + r + 1)
                    dve.tensor_tensor(tok[:, a, r].rearrange("p b f -> p (b f)"), ps_tok[:, r % 2, 0:384],
                                      k["bias_row"][:].rearrange("p b f -> p (b f)"), ALU.add).then_inc(tok_out, 1)

            dve.tensor_copy(tokens[:, :, N:NP], tokens[:, :, N - 2:N]).then_inc(pads, 1)
            two_stages(dve, NCH, norm, products, [(0, 0), (1, 0), (1, 1), (0, 1)])


def orthogonalise(nc, gram, m_t, top_dram, k):
    sem = nc.semaphore
    KH = 2 * H
    with ExitStack() as ctx:
        top_in = ctx.enter_context(sem("top_in"))
        aug_zero = ctx.enter_context(sem("aug_zero"))
        turned = ctx.enter_context(sem("turned"))
        dve_step = ctx.enter_context(sem("dve_step"))
        roots = ctx.enter_context(sem("roots"))
        m_turned = ctx.enter_context(sem("m_turned"))
        aug = ctx.enter_context(nc.sbuf_tensor("aug", [128, KH, D, 2 * D], F32))
        top = ctx.enter_context(nc.sbuf_tensor("top", [128, D, KH, D], F32))
        rows = ctx.enter_context(nc.sbuf_tensor("head_rows", [128, KH, D, D], F32))
        prods = ctx.enter_context(nc.sbuf_tensor("prods", [128, KH, D, D], F32))
        piv = ctx.enter_context(nc.sbuf_tensor("piv", [128, KH], F32))
        inv_piv = ctx.enter_context(nc.sbuf_tensor("inv_piv", [128, KH], F32))
        fac = ctx.enter_context(nc.sbuf_tensor("fac", [128, KH, D], F32))
        diag = ctx.enter_context(nc.sbuf_tensor("diag", [128, KH, D], F32))
        rs = ctx.enter_context(nc.sbuf_tensor("rs", [128, KH, D], F32))
        newton = ctx.enter_context(nc.sbuf_tensor("newton", [128, KH, D], F32))
        sign = ctx.enter_context(nc.sbuf_tensor("sign", [128, KH, D], F32))
        wq = ctx.enter_context(nc.sbuf_tensor("wq", [128, H, D, D], F32))
        m_sum = ctx.enter_context(nc.sbuf_tensor("m_sum", [128, D, 2, H, D], F32))
        ps_turn = ctx.enter_context(nc.psum_tensor("ps_turn", [128, 8, 512], F32))
        block = ctx.enter_context(nc.Block())
        marks = {}

        @block.sync
        def _(sp):
            sp.dma_start(top[:].rearrange("p n k d -> p (n k d)"), top_dram.rearrange("b m f -> b (m f)")).then_inc(top_in, 16)

        @block.gpsimd
        def _(pool):
            pool.memset(aug[:], 0.0).then_inc(aug_zero, 1)
            pool.wait_ge(aug_zero, 1)
            for i in range(D):
                pool.memset(aug[:, :, i, D + i], 1.0).then_inc(aug_zero, 1)

        @block.scalar
        def _(act):
            act.wait_ge(dve_step, DIAG_STEP)
            act.activation(rs[:], diag[:], ACT.Sqrt).then_inc(roots, 1)

        @block.vector
        def _(dve):
            done = 0

            def step(ins):
                nonlocal done
                done += 1
                ins.then_inc(dve_step, 1)
                dve.wait_ge(dve_step, done)

            def tt(out, a, b, op):
                step(dve.tensor_tensor(out, a, b, op))

            dve.wait_ge(aug_zero, 1 + D)
            for n in range(2):
                dve.wait_ge(turned, n + 1)
                step(dve.tensor_copy(aug[:].rearrange("p k i c -> p (k i) c")[:, :, 4 * n:4 * n + 4].rearrange("p a e -> p e a"),
                                     ps_turn[:, n, :].rearrange("p (e a) -> p e a", e=4)))
            for j in range(D - 1):
                left = D - 1 - j
                step(dve.reciprocal(inv_piv[:], aug[:, :, j, j]))
                tt(fac[:, :, 0:left], aug[:, :, j + 1:D, j], inv_piv[:].unsqueeze(2).broadcast_to([128, KH, left]), ALU.mult)
                tt(prods[:, :, 0:left, :], fac[:, :, 0:left].unsqueeze(3).broadcast_to([128, KH, left, D]),
                   aug[:, :, j, j + 1:j + 1 + D].unsqueeze(2).broadcast_to([128, KH, left, D]), ALU.mult)
                tt(aug[:, :, j + 1:D, j + 1:j + 1 + D], aug[:, :, j + 1:D, j + 1:j + 1 + D], prods[:, :, 0:left, :], ALU.subtract)
            step(dve.tensor_copy(diag[:], aug[:].rearrange("p k i c -> p k (i c)")[:, :, 0:D * 2 * D:2 * D + 1]))
            assert done == DIAG_STEP
            dve.wait_ge(roots, 1)
            step(dve.reciprocal(rs[:], rs[:]))
            tt(newton[:], rs[:], rs[:], ALU.mult)
            tt(newton[:], newton[:], diag[:], ALU.mult)
            step(dve.tensor_scalar(newton[:], newton[:], -0.5, 1.5, ALU.mult, ALU.add))
            tt(rs[:], rs[:], newton[:], ALU.mult)
            dve.wait_ge(top_in, 16)
            for d in range(D):
                cols = D - d
                out = rows if d == 0 else prods
                tt(out[:, :, :, 0:cols] if d else out[:], top[:, :, :, d].rearrange("p n k -> p k n").unsqueeze(3).broadcast_to([128, KH, D, cols]),
                   aug[:, :, d:D, D + d].unsqueeze(2).broadcast_to([128, KH, D, cols]), ALU.mult)
                if d:
                    tt(rows[:, :, :, d:D], rows[:, :, :, d:D], prods[:, :, :, 0:cols], ALU.add)
            tt(rows[:], rows[:], rs[:].unsqueeze(2).broadcast_to([128, KH, D, D]), ALU.mult)
            for j in range(D):
                left = D - 1 - j
                step(dve.tensor_scalar(sign[:, :, j], rows[:, :, j, j], 0.0, -2.0, ALU.is_ge, ALU.mult))
                step(dve.tensor_scalar(sign[:, :, j], sign[:, :, j], 1.0, None, ALU.add))
                if not left:
                    break
                tt(piv[:], rows[:, :, j, j], sign[:, :, j], ALU.subtract)
                step(dve.reciprocal(inv_piv[:], piv[:]))
                tt(fac[:, :, 0:left], rows[:, :, j + 1:D, j], inv_piv[:].unsqueeze(2).broadcast_to([128, KH, left]), ALU.mult)
                tt(prods[:, :, 0:left, 0:left], fac[:, :, 0:left].unsqueeze(3).broadcast_to([128, KH, left, left]),
                   rows[:, :, j, j + 1:D].unsqueeze(2).broadcast_to([128, KH, left, left]), ALU.mult)
                tt(rows[:, :, j + 1:D, j + 1:D], rows[:, :, j + 1:D, j + 1:D], prods[:, :, 0:left, 0:left], ALU.subtract)
            tt(sign[:], sign[:], rs[:], ALU.mult)
            tt(sign[:, 0:H, :], sign[:, 0:H, :], sign[:, H:KH, :], ALU.mult)
            tt(wq[:], aug[:, 0:H, :, D:2 * D], sign[:, 0:H, :].unsqueeze(3).broadcast_to([128, H, D, D]), ALU.mult)
            m_view = m_sum[:, :, 0].rearrange("p d h e -> p h d e")
            for j in range(D - 1, -1, -1):
                n = j + 1
                out = m_view if j == D - 1 else prods[:, 0:H, 0:n, 0:n]
                tt(out, wq[:, :, j, 0:n].unsqueeze(3).broadcast_to([128, H, n, n]),
                   aug[:, H:KH, j, D:D + n].unsqueeze(2).broadcast_to([128, H, n, n]), ALU.mult)
                if j < D - 1:
                    tt(m_view[:, :, 0:n, 0:n], m_view[:, :, 0:n, 0:n], prods[:, 0:H, 0:n, 0:n], ALU.add)
            step(dve.tensor_copy(m_sum[:, :, 1].rearrange("p d h e -> p d (h e)"), m_sum[:, :, 0].rearrange("p d h e -> p d (h e)")))
            marks["m"] = done
            for n in range(2):
                dve.wait_ge(m_turned, n + 1)
                for b in range(2):
                    q = slice(64 * b, 64 * b + 64)
                    step(dve.tensor_copy(m_t[q, :, 4 * n:4 * n + 4].rearrange("p i d -> p d i"),
                                         ps_turn[q, 2 + n, :].rearrange("p (d i b) -> p d i b", d=4, b=2)[:, :, :, b]))

        @block.tensor
        def _(pe):
            for e in range(D):
                for g in range(4):
                    mm = pe.matmul(ps_turn[:, e // 4, 128 * (e % 4):128 * (e % 4) + 128], gram[:, :, 8 * g + e], k["ident_g"][:, g, :],
                                   start=(g == 0), stop=(g == 3))
                if e % 4 == 3:
                    mm.then_inc(turned, 1)
            pe.wait_ge(dve_step, marks["m"])
            for d in range(D):
                mm = pe.transpose(ps_turn[:, 2 + d // 4, 128 * (d % 4):128 * (d % 4) + 128],
                                  m_sum[:, d].rearrange("p b h e -> p (b h e)"), k["ident"][:])
                if d % 4 == 3:
                    mm.then_inc(m_turned, 1)


DIAG_STEP = 2 + 4 * (D - 1) + 1


def attend(nc, q_cm, k_cm, m_t, o_cm, v_dram, k):
    sem = nc.semaphore
    N2 = 2 * N
    with ExitStack() as ctx:
        names = ("q_zero q_ready m_ready keys_ready turned_ready v_ready kt_done kt_out dots_done squared mixed keys_used "
                 "max_done max_turned max_ready max_spread max_out sub_done exp_done sum_done av_done inv_done out_done blk_zero r_done")
        s = {n: ctx.enter_context(sem(n)) for n in names.split()}
        v_in = [ctx.enter_context(sem(f"v_in{a}")) for a in range(2)]

        def sb(name, shape):
            return ctx.enter_context(nc.sbuf_tensor(name, shape, F32))

        m_blk = sb("m_blk", [128, 2, 16, D])
        k_blk = sb("k_blk", [128, 2, NTAU, 2, H, 8])
        k_mix = sb("k_mix", [128, 2, NT, 2, H, 8])
        v_rep = sb("v_rep", [128, 2, 2, NT * C])
        v_blk = sb("v_blk", [128, 2, 2, NT, C])
        k_turn = sb("k_turn", [128, 2, NP])
        q_z = sb("q_z", [128, 2, N2])
        sq = sb("sq", [128, 6, 2 * N2])
        top = sb("row_max", [128, N2])
        top16 = sb("row_max16", [N, 2, 2, H])
        top_e = sb("row_max_e", [N, 2, H, 8])
        shift = sb("shift", [128, N2])
        prob = sb("prob", [128, NT, N2])
        sums = sb("sums", [128, 2, N2])
        inv = sb("inv", [128, N])
        ps_dot = ctx.enter_context(nc.psum_tensor("ps_dot", [128, 2, 512], F32))
        ps_a = ctx.enter_context(nc.psum_tensor("ps_a", [128, 3, 512], F32))
        ps_x = ctx.enter_context(nc.psum_tensor("ps_x", [128, 512], F32))
        ps_b = ctx.enter_context(nc.psum_tensor("ps_b", [128, 512], F32))
        ps_o = ctx.enter_context(nc.psum_tensor("ps_o", [128, 512], F32))
        block = ctx.enter_context(nc.Block())

        def steps(eng, step):
            step(0, 0, False, True)
            with eng.Fori(0, (PAIRS - 2) // 2) as twice:
                c = twice * 2
                step(c + 1, 1, True, True)
                step(c + 2, 0, True, True)
            step(PAIRS - 1, 1, True, False)

        @block.sync
        def _(sp):
            def load(i, a):
                if not isinstance(i, int):
                    sp.wait_ge(s["v_ready"], i - 1)
                for b in range(2):
                    src = v_dram[span(2 * i + b, 1)].rearrange("b (mj mi t) f -> mi mj (b t f)", mi=2, t=NT)
                    for mi in range(2):
                        sp.dma_start(v_rep[64 * mi:64 * mi + 64, a, b, :], src[mi].unsqueeze(0).broadcast_to([8, 8, NT * C])).then_inc(v_in[a], 16)

            load(0, 0)
            load(1, 1)
            with sp.Fori(1, (PAIRS) // 2) as twice:
                i = twice * 2
                load(i, 0)
                load(i + 1, 1)

        @block.gpsimd
        def _(pool):
            def build(i, a, n):
                pool.tensor_tensor(m_blk[:, a], m_t[:, span(i, 1), :].broadcast_to([128, 16, D]),
                                   k["mask16"][:].unsqueeze(2).broadcast_to([128, 16, D]), ALU.mult).then_inc(s["m_ready"], 1)
                if not (isinstance(i, int) and i < 2):
                    pool.wait_ge(s["keys_used"], i - 1)
                key = k_cm[:, span(i, 1), :].rearrange("p i (mj tau) -> p (i tau) mj", tau=NTAU)
                heads = k["hmask"][:].unsqueeze(1).unsqueeze(3)

                def blocked(kind, view):
                    return pool.tensor_tensor(k_blk[:, a, :, kind], view.unsqueeze(2).broadcast_to([128, NTAU, H, 8]),
                                              heads.broadcast_to([128, NTAU, H, 8]), ALU.mult)

                blocked(0, key).then_inc(s["keys_ready"], 1)
                for mi in range(2):
                    pool.tensor_tensor(k_mix[:, a, :, mi], key[:, NT * mi:NT * mi + NT].unsqueeze(2).broadcast_to([128, NT, H, 8]),
                                       k["conv1"].unsqueeze(1).unsqueeze(3).broadcast_to([128, NT, H, 8]), ALU.mult).then_inc(s["keys_ready"], 1)
                pool.wait_ge(s["kt_out"], i + 1)
                blocked(1, k_turn[:, a].rearrange("p (mj tau) -> p tau mj", tau=NTAU)).then_inc(s["turned_ready"], 1)
                pool.wait_ge(v_in[a], 64 * (n + 1))
                if not (isinstance(i, int) and i < 2):
                    pool.wait_ge(s["av_done"], i - 1)
                for b in range(2):
                    mm = pool.tensor_tensor(v_blk[:, a, b].rearrange("p t (o d) -> p (t o) d", o=H),
                                            v_rep[:, a, b].rearrange("p (t o d) -> p (t o) d", o=H, t=NT),
                                            k["vmask"][:].rearrange("p t o -> p (t o)").unsqueeze(2).broadcast_to([128, NT * H, D]), ALU.mult)
                mm.then_inc(s["v_ready"], 1)

            build(0, 0, 0)
            build(1, 1, 0)
            with pool.Fori(1, (PAIRS) // 2) as twice:
                i = twice * 2
                build(i, 0, twice)
                build(i + 1, 1, twice)

        @block.tensor
        def _(pe):
            def turn_keys(i, a):
                pe.wait_ge(s["m_ready"], i + 1)
                pe.wait_ge(s["kt_out"], i)
                pe.matmul(ps_x[:, 256:256 + NP], m_blk[:, a].rearrange("p q d -> p (q d)"), k_cm[:, span(i, 1), :],
                          start=True, stop=True).then_inc(s["kt_done"], 1)

            def soft(prev, a, part):
                if part == 0:
                    pe.wait_ge(s["max_done"], prev + 1)
                    for b in range(2):
                        mm = pe.transpose(ps_x[0:N, 128 * b:128 * b + 128], top[:, N * b:N * b + N], k["ident"][:])
                    mm.then_inc(s["max_turned"], 1)
                if part == 1:
                    pe.wait_ge(s["max_ready"], prev + 1)
                    for mi in range(2):
                        for b in range(2):
                            mm = pe.matmul(ps_b[64 * mi:64 * mi + 64, N * b:N * b + N], top_e[:, b].rearrange("p o m -> p (o m)"),
                                           k["ident"][0:N, 0:N], start=True, stop=True)
                    mm.then_inc(s["max_spread"], 1)
                if part == 2:
                    pe.wait_ge(s["exp_done"], prev + 1)
                    pe.wait_ge(s["v_ready"], prev + 1)
                    pe.wait_ge(s["out_done"], prev)
                    for t in range(NT):
                        for b in range(2):
                            pe.matmul(ps_o[64 * b:64 * b + 64, 0:N], v_blk[:, a, b, t, :], prob[:, t, N * b:N * b + N],
                                      start=(t == 0), stop=(t == NT - 1))
                    pe.wait_ge(s["sum_done"], prev + 1)
                    for n in range(2):
                        for b in range(2):
                            mm = pe.matmul(ps_o[64 * b:64 * b + 64, NP:NP + N], k["den_w"][:, n, :], sums[:, n, N * b:N * b + N],
                                           start=(n == 0), stop=(n == 1))
                    mm.then_inc(s["av_done"], 1)

            def step(i, a, has_prev, has_next):
                prev = i - 1
                pe.wait_ge(s["q_ready"], i + 1)
                pe.wait_ge(s["keys_ready"], 3 * (i + 1))
                pe.wait_ge(s["turned_ready"], i + 1)
                for g in range(6):
                    j, mi = divmod(g, 2)
                    if has_prev or g >= 2:
                        pe.wait_ge(s["squared"], 6 * i + g - 1)
                    for t in (2 * j, 2 * j + 1):
                        mm = pe.matmul(ps_dot[:, g % 2, N2 * (t % 2):N2 * (t % 2) + N2],
                                       k_blk[:, a, mi * NT + t].rearrange("p k h m -> p (k h m)"), q_z[:, a, :], start=True, stop=True)
                    mm.then_inc(s["dots_done"], 1)
                    if has_prev and g == 0:
                        soft(prev, 1 - a, 0)
                    if has_prev and g == 2:
                        soft(prev, 1 - a, 1)
                    if has_next and g == 3:
                        turn_keys(i + 1, 1 - a)
                if has_prev:
                    pe.wait_ge(s["sub_done"], prev + 1)
                for j in range(3):
                    for t in (2 * j, 2 * j + 1):
                        mm = pe.matmul(ps_a[:, j, N2 * (t % 2):N2 * (t % 2) + N2], k_mix[:, a, t].rearrange("p q o m -> p (q o m)"),
                                       q_z[:, a, :], start=(t % 2 == 0), stop=False, skip_group_check=True)
                    if j == 2:
                        mm.then_inc(s["keys_used"], 1)
                    for mi in range(2):
                        pe.wait_ge(s["squared"], 6 * i + 2 * j + mi + 1)
                        mm = pe.matmul(ps_a[64 * mi:64 * mi + 64, j, 0:2 * N2], k["mix_w"][:], sq[:, 2 * j + mi, :],
                                       start=False, stop=True, skip_group_check=True)
                mm.then_inc(s["mixed"], 1)
                if has_prev:
                    soft(prev, 1 - a, 2)

            turn_keys(0, 0)
            steps(pe, step)
            soft(PAIRS - 1, 1, 0)
            soft(PAIRS - 1, 1, 1)
            soft(PAIRS - 1, 1, 2)

        @block.scalar
        def _(act):
            def turned_out(i, a):
                act.wait_ge(s["kt_done"], i + 1)
                if not (isinstance(i, int) and i < 2):
                    act.wait_ge(s["turned_ready"], i - 1)
                act.activation(k_turn[:, a, :], ps_x[:, 256:256 + NP], ACT.Copy).then_inc(s["kt_out"], 1)

            def shift_out(prev):
                act.wait_ge(s["max_spread"], prev + 1)
                act.wait_ge(s["sub_done"], prev)
                act.activation(shift[:], ps_b[:, 0:N2], ACT.Identity, bias=k["conv_const"]).then_inc(s["max_out"], 1)

            def exps(prev):
                act.wait_ge(s["sub_done"], prev + 1)
                act.activation(prob[:], prob[:], ACT.Exp, bias=k["conv_const"]).then_inc(s["exp_done"], 1)

            def step(i, a, has_prev, has_next):
                for g in range(6):
                    if has_prev and g == 0:
                        act.wait_ge(s["mixed"], i)
                    act.wait_ge(s["dots_done"], 6 * i + g + 1)
                    act.activation(sq[:, g, :], ps_dot[:, g % 2, 0:2 * N2], ACT.Square).then_inc(s["squared"], 1)
                    if has_prev and g == 2:
                        shift_out(i - 1)
                    if has_next and g == 3:
                        turned_out(i + 1, 1 - a)
                if has_prev:
                    exps(i - 1)

            turned_out(0, 0)
            steps(act, step)
            shift_out(PAIRS - 1)
            exps(PAIRS - 1)

        @block.vector
        def _(dve):
            def queries(i, a):
                if not (isinstance(i, int) and i < 2):
                    dve.wait_ge(s["keys_used"], i - 1)
                for b in range(2):
                    q = slice(64 * b, 64 * b + 64)
                    cp = dve.tensor_copy(q_z[q, a, N * b:N * b + N], q_cm[q, span(i, 1), 0:N])
                cp.then_inc(s["q_ready"], 1)

            def maxima(prev):
                dve.wait_ge(s["mixed"], prev + 1)
                dve.wait_ge(s["max_turned"], prev)
                dve.tensor_reduce(top[:], ps_a[:, :, 0:2 * N2].rearrange("p j (t n) -> p n j t", t=2), AX.XY, ALU.max).then_inc(s["max_done"], 1)
                dve.wait_ge(s["max_turned"], prev + 1)
                dve.tensor_reduce(top16[:].rearrange("p b m o -> p (b m o)"), ps_x[0:N, 0:256].rearrange("p (q m) -> p q m", m=8),
                                  AX.X, ALU.max).then_inc(s["r_done"], 1)
                dve.wait_ge(s["r_done"], prev + 1)
                dve.wait_ge(s["max_spread"], prev)
                dve.tensor_tensor(top_e[:], top16[:, :, 0].unsqueeze(3).broadcast_to([N, 2, H, 8]),
                                  top16[:, :, 1].unsqueeze(3).broadcast_to([N, 2, H, 8]), ALU.max).then_inc(s["max_ready"], 1)

            def output(i):
                dve.wait_ge(s["av_done"], i + 1)
                dve.reciprocal(inv[:], ps_o[:, NP:NP + N]).then_inc(s["inv_done"], 1)
                dve.wait_ge(s["inv_done"], i + 1)
                dve.tensor_tensor(o_cm[:, span(i, 1), 0:N].rearrange("p i n -> p (i n)"), ps_o[:, 0:N], inv[:], ALU.mult).then_inc(s["out_done"], 1)

            def shifted(prev, first=False):
                dve.wait_ge(s["max_out"], prev + 1)
                dve.wait_ge(s["av_done"], prev)
                dve.tensor_tensor(prob[:].rearrange("p (j t) n -> p j t n", t=2), ps_a[:, :, 0:2 * N2].rearrange("p j (t n) -> p j t n", t=2),
                                  shift[:].unsqueeze(1).unsqueeze(1).broadcast_to([128, 3, 2, N2]), ALU.subtract).then_inc(s["sub_done"], 1)

            def sums_of(prev):
                dve.wait_ge(s["exp_done"], prev + 1)
                dve.tensor_reduce(sums[:, 0, :], prob[:, 0:4, :].rearrange("p t n -> p n t"), AX.X, ALU.add)
                dve.tensor_tensor(sums[:, 1, :], prob[:, 4, :], prob[:, 5, :], ALU.add).then_inc(s["sum_done"], 1)

            def step(i, a, has_prev, has_next):
                if has_prev:
                    maxima(i - 1)
                if has_next:
                    queries(i + 1, 1 - a)
                if has_prev:
                    shifted(i - 1)
                    if has_prev == "two":
                        output(i - 2)
                    sums_of(i - 1)

            dve.memset(q_z[:], 0.0).then_inc(s["q_zero"], 1)
            dve.wait_ge(s["q_zero"], 1)
            queries(0, 0)
            step(0, 0, False, True)
            step(1, 1, True, True)
            with dve.Fori(1, (PAIRS) // 2 - 1) as twice:
                i = twice * 2
                step(i, 0, "two", True)
                step(i + 1, 1, "two", True)
            step(PAIRS - 2, 0, "two", True)
            step(PAIRS - 1, 1, "two", False)
            maxima(PAIRS - 1)
            shifted(PAIRS - 1)
            output(PAIRS - 2)
            sums_of(PAIRS - 1)
            output(PAIRS - 1)


def feed_forward(nc, tokens, o_cm, out, k):
    sem = nc.semaphore
    with ExitStack() as ctx:
        names = ("proj_done h1_done mean_done centered squared var_done std_done rstd_done xn_done hid_done hid_out sel_done "
                 "lay_done lay_out out_done row_out")
        s = {n: ctx.enter_context(sem("f_" + n)) for n in names.split()}
        stored = [ctx.enter_context(sem(f"out_stored{a}")) for a in range(2)]

        def sb(name, shape):
            return ctx.enter_context(nc.sbuf_tensor(name, shape, F32))

        h1 = sb("h1", [128, 2, CP, N])
        xc = sb("f_xc", [128, 2, CP, N])
        sq = sb("f_sq", [128, 2, CP, N])
        rstd = sb("f_rstd", [128, 2, CP, N])
        xn = sb("f_xn", [128, 2, CP, N])
        hid = sb("hid", [128, 3, CP, 2, N])
        w_sel = sb("w_sel", [128, 2, CP, LAYERS, HID + 1])
        rows = sb("rows", [N, 2, CP, 2 * C])
        ps = ctx.enter_context(nc.psum_tensor("ps_f", [128, 8, 512], F32))
        block = ctx.enter_context(nc.Block())
        W = CP * N

        def flat(view):
            return view.rearrange("p r m -> p (r m)")

        @block.sync
        def _(sp):
            def store(c, a):
                sp.wait_ge(s["row_out"], c + 1)
                sp.dma_start(out[span(c, 2 * CP)].rearrange("b n f -> n b f"),
                             rows[:, a].rearrange("n r (b f) -> n (r b) f", b=2)).then_inc(stored[a], 16)

            with sp.Fori(0, (NCH) // 2) as twice:
                c = twice * 2
                store(c, 0)
                store(c + 1, 1)
            for a in range(2):
                sp.wait_ge(stored[a], 16 * NCH // 2)

        @block.gpsimd
        def _(pool):
            def select(c, a):
                if not (isinstance(c, int) and c < 2):
                    pool.wait_ge(s["lay_out"], 2 * CP * (c - 1))
                for r in range(CP):
                    e = pool.value_load(k["route"][0:1, span(c * CP + r, 1)], min_val=0, max_val=EXP)
                    pool.tensor_copy(w_sel[:, a, r].rearrange("p l f -> p (l f)"),
                                     k["ffn_w"][:, bass.ds(e, 1)].rearrange("p e l f -> p (e l f)")).then_inc(s["sel_done"], 1)

            select(0, 0)
            select(1, 1)
            with pool.Fori(1, (NCH) // 2) as twice:
                c = twice * 2
                select(c, 0)
                select(c + 1, 1)

        @block.tensor
        def _(pe):
            def norm(part, c, a, n):
                if part == 0:
                    pe.wait_ge(s["h1_done"], c)
                    pe.matmul(ps[:, 0, 0:W], k["w_bd"][:, 3, :], o_cm[:, span(c, CP), 0:N], start=True, stop=True).then_inc(s["proj_done"], 1)
                if part == 1:
                    pe.wait_ge(s["h1_done"], c + 1)
                    pe.wait_ge(s["centered"], c)
                    pe.matmul(ps[:, 1, 0:W], k["mean_w"][:], flat(h1[:, a]), start=True, stop=True).then_inc(s["mean_done"], 1)
                if part == 2:
                    pe.wait_ge(s["squared"], c + 1)
                    pe.wait_ge(s["std_done"], c)
                    pe.matmul(ps[:, 2, 0:W], k["mean_w"][:], flat(sq[:, a]), start=True, stop=True).then_inc(s["var_done"], 1)

            def layer(l, c, a, rs):
                for r in rs:
                    u = l * CP + r
                    if l == 0:
                        pe.wait_ge(s["sel_done"], CP * c + r + 1)
                    else:
                        pe.wait_ge(s["lay_out"], 2 * CP * c + r + 1)
                    pe.wait_ge(s["lay_out"], 2 * CP * c + max(u - 1, 0))
                    pe.matmul(ps[:, 4 + u % 2, 0:2 * N], w_sel[:, a, r, l, 0:HID], hid[:, l, r].rearrange("p b n -> p (b n)"),
                              start=True, stop=True).then_inc(s["lay_done"], 1)

            def layers(part, c, a, n):
                if part == 0:
                    pe.wait_ge(s["xn_done"], c + 1)
                    pe.wait_ge(s["hid_out"], 2 * c)
                    for b in range(2):
                        pe.matmul(ps[:, (3, 7)[b], 0:W], k["wi_bd"][:, b, :], flat(xn[:, a]), start=True, stop=True).then_inc(s["hid_done"], 1)
                if part == 1:
                    pe.wait_ge(s["hid_out"], 2 * c + 2)
                    layer(0, c, a, (0, 1))
                if part == 2:
                    layer(0, c, a, (2, 3))
                    layer(1, c, a, range(CP))
                    pe.wait_ge(s["row_out"], c)
                    for r in range(CP):
                        pe.wait_ge(s["lay_out"], 2 * CP * c + CP + r + 1)
                        o = ps[0:N, 6, 2 * C * r:2 * C * r + 2 * C]
                        pe.matmul(o, h1[:, a, r, :], k["ident"][:], start=True, stop=False, skip_group_check=True)
                        for b in range(2):
                            mm = pe.matmul(o[:, C * b:C * b + C], hid[:, 2, r, b, :], k["wo_t"][:], start=False, stop=True, skip_group_check=True)
                    mm.then_inc(s["out_done"], 1)

            two_stages(pe, NCH, norm, layers, [(0, 0), (1, 0), (0, 1), (1, 1), (0, 2), (1, 2)])

        @block.scalar
        def _(act):
            def norm(part, c, a, n):
                if part == 1:
                    act.wait_ge(s["centered"], c + 1)
                    act.wait_ge(s["var_done"], c)
                    act.activation(sq[:, a], xc[:, a], ACT.Square).then_inc(s["squared"], 1)
                if part == 2:
                    act.wait_ge(s["var_done"], c + 1)
                    act.wait_ge(s["xn_done"], c)
                    act.activation(flat(rstd[:, a]), ps[:, 2, 0:W], ACT.Sqrt, bias=k["ln_eps"][:, 0:1]).then_inc(s["std_done"], 1)

            def layers(part, c, a, n):
                if part == 0:
                    act.wait_ge(s["lay_done"], 2 * CP * c)
                    for b in range(2):
                        act.wait_ge(s["hid_done"], 2 * c + b + 1)
                        act.activation(hid[:, 0, :, b, :], ps[:, (3, 7)[b], 0:W].rearrange("p (r n) -> p r n", r=CP), ACT.Relu,
                                       bias=k["ffn_bias"][:, 34:35]).then_inc(s["hid_out"], 1)
                    return
                act.wait_ge(s["out_done"], c)
                for u in ((0, 1), range(2, 2 * CP))[part - 1]:
                    l, r = divmod(u, CP)
                    act.wait_ge(s["lay_done"], 2 * CP * c + u + 1)
                    act.activation(hid[:, l + 1, r].rearrange("p b n -> p (b n)"), ps[:, 4 + u % 2, 0:2 * N], ACT.Relu,
                                   bias=w_sel[:, a, r, l, HID:HID + 1]).then_inc(s["lay_out"], 1)

            two_stages(act, NCH, norm, layers, [(1, 0), (0, 1), (1, 1), (0, 2), (1, 2)])

        @block.vector
        def _(dve):
            def norm(part, c, a, n):
                if part == 0:
                    dve.wait_ge(s["proj_done"], c + 1)
                    if not (isinstance(c, int) and c < 2):
                        dve.wait_ge(s["out_done"], c - 1)
                    dve.scalar_tensor_tensor(out=h1[:, a], in0=ps[:, 0, 0:W].rearrange("p (r n) -> p r n", r=CP), scalar=k["proj_bias"],
                                             in1=tokens[:, span(c, CP), 0:N], op0=ALU.add, op1=ALU.add).then_inc(s["h1_done"], 1)
                    dve.wait_ge(s["mean_done"], c + 1)
                    dve.wait_ge(s["h1_done"], c + 1)
                    dve.tensor_tensor(flat(xc[:, a]), flat(h1[:, a]), ps[:, 1, 0:W], ALU.subtract).then_inc(s["centered"], 1)
                if part == 1:
                    dve.wait_ge(s["std_done"], c + 1)
                    dve.reciprocal(rstd[:, a], rstd[:, a]).then_inc(s["rstd_done"], 1)
                    dve.wait_ge(s["rstd_done"], c + 1)
                    if not (isinstance(c, int) and c < 2):
                        dve.wait_ge(s["hid_done"], 2 * (c - 1))
                    dve.tensor_tensor(xn[:, a], xc[:, a], rstd[:, a], ALU.mult).then_inc(s["xn_done"], 1)

            def layers(part, c, a, n):
                dve.wait_ge(stored[a], 16 * n)
                dve.wait_ge(s["out_done"], c + 1)
                dve.tensor_tensor(rows[:, a], ps[0:N, 6, :].rearrange("p (r f) -> p r f", r=CP),
                                  k["bo_row"][:].rearrange("p b f -> p (b f)").unsqueeze(1).broadcast_to([N, CP, 2 * C]),
                                  ALU.add).then_inc(s["row_out"], 1)

            two_stages(dve, NCH, norm, layers, [(0, 0), (0, 1), (1, 0)])


def audio_layer(nc, p, out, debug=None):
    with ExitStack() as ctx:
        def sb(name, shape, dt=F32):
            return ctx.enter_context(nc.sbuf_tensor(name, shape, dt))

        cols = sb("cols", [128, 56])
        k = {
            "ident": sb("ident", [128, 128]), "ident_g": sb("ident_g", [128, 4, 128]),
            "score_w": sb("score_w", [128, GP, 32]), "pair_sel": sb("pair_sel", [96, GP, 128], BF16),
            "mean_w": sb("mean_w", [128, 128]), "w_bd": sb("w_bd", [128, 4, 128]), "w_tok": sb("w_tok", [128, 2, 192]),
            "wi_bd": sb("wi_bd", [128, 2, HID]), "wo_t": sb("wo_t", [128, C]), "mask16": sb("mask16", [128, 16]),
            "delta_q": sb("delta_q", [128, 16, 8]), "delta": sb("delta", [128, 8]), "hmask": sb("hmask", [128, 8]),
            "mix_w": sb("mix_w", [128, 64]), "cols": cols, "conv1": cols[:, 16:24], "conv_const": cols[:, 12:13],
            "vmask": sb("vmask", [128, NT, H]), "den_w": sb("den_w", [128, 2, 64]), "tok_bias": cols[0:32, 4:5],
            "qkv_bias": cols[:, 0:3], "proj_bias": cols[:, 3:4], "ln_eps": sb("ln_eps", [128, 1]),
            "bias_row": sb("bias_row", [96, 2, 192]), "bo_row": sb("bo_row", [N, 2, C]),
            "ffn_w": sb("ffn_w", [128, EXP + 1, LAYERS, HID + 1]), "ffn_bias": sb("ffn_bias", [128, 35]),
            "route_in": sb("route_in", [1, PAIRS], I32), "route": sb("route", [1, PAIRS], I32),
        }
        tokens = sb("tokens", [128, PAIRS, NP])
        v_dram = nc.dram_tensor("v_rows", (B, NP, C), F32).ap()
        top_dram = nc.dram_tensor("top_rows", (B, D, 2 * C), F32).ap()

        with ExitStack() as first:
            x_g = first.enter_context(nc.sbuf_tensor("x_g", [128, 2, GP, TP], F32))
            x_in = [[first.enter_context(nc.semaphore(f"x_in{a}{q}")) for q in range(GROUP_LOADS)] for a in range(2)]
            constants(nc, p, x_g, x_in, k)
            pool_windows(nc, p["x"], x_g, x_in, tokens, k)
        with nc.sbuf_tensor("q_cm", [128, PAIRS, NP], F32) as q_cm, nc.sbuf_tensor("k_cm", [128, PAIRS, NP], F32) as k_cm, \
                nc.sbuf_tensor("m_t", [128, PAIRS, D], F32) as m_t:
            with nc.sbuf_tensor("gram", [128, B, 32], F32) as gram:
                project(nc, tokens, q_cm, k_cm, gram, v_dram, top_dram, k)
                orthogonalise(nc, gram, m_t, top_dram, k)
            attend(nc, q_cm, k_cm, m_t, q_cm, v_dram, k)
            feed_forward(nc, tokens, q_cm, out, k)


def laid_out(given):
    g = {name.replace("L0_", "").replace("attn_", "").replace("ffn_", ""): np.asarray(a) for name, a in given.items()}

    def col(a):
        return np.asarray(a).reshape(-1, 1)

    def by_head(a):
        return np.tile(np.repeat(a, 8, axis=0), (2, 1))

    wide = np.repeat(np.asarray(g["conv_w"]).T[H:3 * H], 8, axis=0)
    columns = [
        np.tile(g["b_qkv"].reshape(3, C).T, (2, 1)),
        np.tile(col(g["b_proj"]), (2, 1)),
        np.repeat(col(g["tok_b"]), 128, axis=0),
        np.tile(col(g["tok_w"]), (2, 1)),
        np.repeat(col(g["scale"]), 128, axis=0),
        np.repeat(np.concatenate([col(g["riem_scale"]), col(g["grassman_scale"])]), 64, axis=0),
        by_head(col(g["bn_gamma"][0:H])), by_head(col(g["bn_var"][0:H])),
        np.repeat(col(g["bn_gamma"][H:3 * H]), 8, axis=0), np.repeat(col(g["bn_var"][H:3 * H]), 8, axis=0),
        by_head(col(g["conv_b"])),
        np.zeros((128, 3), np.float32),
        by_head(g["conv_w"].T[0:H]),
        wide,
        by_head(g["conv_w"]),
    ]
    square = np.concatenate([g["w_qkv"].reshape(3, C, C), g["w_proj"][None]]).transpose(1, 0, 2)
    rows = [np.tile(g["b_qkv"], 2), np.tile(g["bo"], 2), g["bn_gamma"], g["bn_beta"], g["bn_mean"], g["bn_var"]]
    return {
        "x": g["x"], "columns": np.concatenate(columns, axis=1), "square": np.tile(square, (2, 1, 1)),
        "rows": np.concatenate(rows).reshape(1, -1), "Wi": g["Wi"], "Wo": g["Wo"], "Wr": g["Wr"], "Ws": g["Ws"],
        "biases": np.concatenate([g["br"].reshape(-1, HID), g["bs"].reshape(-1, HID), g["bi"].reshape(1, HID)]),
        "route_id": g["route_id"].reshape(1, PAIRS),
    }


def kernel(**inputs):
    import numpy as _np
    import concourse.bacc as _bacc
    from concourse import mybir as _mybir
    from concourse.bass_utils import run_bass_kernel_spmd as _run

    nc = _bacc.Bacc("TRN2", target_bir_lowering=False, num_devices=1)
    arrays, p = {}, {}
    for name, a in laid_out(inputs).items():
        a = _np.ascontiguousarray(a)
        arrays[f"in_{name}_dram"] = a
        p[name] = nc.dram_tensor(f"in_{name}_dram", a.shape, _mybir.dt.from_np(a.dtype), kind="ExternalInput").ap()
    out = nc.dram_tensor("out_0_dram", (B, N, C), F32, kind="ExternalOutput").ap()
    audio_layer(nc, p, out)
    r = _run(nc, [arrays], core_ids=[0])
    return r.results[0]["out_0_dram"]
```

```python
from contextlib import ExitStack

import numpy as np
import concourse.bass as bass
import concourse.mybir as mybir

F32 = mybir.dt.float32
BF16 = mybir.dt.bfloat16
I32 = mybir.dt.int32
ALU = mybir.AluOpType
ACT = mybir.ActivationFunctionType
AX = mybir.AxisListType

B, C, T = 128, 64, 750
WIN = 8
N = (T + WIN - 1) // WIN
NP = 96
TP = N * WIN
H, D = 8, 8
PAIRS = B // 2
NT, NTAU = 6, 12
HID, EXP, LAYERS = 128, 16, 2
GP = 16
NG = PAIRS // GP
CP = 4
NCH = PAIRS // CP
HALF = TP // 2
LN_EPS = 1e-5
BN_EPS = 1e-5


def raw(ap, offset, pattern):
    return bass.AP(ap.tensor, offset, pattern)


def score_pair(pe, x_g, x_in, ps_score, k, a, n, turn):
    if n % 4 == 0:
        pe.wait_ge(x_in[a][n // 4], 16 * (turn + 1))
    for quarter in range(4):
        mm = pe.matmul(ps_score[32 * quarter:32 * quarter + 32, 0:TP // 4], k["score_w"][:, n, :],
                       x_g[:, a, n, quarter * (TP // 4):(quarter + 1) * (TP // 4)], start=(n == 0), stop=(n == GP - 1))
    return mm


def constants(nc, p, x_g, x_in, ps_score, k):
    sem = nc.semaphore
    with ExitStack() as ctx:
        param_in = ctx.enter_context(sem("param_in"))
        pool_step = ctx.enter_context(sem("pool_step"))
        dve_step = ctx.enter_context(sem("dve_step"))
        act_step = ctx.enter_context(sem("act_step"))
        pe_step = ctx.enter_context(sem("pe_step"))
        upper_done = ctx.enter_context(sem("upper_done"))
        ones = ctx.enter_context(nc.sbuf_tensor("ones", [128, 1], F32))
        upper = ctx.enter_context(nc.sbuf_tensor("upper", [128, 1], F32))
        row_sel = ctx.enter_context(nc.sbuf_tensor("row_sel", [128, 2, 32], F32))
        bn_rows = ctx.enter_context(nc.sbuf_tensor("bn_rows", [128, 4, 24], F32))
        dot_sum = ctx.enter_context(nc.sbuf_tensor("dot_sum", [128, 1], F32))
        w_in = ctx.enter_context(nc.sbuf_tensor("w_in", [128, 4, 64], F32))
        wi_in = ctx.enter_context(nc.sbuf_tensor("wi_in", [128, 64], F32))
        wo_in = ctx.enter_context(nc.sbuf_tensor("wo_in", [64, 128], F32))
        bias_in = ctx.enter_context(nc.sbuf_tensor("bias_in", [35, 128], F32))
        cols = k["cols"]
        tokw, conv2, conv_rows = cols[:, 5:6], cols[:, 24:32], cols[:, 32:56]
        bn_col = cols[:, 8:12].rearrange("p (n v) -> p n v", n=2)
        route_f = ctx.enter_context(nc.sbuf_tensor("route_f", [1, 5, PAIRS], F32))
        ps_t = ctx.enter_context(nc.psum_tensor("ps_t", [128, 2, 512], F32))
        block = ctx.enter_context(nc.Block())
        LOADS = []
        marks = {}

        @block.sync
        def _(sp):
            def load(dst, src):
                sp.dma_start(dst, src).then_inc(param_in, 16)
                LOADS.append(1)

            load(cols[:], p["columns"])
            load(w_in[:], p["square"])
            load(k["bias_row"][:].rearrange("n b f -> n (b f)"), raw(p["rows"], 0, [[0, NP], [1, 2 * 3 * C]]))
            load(bn_rows[:].rearrange("p n f -> p (n f)"), raw(p["rows"], 2 * 3 * C, [[0, 128], [1, 4 * 3 * H]]))
            load(wi_in[:, :], p["Wi"])
            load(wo_in[:, :], p["Wo"])
            load(bias_in[:, :], p["biases"])
            load(k["route_in"][:, :], p["route_id"])
            sp.wait_ge(param_in, 16 * len(LOADS))

        n_loads = len(LOADS)

        @block.gpsimd
        def _(pool):
            done = 0

            def step(ins):
                nonlocal done
                done += 1
                ins.then_inc(pool_step, 1)
                pool.wait_ge(pool_step, done)

            def diagonal(view, base, pattern, mult):
                step(pool.affine_select(out=view, in_=view, compare_op=ALU.not_equal, fill=1.0, base=base,
                                        pattern=pattern, channel_multiplier=mult))

            step(pool.memset(k["ident"][:], 0.0))
            step(pool.memset(k["score_w"][:], 0.0))
            diagonal(k["ident"][:], 0, [[-1, 128]], 1)
            for b in range(2):
                diagonal(k["score_w"][64 * b:64 * b + 64], -b, [[-2, GP], [1, 32]], 0)
            marks["score_w"] = done
            step(pool.memset(row_sel[:], 0.0))
            for name in ("w_bd", "w_tok", "wi_bd", "delta_q", "mean_w"):
                step(pool.memset(k[name][:], 0.0))
                marks.setdefault("zeroed", done + 2)
            step(pool.memset(k["mask16"][:], 1.0))
            step(pool.memset(k["pair_mask"][:], 1.0))
            step(pool.memset(k["ln_eps"][:], LN_EPS))
            step(pool.memset(ones[:], 1.0))
            step(pool.memset(upper[0:64, :], 0.0))
            step(pool.memset(upper[64:128, :], 1.0))
            for b in range(2):
                q = slice(64 * b, 64 * b + 64)
                step(pool.memset(k["mean_w"][q, q], 1.0 / C))
            m = k["mask16"][:]
            step(pool.affine_select(out=m, in_=m, compare_op=ALU.is_ge, fill=0.0, base=0,
                                    pattern=[[-8, 16]], channel_multiplier=1))
            step(pool.affine_select(out=m, in_=m, compare_op=ALU.is_ge, fill=0.0, base=7,
                                    pattern=[[8, 16]], channel_multiplier=-1))
            m = k["pair_mask"][:]
            step(pool.affine_select(out=m, in_=m, compare_op=ALU.is_ge, fill=0.0, base=0,
                                    pattern=[[-2, PAIRS]], channel_multiplier=1))
            step(pool.affine_select(out=m, in_=m, compare_op=ALU.is_ge, fill=0.0, base=1,
                                    pattern=[[2, PAIRS]], channel_multiplier=-1))
            diagonal(k["delta_q"][:], 0, [[-8, 16], [-1, 8]], 1)
            for quarter in range(4):
                diagonal(row_sel[32 * quarter:32 * quarter + 32, quarter % 2, :], 0, [[-1, 32]], 1)
            marks["pool"] = done
            pool.wait_ge(upper_done, 1)
            for t in range(NT):
                step(pool.tensor_tensor(k["vmask"][:, t, :], k["hmask"][:], (ones if t < 4 else upper)[:, 0:1].broadcast_to([128, H]), ALU.mult))
            for n, t in enumerate((0, 4)):
                step(pool.tensor_tensor(k["den_w"][:, n, :].rearrange("p (o d) -> p o d", o=8),
                                        k["vmask"][:, t, :].unsqueeze(2).broadcast_to([128, 8, 8]),
                                        ones[:].unsqueeze(2).broadcast_to([128, 8, 8]), ALU.mult))

        @block.vector
        def _(dve):
            done = 0

            def step(ins):
                nonlocal done
                done += 1
                ins.then_inc(dve_step, 1)
                dve.wait_ge(dve_step, done)

            step(dve.memset(x_g[:, :, :, T:TP], 0.0))
            dve.wait_ge(param_in, 16 * n_loads)
            dve.wait_ge(pool_step, marks["score_w"])
            step(dve.tensor_scalar(k["score_w"][:], k["score_w"][:], tokw, None, ALU.mult))
            marks["x"] = done
            step(dve.tensor_scalar(bn_rows[:, 3, :], bn_rows[:, 3, :], BN_EPS, None, ALU.add))
            step(dve.tensor_scalar(bn_col[:, :, 1], bn_col[:, :, 1], BN_EPS, None, ALU.add))
            marks["bn"] = done
            dve.wait_ge(act_step, 2)
            step(dve.reciprocal(bn_rows[:, 3, :], bn_rows[:, 3, :]))
            step(dve.reciprocal(bn_col[:, :, 1], bn_col[:, :, 1]))
            step(dve.tensor_tensor(bn_rows[:, 0, :], bn_rows[:, 0, :], bn_rows[:, 3, :], ALU.mult))
            step(dve.tensor_tensor(bn_col[:, :, 0], bn_col[:, :, 0], bn_col[:, :, 1], ALU.mult))
            step(dve.tensor_tensor(bn_rows[:, 2, :], bn_rows[:, 2, :], bn_rows[:, 0, :], ALU.mult))
            step(dve.tensor_tensor(bn_rows[:, 1, :], bn_rows[:, 1, :], bn_rows[:, 2, :], ALU.subtract))
            step(dve.tensor_tensor(conv_rows, conv_rows, bn_rows[:, 1, :], ALU.mult))
            step(dve.tensor_reduce(dot_sum[:], conv_rows, AX.X, ALU.add))
            step(dve.tensor_tensor(k["conv_const"], k["conv_const"], dot_sum[:], ALU.add))
            step(dve.tensor_scalar(k["conv1"], k["conv1"], bn_col[:, 0, 0:1], cols[:, 6:7], ALU.mult, ALU.mult))
            step(dve.tensor_scalar(conv2, conv2, bn_col[:, 1, 0:1], cols[:, 7:8], ALU.mult, ALU.mult))
            dve.wait_ge(pool_step, marks["zeroed"])
            dve.wait_ge(pe_step, 1)
            for b in range(2):
                q = slice(64 * b, 64 * b + 64)
                for s in range(4):
                    step(dve.tensor_copy(k["w_bd"][q, s, q], ps_t[q, 0, s * 128 + 64 * b:s * 128 + 64 * b + 64]))
            dve.wait_ge(pe_step, 2)
            for b in range(2):
                q = slice(64 * b, 64 * b + 64)
                for s in range(3):
                    step(dve.tensor_copy(k["w_tok"][q, b, 64 * s:64 * s + 64], k["w_bd"][q, s, q]))
                step(dve.tensor_copy(k["wi_bd"][q, b, :], ps_t[q, 1, 0:128]))
            step(dve.tensor_copy(k["wo_t"][:], ps_t[:, 1, 128:192]))
            step(dve.tensor_copy(k["ffn_bias"][:, 0:35], ps_t[:, 1, 192:227]))
            for l in range(LAYERS):
                step(dve.tensor_copy(k["ffn_w"][:, EXP, l, HID:HID + 1], k["ffn_bias"][:, 32 + l:33 + l]))
                step(dve.tensor_scalar(k["ffn_w"][:, 0:EXP, l, HID], k["ffn_bias"][:, 16 * l:16 * l + 16],
                                       k["ffn_bias"][:, 32 + l:33 + l], None, ALU.add))
            step(dve.tensor_copy(route_f[:, 0, :], k["route_in"][:, :]))
            step(dve.tensor_scalar(route_f[:, 1, :], route_f[:, 0, :], 0.0, None, ALU.is_ge))
            step(dve.tensor_scalar(route_f[:, 2, :], route_f[:, 0, :], float(EXP), None, ALU.is_lt))
            step(dve.tensor_tensor(route_f[:, 1, :], route_f[:, 1, :], route_f[:, 2, :], ALU.mult))
            step(dve.tensor_scalar(route_f[:, 3, :], route_f[:, 0, :], 0.0, float(EXP), ALU.max, ALU.min))
            step(dve.tensor_scalar(route_f[:, 3, :], route_f[:, 3, :], -float(EXP), None, ALU.add))
            step(dve.tensor_tensor(route_f[:, 3, :], route_f[:, 3, :], route_f[:, 1, :], ALU.mult))
            step(dve.tensor_scalar(k["route"][:, :], route_f[:, 3, :], float(EXP), None, ALU.add))
            dve.wait_ge(pool_step, marks["pool"])
            step(dve.tensor_reduce(k["delta"][:], k["delta_q"][:].rearrange("p q m -> p m q"), AX.X, ALU.add))
            step(dve.tensor_tensor(k["hmask"][:], k["mask16"][:, 0:8], k["mask16"][:, 8:16], ALU.add))
            step(dve.tensor_tensor(upper[:], upper[:], k["delta"][:, 7:8], ALU.mult))
            step(dve.tensor_scalar(upper[:], upper[:], -1.0, 1.0, ALU.mult, ALU.add))
            dve.sem_inc(upper_done, 1)
            for b in range(2):
                step(dve.tensor_reduce(k["batch_sel"][:, 64 * b:64 * b + 1], k["ident"][:, b:128:2], AX.X, ALU.add))
                step(dve.tensor_copy(k["batch_sel"][:, 64 * b + 1:64 * b + 64], k["batch_sel"][:, 64 * b:64 * b + 1].broadcast_to([128, 63])))
            step(dve.tensor_reduce(k["mask4"][:], k["mask16"][:].rearrange("p (j g) -> p g j", g=4), AX.X, ALU.add))
            step(dve.tensor_tensor(k["mix_w"][:].rearrange("p (o m) -> p o m", o=8),
                                   conv2.unsqueeze(2).broadcast_to([128, 8, 8]),
                                   k["delta"][:].unsqueeze(1).broadcast_to([128, 8, 8]), ALU.mult))

        @block.scalar
        def _(act):
            load_quarter(act, p["x"], x_g, x_in, 0, 0, 0)
            act.wait_ge(param_in, 16 * n_loads)
            for q in range(1, 2 * GROUP_LOADS):
                load_quarter(act, p["x"], x_g, x_in, q // GROUP_LOADS, q // GROUP_LOADS, q % GROUP_LOADS)
            act.wait_ge(dve_step, marks["bn"])
            act.activation(bn_rows[:, 3, :], bn_rows[:, 3, :], ACT.Sqrt).then_inc(act_step, 1)
            act.activation(bn_col[:, :, 1], bn_col[:, :, 1], ACT.Sqrt).then_inc(act_step, 1)
            act.wait_ge(pool_step, marks["pool"])
            for half in range(2):
                act.activation(k["pair_sel"][:, half].rearrange("p n (b c) -> p (n b) c", b=2),
                               row_sel[:, half, :].unsqueeze(2).broadcast_to([128, 32, C]), ACT.Copy)

        @block.tensor
        def _(pe):
            pe.wait_ge(param_in, 16 * n_loads)
            pe.wait_ge(pool_step, marks["score_w"])
            for s in range(4):
                mm = pe.transpose(ps_t[0:64, 0, s * 128:s * 128 + 128], w_in[:, s, :], k["ident"][:])
            mm = pe.transpose(ps_t[0:64, 1, 0:128], wi_in[:, :], k["ident"][:])
            for s in range(4):
                mm = pe.matmul(ps_t[64:128, 0, s * 128:s * 128 + 128], w_in[:, s, :], k["ident"][:], start=True, stop=True)
            mm.then_inc(pe_step, 1)
            pe.matmul(ps_t[64:128, 1, 0:128], wi_in[:, :], k["ident"][:], start=True, stop=True)
            pe.transpose(ps_t[:, 1, 128:192], wo_in[:, :], k["ident"][0:64, 0:64])
            pe.transpose(ps_t[:, 1, 192:227], bias_in[0:35, :], k["ident"][0:35, 0:35]).then_inc(pe_step, 1)
            pe.wait_ge(dve_step, marks["x"])
            for n in range(GP):
                score_pair(pe, x_g, x_in, ps_score, k, 0, n, 0)


GROUP_LOADS = GP // 4
AHEAD_STEPS = 10


def load_quarter(eng, x, x_g, x_in, g, a, q):
    rows = x.rearrange("b f t -> (b f) t").rearrange("(n p) t -> p n t", p=128)
    at = g * GP + 4 * q
    eng.dma_start(x_g[:, a, 4 * q:4 * q + 4, 0:T],
                  rows[:, slice(at, at + 4) if isinstance(g, int) else bass.ds(at, 4), :]).then_inc(x_in[a][q], 16)


def pool_windows(nc, x, x_g, x_in, ps_score, tokens, k):
    sem = nc.semaphore
    HP = GP // 2
    with ExitStack() as ctx:
        names = ("lo_zero scores_done scores_out maxima shifted exps sums_done inv_done weights_done hi_done rest_done "
                 "mid_done mid_moved lo_done spread_done even_done odd_out odd_done odd_pooled")
        s = {n: ctx.enter_context(sem("p_" + n)) for n in names.split()}
        soft = ctx.enter_context(nc.sbuf_tensor("soft", [64, N // 2, WIN], F32))
        rest = ctx.enter_context(nc.sbuf_tensor("rest", [64, HALF], F32))
        mid = ctx.enter_context(nc.sbuf_tensor("mid", [64, HALF], BF16))
        stat = ctx.enter_context(nc.sbuf_tensor("stat", [64, 3, N // 2], F32))
        parts = ctx.enter_context(nc.sbuf_tensor("parts", [128, 2, 2, HALF], BF16))
        w_odd = ctx.enter_context(nc.sbuf_tensor("w_odd", [128, 2, TP], F32))
        prod = ctx.enter_context(nc.sbuf_tensor("prod", [128, 2, 2, TP], F32))
        ps_spread = ctx.enter_context(nc.psum_tensor("ps_spread", [128, 4, 512], F32))
        block = ctx.enter_context(nc.Block())
        flat = soft[:].rearrange("p w k -> p (w k)")
        AHEAD = [range(GP * n // AHEAD_STEPS, GP * (n + 1) // AHEAD_STEPS) if n < AHEAD_STEPS else range(0) for n in range(GP)]

        def halves(view):
            return view.rearrange("p (a t) -> p a t", a=2)

        @block.sync
        def _(sp):
            with sp.Fori(1, NG // 2) as n:
                for a in range(2):
                    for q in range(GROUP_LOADS):
                        for products in (s["even_done"], s["odd_done"]):
                            sp.wait_ge(products, (2 * n + a - 2) * (GP // 2) + 2 * q + 2)
                        load_quarter(sp, x, x_g, x_in, 2 * n + a, a, q)

        def groups(eng, group):
            group(0, 0, 0, True)
            with eng.Fori(0, NG // 2 - 1) as n:
                group(2 * n + 1, 1, n, True)
                group(2 * n + 2, 0, n + 1, True)
            group(NG - 1, 1, NG // 2 - 1, False)

        @block.tensor
        def _(pe):
            def score(a, n, turn):
                mm = score_pair(pe, x_g, x_in, ps_score, k, a, n, turn)
                if n == GP - 1:
                    mm.then_inc(s["scores_done"], 1)

            def group(g, a, twin, has_next):
                if has_next:
                    pe.wait_ge(s["scores_out"], g + 1)
                pe.wait_ge(s["mid_moved"], g + 1)
                pe.wait_ge(s["lo_done"], g + 1)
                for n in range(GP):
                    pe.wait_ge(s["odd_out" if n % 2 else "even_done"], g * HP + n // 2)
                    for half in range(2):
                        for part in range(2):
                            mm = pe.matmul(ps_spread[:, 2 * (n % 2) + half, 0:HALF], k["pair_sel"][:, half, n, :], parts[:, a, part, :],
                                           start=(part == 0), stop=(part == 1))
                    mm.then_inc(s["spread_done"], 1)
                    if has_next:
                        for ahead in AHEAD[n]:
                            score(1 - a, ahead, twin + a)

            pe.wait_ge(s["lo_zero"], 1)
            groups(pe, group)

        def parted(eng, i, a, part):
            if part == "hi":
                eng.wait_ge(s["weights_done"], i + 1)
                eng.activation(parts[0:64, a, 0, :], flat, ACT.Copy).then_inc(s["hi_done"], 1)
            if part == "rest":
                eng.wait_ge(s["hi_done"], i + 1)
                eng.tensor_tensor(rest[:], flat, parts[0:64, a, 0, :], ALU.subtract).then_inc(s["rest_done"], 1)
            if part == "mid":
                eng.wait_ge(s["rest_done"], i + 1)
                eng.activation(mid[:], rest[:], ACT.Copy).then_inc(s["mid_done"], 1)
                eng.wait_ge(s["mid_done"], i + 1)
                eng.activation(parts[64:128, a, 0, :], mid[:], ACT.Copy).then_inc(s["mid_moved"], 1)
            if part == "lo":
                eng.wait_ge(s["mid_done"], i + 1)
                eng.tensor_tensor(parts[0:64, a, 1, :], rest[:], mid[:], ALU.subtract).then_inc(s["lo_done"], 1)

        @block.scalar
        def _(act):
            def softmax(i, a, part):
                if part == 0:
                    if not (isinstance(i, int) and i == 0):
                        act.wait_ge(s["scores_done"], i)
                    for quarter in range(4):
                        rows = slice(32 * quarter, 32 * quarter + 32)
                        half, at = divmod(quarter, 2)
                        out = act.activation(flat[32 * half:32 * half + 32, at * (TP // 4):(at + 1) * (TP // 4)], ps_score[rows, 0:TP // 4],
                                             ACT.Identity, bias=k["tok_bias"][rows])
                    out.then_inc(s["scores_out"], 1)
                if part == 1:
                    act.wait_ge(s["shifted"], i + 1)
                    act.activation(soft[:], soft[:], ACT.Exp).then_inc(s["exps"], 1)
                if part == 2:
                    parted(act, i, a, "hi")
                if part == 3:
                    parted(act, i, a, "mid")

            def group(g, a, twin, has_next):
                for n in range(HP):
                    act.wait_ge(s["spread_done"], g * GP + 2 * n + 2)
                    if not (isinstance(g, int) and g == 0 and n < 2):
                        act.wait_ge(s["odd_done"], g * HP + n - 1)
                    act.activation(halves(w_odd[:, n % 2, :]), ps_spread[:, 2:4, 0:HALF], ACT.Copy).then_inc(s["odd_out"], 1)
                    if has_next:
                        for part in {4: (0, 1), 5: (2,), 6: (3,)}.get(n, ()):
                            softmax(g + 1, 1 - a, part)

            for part in range(4):
                softmax(0, 0, part)
            groups(act, group)

        @block.gpsimd
        def _(pool):
            def group(g, a, twin, has_next):
                for n in range(HP):
                    pool.wait_ge(s["odd_out"], g * HP + n + 1)
                    if not (isinstance(g, int) and g == 0 and n < 2):
                        pool.wait_ge(s["odd_pooled"], g * HP + n - 1)
                    pool.tensor_tensor(prod[:, 1, n % 2, :], x_g[:, a, 2 * n + 1, :], w_odd[:, n % 2, :], ALU.mult).then_inc(s["odd_done"], 1)
                    if has_next and n == 5:
                        parted(pool, g + 1, 1 - a, "rest")
                    if has_next and n == 6:
                        parted(pool, g + 1, 1 - a, "lo")

            pool.memset(parts[64:128, :, 1, :], 0.0).then_inc(s["lo_zero"], 1)
            parted(pool, 0, 0, "rest")
            parted(pool, 0, 0, "lo")
            groups(pool, group)

        @block.vector
        def _(dve):
            def softmax(i, part):
                def over(view):
                    return view.unsqueeze(2).broadcast_to([64, N // 2, WIN])

                if part == 0:
                    dve.wait_ge(s["scores_out"], i + 1)
                    dve.tensor_reduce(stat[:, 0, :], soft[:], AX.X, ALU.max).then_inc(s["maxima"], 1)
                    dve.wait_ge(s["maxima"], i + 1)
                    dve.tensor_tensor(soft[:], soft[:], over(stat[:, 0, :]), ALU.subtract).then_inc(s["shifted"], 1)
                if part == 1:
                    dve.wait_ge(s["exps"], i + 1)
                    dve.tensor_reduce(stat[:, 1, :], soft[:], AX.X, ALU.add).then_inc(s["sums_done"], 1)
                    dve.wait_ge(s["sums_done"], i + 1)
                    dve.reciprocal(stat[:, 2, :], stat[:, 1, :]).then_inc(s["inv_done"], 1)
                    dve.wait_ge(s["inv_done"], i + 1)
                    dve.tensor_tensor(soft[:], soft[:], over(stat[:, 2, :]), ALU.mult).then_inc(s["weights_done"], 1)

            def pooled(g, n, which, view):
                at = slice(g * GP + n, g * GP + n + 1) if isinstance(g, int) else bass.ds(g * GP + n, 1)
                return dve.tensor_reduce(tokens[:, at, 0:N], view.rearrange("p (w k) -> p w k", k=WIN), AX.X, ALU.add)

            def odd(g, n):
                dve.wait_ge(s["odd_done"], g * HP + n + 1)
                pooled(g, 2 * n + 1, 1, prod[:, 1, n % 2, :]).then_inc(s["odd_pooled"], 1)

            def group(g, a, twin, has_next):
                for n in range(HP):
                    dve.wait_ge(s["spread_done"], g * GP + 2 * n + 1)
                    dve.tensor_tensor(halves(prod[:, 0, n % 2, :]), halves(x_g[:, a, 2 * n, :]), ps_spread[:, 0:2, 0:HALF],
                                      ALU.mult).then_inc(s["even_done"], 1)
                    if n:
                        odd(g, n - 1)
                    dve.wait_ge(s["even_done"], g * HP + n + 1)
                    pooled(g, 2 * n, 0, prod[:, 0, n % 2, :])
                    if has_next and n in (4, 5):
                        softmax(g + 1, n - 4)
                odd(g, HP - 1)

            softmax(0, 0)
            softmax(0, 1)
            groups(dve, group)


def span(c, n):
    return slice(c * n, c * n + n) if isinstance(c, int) else bass.ds(c * n, n)


def staggered(eng, count, stages):
    last = max(lag for lag, _ in stages)

    def edge(c):
        for lag, part in stages:
            if 0 <= c - lag < count:
                part(c - lag, (c - lag) % 2)

    peeled = last + 2 + last % 2
    for c in range(peeled):
        edge(c)
    with eng.Fori(peeled // 2, count // 2) as twice:
        for parity in range(2):
            for lag, part in stages:
                part(2 * twice + parity - lag, (parity - lag) % 2)
    for c in range(count, count + last):
        edge(c)


def later(c, behind):
    return not isinstance(c, int) or c >= behind


def centre(nc, x_cm, xc, rstd_t, width, k, o_cm=None):
    sem = nc.semaphore
    tag = "c1_" if o_cm is not None else "c0_"
    with ExitStack() as ctx:
        names = "added proj_done mean_done centered squared var_done std_done rstd_done turned"
        s = {n: ctx.enter_context(sem(tag + n)) for n in names.split()}
        sq = ctx.enter_context(nc.sbuf_tensor(tag + "sq", [128, 2, CP, width], F32))
        std = ctx.enter_context(nc.sbuf_tensor(tag + "std", [width, B], F32))
        rstd = ctx.enter_context(nc.sbuf_tensor(tag + "rstd", [width, B], F32))
        ps_proj = ctx.enter_context(nc.psum_tensor(tag + "proj", [128, 2, 512], F32))
        ps_mean = ctx.enter_context(nc.psum_tensor(tag + "mean", [128, 2, 512], F32))
        ps_var = ctx.enter_context(nc.psum_tensor(tag + "var", [width, 512], F32))
        ps_turn = ctx.enter_context(nc.psum_tensor(tag + "turn", [128, 512], F32))
        block = ctx.enter_context(nc.Block())
        W = CP * width

        def part_of(t, c):
            return t[:, span(c, CP), 0:width]

        def rows(bank):
            return bank.rearrange("p (r m) -> p r m", r=CP)

        @block.tensor
        def _(pe):
            def proj(c, a):
                if later(c, 2):
                    pe.wait_ge(s["added"], c - 1)
                pe.matmul(ps_proj[:, a, 0:W], k["w_bd"][:, 3, :], part_of(o_cm, c), start=True, stop=True).then_inc(s["proj_done"], 1)

            def mean(c, a):
                pe.wait_ge(s["added"], 1 if o_cm is None else c + 1)
                if later(c, 2):
                    pe.wait_ge(s["centered"], c - 1)
                pe.matmul(ps_mean[:, a, 0:W], k["mean_w"][:], part_of(x_cm, c), start=True, stop=True).then_inc(s["mean_done"], 1)

            def variance(c, a):
                pe.wait_ge(s["squared"], c + 1)
                for r in range(CP):
                    col = (c * CP + r) * 2
                    mm = pe.matmul(ps_var[:, slice(col, col + 2) if isinstance(c, int) else bass.ds(col, 2)], sq[:, a, r, :],
                                   k["mean_w"][:, 0:128:64], start=True, stop=True)
                mm.then_inc(s["var_done"], 1)

            staggered(pe, NCH, ([(0, proj)] if o_cm is not None else []) + [(1, mean), (3, variance)])
            pe.wait_ge(s["rstd_done"], 1)
            pe.transpose(ps_turn[:, 0:width], rstd[:], k["ident"][0:width, 0:width]).then_inc(s["turned"], 1)

        @block.scalar
        def _(act):
            def square(c, a):
                act.wait_ge(s["centered"], c + 1)
                if later(c, 2):
                    act.wait_ge(s["var_done"], c - 1)
                act.activation(sq[:, a], part_of(xc, c), ACT.Square).then_inc(s["squared"], 1)

            staggered(act, NCH, [(0, square)])
            act.wait_ge(s["var_done"], NCH)
            act.activation(std[:], ps_var[:, 0:B], ACT.Sqrt, bias=k["ln_eps"][0:width, 0:1]).then_inc(s["std_done"], 1)

        @block.vector
        def _(dve):
            def add(c, a):
                dve.wait_ge(s["proj_done"], c + 1)
                dve.scalar_tensor_tensor(out=part_of(x_cm, c), in0=rows(ps_proj[:, a, 0:W]), scalar=k["proj_bias"],
                                         in1=part_of(x_cm, c), op0=ALU.add, op1=ALU.add).then_inc(s["added"], 1)

            def subtract(c, a):
                dve.wait_ge(s["mean_done"], c + 1)
                if o_cm is not None:
                    dve.wait_ge(s["added"], c + 1)
                dve.tensor_tensor(part_of(xc, c), part_of(x_cm, c), rows(ps_mean[:, a, 0:W]), ALU.subtract).then_inc(s["centered"], 1)

            if o_cm is None:
                dve.tensor_copy(x_cm[:, :, N:NP], x_cm[:, :, N - 2:N]).then_inc(s["added"], 1)
                dve.wait_ge(s["added"], 1)
            staggered(dve, NCH, ([(0, add)] if o_cm is not None else []) + [(1, subtract)])
            dve.wait_ge(s["std_done"], 1)
            dve.reciprocal(rstd[:], std[:]).then_inc(s["rstd_done"], 1)
            dve.wait_ge(s["turned"], 1)
            dve.tensor_copy(rstd_t[:, 0:width], ps_turn[:, 0:width])


def mask_rstd(pool, rstd_t, rstd_of, rstd_done, masked, width, k):
    def mask(c, a):
        if later(c, 2):
            pool.wait_ge(rstd_done, c - 1)
        pool.tensor_tensor(rstd_of[:, a], rstd_t[:, 0:width].unsqueeze(1).broadcast_to([128, CP, width]),
                           k["pair_mask"][:, span(c, CP)].unsqueeze(2).broadcast_to([128, CP, width]), ALU.mult).then_inc(masked, 1)

    staggered(pool, NCH, [(0, mask)])


def project(nc, xc, rstd_t, gram, v_dram, top_dram, k):
    sem = nc.semaphore
    with ExitStack() as ctx:
        masked = ctx.enter_context(sem("masked"))
        rstd_done = ctx.enter_context(sem("rstd_done"))
        xn_done = ctx.enter_context(sem("xn_done"))
        xn_kept = ctx.enter_context(sem("xn_kept"))
        tok_done = ctx.enter_context(sem("tok_done"))
        tok_out = ctx.enter_context(sem("tok_out"))
        gram_done = ctx.enter_context(sem("gram_done"))
        gram_out = ctx.enter_context(sem("gram_out"))
        stored = [ctx.enter_context(sem(f"stored{a}")) for a in range(2)]
        rstd_of = ctx.enter_context(nc.sbuf_tensor("rstd_of", [128, 2, CP, NP], F32))
        xn = ctx.enter_context(nc.sbuf_tensor("xn", [128, 2, CP, NP], F32))
        own = ctx.enter_context(nc.sbuf_tensor("own", [128, 2, 2 * CP, D, 4], F32))
        tok = ctx.enter_context(nc.sbuf_tensor("tok", [96, 2, CP, 2, 192], F32))
        ps_rstd = ctx.enter_context(nc.psum_tensor("ps_rstd", [128, 512], F32))
        ps_tok = ctx.enter_context(nc.psum_tensor("ps_tok", [96, CP, 512], F32))
        ps_gram = ctx.enter_context(nc.psum_tensor("ps_gram", [128, 512], F32))
        block = ctx.enter_context(nc.Block())
        W = CP * NP

        def flat(view):
            return view.rearrange("p r m -> p (r m)")

        @block.sync
        def _(sp):
            def store(c, a):
                sp.wait_ge(tok_out, CP * (c + 1))
                sp.dma_start(v_dram[bass.ds(c * 2 * CP, 2 * CP)].rearrange("b m f -> m b f"),
                             tok[:, a].rearrange("p r b f -> p (r b) f")[:, :, 128:192]).then_inc(stored[a], 16)
                sp.dma_start(top_dram[bass.ds(c * 2 * CP, 2 * CP)].rearrange("b m f -> m b f"),
                             tok[0:8, a].rearrange("p r b f -> p (r b) f")[:, :, 0:128]).then_inc(stored[a], 16)

            with sp.Fori(0, (NCH) // 2) as twice:
                c = twice * 2
                store(c, 0)
                store(c + 1, 1)
            for a in range(2):
                sp.wait_ge(stored[a], 32 * NCH // 2)

        @block.tensor
        def _(pe):
            def spread(c, a):
                pe.wait_ge(masked, c + 1)
                pe.wait_ge(xn_done, c)
                pe.matmul(ps_rstd[:, 0:W], k["batch_sel"][:], flat(rstd_of[:, a]), start=True, stop=True).then_inc(rstd_done, 1)

            def rows_of(c, a):
                pe.wait_ge(xn_done, c + 1)
                for r in range(CP):
                    if later(c, 1):
                        pe.wait_ge(tok_out, CP * (c - 1) + r + 1)
                    pe.matmul(ps_tok[:, r, 0:384], xn[:, a, r, :], k["w_tok"][:].rearrange("p b f -> p (b f)"),
                              start=True, stop=True).then_inc(tok_done, 1)

            def grams(c, a):
                pe.wait_ge(gram_out, c)
                pe.wait_ge(tok_out, CP * (c + 1))
                for r in range(CP):
                    for b in range(2):
                        for j in range(4):
                            rows = tok[0:N, a, r, b, 32 * j:32 * j + 32]
                            mm = pe.matmul(ps_gram[32 * j:32 * j + 32, 64 * r + 32 * b:64 * r + 32 * b + 32], rows, rows,
                                           start=True, stop=True)
                mm.then_inc(gram_done, 1)

            staggered(pe, NCH, [(0, spread), (1, rows_of), (2, grams)])

        @block.gpsimd
        def _(pool):
            mask_rstd(pool, rstd_t, rstd_of, rstd_done, masked, NP, k)

        @block.scalar
        def _(act):
            def keep(c, a):
                act.wait_ge(xn_done, c + 1)
                act.activation(xc[:, span(c, CP), :], xn[:, a], ACT.Copy).then_inc(xn_kept, 1)

            staggered(act, NCH, [(0, keep)])

        @block.vector
        def _(dve):
            def normed(c, a):
                dve.wait_ge(rstd_done, c + 1)
                if later(c, 2):
                    dve.wait_ge(tok_done, CP * (c - 1))
                    dve.wait_ge(xn_kept, c - 1)
                dve.tensor_tensor(xn[:, a], xc[:, span(c, CP), :], ps_rstd[:, 0:W].rearrange("p (r m) -> p r m", r=CP),
                                  ALU.mult).then_inc(xn_done, 1)

            def rows_out(c, a):
                if later(c, 2):
                    dve.wait_ge(stored[a], 16 * (c - a))
                    dve.wait_ge(gram_done, c - 1)
                for r in range(CP):
                    dve.wait_ge(tok_done, CP * c + r + 1)
                    dve.tensor_tensor(tok[:, a, r].rearrange("p b f -> p (b f)"), ps_tok[:, r, 0:384],
                                      k["bias_row"][:].rearrange("p b f -> p (b f)"), ALU.add).then_inc(tok_out, 1)

            def grams_out(c, a):
                dve.wait_ge(gram_done, c + 1)
                dve.tensor_tensor(own[:, a], ps_gram[:, 0:256].rearrange("p (b g e) -> p b e g", g=4, e=D),
                                  k["mask4"][:].unsqueeze(1).unsqueeze(1).broadcast_to([128, 2 * CP, D, 4]), ALU.mult).then_inc(gram_out, 1)
                dve.wait_ge(gram_out, c + 1)
                dve.tensor_reduce(gram[:, span(c, 2 * CP), :], own[:, a], AX.X, ALU.add)

            staggered(dve, NCH, [(0, normed), (1, rows_out), (2, grams_out)])


def orthogonalise(nc, p, gram, m_t, top_dram, xn, q_cm, k_cm, k):
    sem = nc.semaphore
    KH = 2 * H
    with ExitStack() as ctx:
        top_in = ctx.enter_context(sem("top_in"))
        aug_zero = ctx.enter_context(sem("aug_zero"))
        turned = ctx.enter_context(sem("turned"))
        top_turned = ctx.enter_context(sem("top_turned"))
        dve_step = ctx.enter_context(sem("dve_step"))
        roots = ctx.enter_context(sem("roots"))
        m_turned = ctx.enter_context(sem("m_turned"))
        experts_in = [ctx.enter_context(sem(f"experts_in{l}")) for l in range(LAYERS)]
        qk_done = ctx.enter_context(sem("qk_done"))
        qk_out = ctx.enter_context(sem("qk_out"))
        experts_done = ctx.enter_context(sem("experts_done"))
        experts_out = ctx.enter_context(sem("experts_out"))
        wr_in = ctx.enter_context(nc.sbuf_tensor("wr_in", [128, LAYERS, EXP + 1, HID], F32))
        aug = ctx.enter_context(nc.sbuf_tensor("aug", [128, KH, D, 3 * D], F32))
        top = ctx.enter_context(nc.sbuf_tensor("top", [128, D, KH, D], F32))
        rows = ctx.enter_context(nc.sbuf_tensor("head_rows", [128, KH, D, D], F32))
        prods = ctx.enter_context(nc.sbuf_tensor("prods", [128, KH, D, D], F32))
        prods_t = ctx.enter_context(nc.sbuf_tensor("prods_t", [128, KH, D - 1, D], F32))
        piv = ctx.enter_context(nc.sbuf_tensor("piv", [128, KH], F32))
        inv_piv = ctx.enter_context(nc.sbuf_tensor("inv_piv", [128, KH], F32))
        fac = ctx.enter_context(nc.sbuf_tensor("fac", [128, KH, D], F32))
        diag = ctx.enter_context(nc.sbuf_tensor("diag", [128, KH, D], F32))
        rs = ctx.enter_context(nc.sbuf_tensor("rs", [128, KH, D], F32))
        newton = ctx.enter_context(nc.sbuf_tensor("newton", [128, KH, D], F32))
        sign = ctx.enter_context(nc.sbuf_tensor("sign", [128, KH, D], F32))
        wq = ctx.enter_context(nc.sbuf_tensor("wq", [128, H, D, D], F32))
        m_sum = ctx.enter_context(nc.sbuf_tensor("m_sum", [128, D, 2, H, D], F32))
        ps_turn = ctx.enter_context(nc.psum_tensor("ps_turn", [128, 8, 512], F32))
        block = ctx.enter_context(nc.Block())
        marks = {}

        @block.sync
        def _(sp):
            sp.dma_start(top[:].rearrange("p n k d -> p (n k d)"), top_dram.rearrange("b m f -> b (m f)")).then_inc(top_in, 16)
            for l in range(LAYERS):
                sp.dma_start(wr_in[:, l, EXP, :], p["Ws"][l, 0]).then_inc(experts_in[l], 16)
                sp.dma_start(wr_in[:, l, 0:EXP, :], p["Wr"][l].rearrange("e o i -> o e i")).then_inc(experts_in[l], 16)

        @block.gpsimd
        def _(pool):
            pool.wait_ge(aug_zero, 1)
            for i in range(D):
                pool.memset(aug[:, :, i, D + i], 1.0).then_inc(aug_zero, 1)

        @block.scalar
        def _(act):
            def queries_keys(c, a):
                for s, out in enumerate((q_cm, k_cm)):
                    act.wait_ge(qk_done, 2 * c + s + 1)
                    act.activation(out[:, span(c, CP), :], ps_turn[:, 4 + 2 * a + s, 0:CP * NP].rearrange("p (r m) -> p r m", r=CP),
                                   ACT.Identity, bias=k["qkv_bias"][:, s:s + 1]).then_inc(qk_out, 1)

            act.wait_ge(top_in, 16)
            act.activation(aug[:, :, :, 2 * D:3 * D], top[:].rearrange("p n k d -> p k d n"), ACT.Copy).then_inc(top_turned, 1)
            staggered(act, NCH, [(0, queries_keys)])
            act.wait_ge(dve_step, DIAG_STEP)
            act.activation(rs[:], diag[:], ACT.Sqrt).then_inc(roots, 1)
            for n, (l, lo, hi) in enumerate(EXPERT_BANKS):
                act.wait_ge(experts_done, n + 1)
                act.activation(k["ffn_w"][:, lo:hi, l, 0:HID], ps_turn[:, 4 + n % 4, 0:HID * (hi - lo)].rearrange("p (e f) -> p e f", f=HID),
                               ACT.Copy).then_inc(experts_out, 1)

        @block.vector
        def _(dve):
            done = 0

            def count(ins):
                nonlocal done
                done += 1
                ins.then_inc(dve_step, 1)

            def step(ins):
                count(ins)
                dve.wait_ge(dve_step, done)

            def tt(out, a, b, op):
                step(dve.tensor_tensor(out, a, b, op))

            dve.memset(aug[:, :, :, D:2 * D], 0.0).then_inc(aug_zero, 1)
            dve.wait_ge(aug_zero, 1 + D)
            for n in range(2):
                dve.wait_ge(turned, n + 1)
                step(dve.tensor_copy(aug[:].rearrange("p k i c -> p (k i) c")[:, :, 4 * n:4 * n + 4].rearrange("p a e -> p e a"),
                                     ps_turn[:, n, :].rearrange("p (e a) -> p e a", e=4)))
            dve.wait_ge(top_turned, 1)
            for j in range(D - 1):
                left = D - 1 - j
                step(dve.reciprocal(inv_piv[:], aug[:, :, j, j]))
                tt(fac[:, :, 0:left], aug[:, :, j + 1:D, j], inv_piv[:].unsqueeze(2).broadcast_to([128, KH, left]), ALU.mult)
                places = ((slice(j + 1, j + 1 + D), prods), (slice(2 * D, 3 * D), prods_t))
                for place, product in places:
                    count(dve.tensor_tensor(product[:, :, 0:left, :], fac[:, :, 0:left].unsqueeze(3).broadcast_to([128, KH, left, D]),
                                            aug[:, :, j, place].unsqueeze(2).broadcast_to([128, KH, left, D]), ALU.mult))
                for place, product in places:
                    dve.wait_ge(dve_step, done - 1)
                    count(dve.tensor_tensor(aug[:, :, j + 1:D, place], aug[:, :, j + 1:D, place], product[:, :, 0:left, :], ALU.subtract))
                dve.wait_ge(dve_step, done - 1)
            dve.wait_ge(dve_step, done)
            step(dve.tensor_copy(diag[:], aug[:].rearrange("p k i c -> p k (i c)")[:, :, 0:D * 3 * D:3 * D + 1]))
            assert done == DIAG_STEP
            dve.wait_ge(roots, 1)
            step(dve.reciprocal(rs[:], rs[:]))
            tt(newton[:], rs[:], rs[:], ALU.mult)
            tt(newton[:], newton[:], diag[:], ALU.mult)
            step(dve.tensor_scalar(newton[:], newton[:], -0.5, 1.5, ALU.mult, ALU.add))
            tt(rs[:], rs[:], newton[:], ALU.mult)
            tt(rows[:], aug[:, :, :, 2 * D:3 * D].rearrange("p k d n -> p k n d"), rs[:].unsqueeze(2).broadcast_to([128, KH, D, D]), ALU.mult)
            for j in range(D):
                left = D - 1 - j
                step(dve.tensor_scalar(sign[:, :, j], rows[:, :, j, j], 0.0, -2.0, ALU.is_ge, ALU.mult))
                if not left:
                    break
                step(dve.scalar_tensor_tensor(out=piv[:], in0=rows[:, :, j, j], scalar=-1.0, in1=sign[:, :, j], op0=ALU.add, op1=ALU.subtract))
                step(dve.reciprocal(inv_piv[:], piv[:]))
                tt(fac[:, :, 0:left], rows[:, :, j + 1:D, j], inv_piv[:].unsqueeze(2).broadcast_to([128, KH, left]), ALU.mult)
                tt(prods[:, :, 0:left, 0:left], fac[:, :, 0:left].unsqueeze(3).broadcast_to([128, KH, left, left]),
                   rows[:, :, j, j + 1:D].unsqueeze(2).broadcast_to([128, KH, left, left]), ALU.mult)
                tt(rows[:, :, j + 1:D, j + 1:D], rows[:, :, j + 1:D, j + 1:D], prods[:, :, 0:left, 0:left], ALU.subtract)
            step(dve.tensor_scalar(sign[:], sign[:], 1.0, None, ALU.add))
            tt(sign[:], sign[:], rs[:], ALU.mult)
            tt(sign[:, 0:H, :], sign[:, 0:H, :], sign[:, H:KH, :], ALU.mult)
            tt(wq[:], aug[:, 0:H, :, D:2 * D], sign[:, 0:H, :].unsqueeze(3).broadcast_to([128, H, D, D]), ALU.mult)
            m_view = m_sum[:, :, 0].rearrange("p d h e -> p h d e")
            for j in range(D - 1, -1, -1):
                n = j + 1
                out = m_view if j == D - 1 else prods[:, 0:H, 0:n, 0:n]
                tt(out, wq[:, :, j, 0:n].unsqueeze(3).broadcast_to([128, H, n, n]),
                   aug[:, H:KH, j, D:D + n].unsqueeze(2).broadcast_to([128, H, n, n]), ALU.mult)
                if j < D - 1:
                    tt(m_view[:, :, 0:n, 0:n], m_view[:, :, 0:n, 0:n], prods[:, 0:H, 0:n, 0:n], ALU.add)
            step(dve.tensor_copy(m_sum[:, :, 1].rearrange("p d h e -> p d (h e)"), m_sum[:, :, 0].rearrange("p d h e -> p d (h e)")))
            marks["m"] = done
            for n in range(2):
                dve.wait_ge(m_turned, n + 1)
                for b in range(2):
                    q = slice(64 * b, 64 * b + 64)
                    step(dve.tensor_copy(m_t[q, :, 4 * n:4 * n + 4].rearrange("p i d -> p d i"),
                                         ps_turn[q, 2 + n, :].rearrange("p (d i b) -> p d i b", d=4, b=2)[:, :, :, b]))

        @block.tensor
        def _(pe):
            for e in range(D):
                mm = pe.matmul(ps_turn[:, e // 4, 128 * (e % 4):128 * (e % 4) + 128], gram[:, :, e], k["ident"][:], start=True, stop=True)
                if e % 4 == 3:
                    mm.then_inc(turned, 1)

            def queries_keys(c, a):
                if later(c, 2):
                    pe.wait_ge(qk_out, 2 * (c - 1))
                for s in range(2):
                    pe.matmul(ps_turn[:, 4 + 2 * a + s, 0:CP * NP], k["w_bd"][:, s, :], xn[:, span(c, CP), :], start=True, stop=True).then_inc(qk_done, 1)

            staggered(pe, NCH, [(0, queries_keys)])
            pe.wait_ge(qk_out, 2 * NCH)
            for n, (l, lo, hi) in enumerate(EXPERT_BANKS):
                pe.wait_ge(experts_in[l], 32)
                if n >= 4:
                    pe.wait_ge(experts_out, n - 3)
                if n >= LAYERS:
                    pe.wait_ge(experts_out, l + 1)
                bank = ps_turn[:, 4 + n % 4, 0:HID * (hi - lo)]
                if lo == EXP:
                    pe.matmul(bank, wr_in[:, l, EXP, :], k["ident"][:], start=True, stop=False)
                    mm = pe.matmul(bank, k["ident"][:], k["ident"][:], start=False, stop=True)
                else:
                    pe.matmul(bank, k["ident"][:], k["ffn_w"][:, EXP:EXP + 1, l, 0:HID].broadcast_to([128, hi - lo, HID]),
                              start=True, stop=False, skip_group_check=True)
                    for e in range(lo, hi):
                        mm = pe.matmul(bank[:, HID * (e - lo):HID * (e - lo) + HID], wr_in[:, l, e, :], k["ident"][:],
                                       start=False, stop=True, skip_group_check=True)
                mm.then_inc(experts_done, 1)
            pe.wait_ge(dve_step, marks["m"])
            for d in range(D):
                mm = pe.transpose(ps_turn[:, 2 + d // 4, 128 * (d % 4):128 * (d % 4) + 128],
                                  m_sum[:, d].rearrange("p b h e -> p (b h e)"), k["ident"][:])
                if d % 4 == 3:
                    mm.then_inc(m_turned, 1)


EXPERT_BANKS = [(l, EXP, EXP + 1) for l in range(LAYERS)] + [(l, e, e + 4) for l in range(LAYERS) for e in range(0, EXP, 4)]
DIAG_STEP = 2 + 6 * (D - 1) + 1


def attend(nc, q_cm, k_cm, m_t, o_cm, v_dram, k):
    sem = nc.semaphore
    N2 = 2 * N
    with ExitStack() as ctx:
        names = ("q_zero q_ready m_ready keys_ready turned_ready v_ready kt_done kt_out dots_done squared mixed keys_used "
                 "max_done max_turned max_ready max_spread max_out sub_done exp_done sum_done av_done inv_done out_done blk_zero r_done")
        s = {n: ctx.enter_context(sem(n)) for n in names.split()}
        v_in = [ctx.enter_context(sem(f"v_in{a}")) for a in range(2)]

        def sb(name, shape):
            return ctx.enter_context(nc.sbuf_tensor(name, shape, F32))

        m_blk = sb("m_blk", [128, 2, 16, D])
        k_blk = sb("k_blk", [128, 2, NTAU, 2, H, 8])
        k_mix = sb("k_mix", [128, 2, NT, 2, H, 8])
        v_rep = sb("v_rep", [128, 2, 2, NT * C])
        v_blk = sb("v_blk", [128, 2, 2, NT, C])
        k_turn = sb("k_turn", [128, 2, NP])
        q_z = sb("q_z", [128, 2, N2])
        sq = sb("sq", [128, 6, 2 * N2])
        top = sb("row_max", [128, N2])
        top16 = sb("row_max16", [N, 2, 2, H])
        top_e = sb("row_max_e", [N, 2, H, 8])
        shift = sb("shift", [128, N2])
        prob = sb("prob", [128, NT, N2])
        sums = sb("sums", [128, 2, N2])
        inv = sb("inv", [128, N])
        ps_dot = ctx.enter_context(nc.psum_tensor("ps_dot", [128, 2, 512], F32))
        ps_a = ctx.enter_context(nc.psum_tensor("ps_a", [128, 3, 512], F32))
        ps_x = ctx.enter_context(nc.psum_tensor("ps_x", [128, 512], F32))
        ps_b = ctx.enter_context(nc.psum_tensor("ps_b", [128, 512], F32))
        ps_o = ctx.enter_context(nc.psum_tensor("ps_o", [128, 512], F32))
        block = ctx.enter_context(nc.Block())

        def steps(eng, step):
            step(0, 0, False, True)
            step(1, 1, True, True)
            with eng.Fori(1, PAIRS // 2 - 1) as twice:
                step(2 * twice, 0, True, True)
                step(2 * twice + 1, 1, True, True)
            step(PAIRS - 2, 0, True, True)
            step(PAIRS - 1, 1, True, False)

        @block.sync
        def _(sp):
            def load(i, a):
                if not isinstance(i, int):
                    sp.wait_ge(s["v_ready"], i - 1)
                for b in range(2):
                    src = v_dram[span(2 * i + b, 1)].rearrange("b (mj mi t) f -> mi mj (b t f)", mi=2, t=NT)
                    for mi in range(2):
                        sp.dma_start(v_rep[64 * mi:64 * mi + 64, a, b, :], src[mi].unsqueeze(0).broadcast_to([8, 8, NT * C])).then_inc(v_in[a], 16)

            load(0, 0)
            load(1, 1)
            with sp.Fori(1, (PAIRS) // 2) as twice:
                i = twice * 2
                load(i, 0)
                load(i + 1, 1)

        @block.gpsimd
        def _(pool):
            def build(i, a, n):
                pool.tensor_tensor(m_blk[:, a], m_t[:, span(i, 1), :].broadcast_to([128, 16, D]),
                                   k["mask16"][:].unsqueeze(2).broadcast_to([128, 16, D]), ALU.mult).then_inc(s["m_ready"], 1)
                if not (isinstance(i, int) and i < 2):
                    pool.wait_ge(s["keys_used"], i - 1)
                key = k_cm[:, span(i, 1), :].rearrange("p i (mj tau) -> p (i tau) mj", tau=NTAU)
                heads = k["hmask"][:].unsqueeze(1).unsqueeze(3)

                def blocked(kind, view):
                    return pool.tensor_tensor(k_blk[:, a, :, kind], view.unsqueeze(2).broadcast_to([128, NTAU, H, 8]),
                                              heads.broadcast_to([128, NTAU, H, 8]), ALU.mult)

                def turned():
                    pool.wait_ge(s["kt_out"], i + 1)
                    blocked(1, k_turn[:, a].rearrange("p (mj tau) -> p tau mj", tau=NTAU)).then_inc(s["turned_ready"], 1)

                blocked(0, key).then_inc(s["keys_ready"], 1)
                first = isinstance(i, int) and i == 0
                if first:
                    turned()
                for mi in range(2):
                    pool.tensor_tensor(k_mix[:, a, :, mi], key[:, NT * mi:NT * mi + NT].unsqueeze(2).broadcast_to([128, NT, H, 8]),
                                       k["conv1"].unsqueeze(1).unsqueeze(3).broadcast_to([128, NT, H, 8]), ALU.mult).then_inc(s["keys_ready"], 1)
                if not first:
                    turned()
                pool.wait_ge(v_in[a], 64 * (n + 1))
                if not (isinstance(i, int) and i < 2):
                    pool.wait_ge(s["av_done"], i - 1)
                for b in range(2):
                    mm = pool.tensor_tensor(v_blk[:, a, b].rearrange("p t (o d) -> p (t o) d", o=H),
                                            v_rep[:, a, b].rearrange("p (t o d) -> p (t o) d", o=H, t=NT),
                                            k["vmask"][:].rearrange("p t o -> p (t o)").unsqueeze(2).broadcast_to([128, NT * H, D]), ALU.mult)
                mm.then_inc(s["v_ready"], 1)

            build(0, 0, 0)
            build(1, 1, 0)
            with pool.Fori(1, (PAIRS) // 2) as twice:
                i = twice * 2
                build(i, 0, twice)
                build(i + 1, 1, twice)

        @block.tensor
        def _(pe):
            def turn_keys(i, a):
                pe.wait_ge(s["m_ready"], i + 1)
                pe.wait_ge(s["kt_out"], i)
                pe.matmul(ps_x[:, 256:256 + NP], m_blk[:, a].rearrange("p q d -> p (q d)"), k_cm[:, span(i, 1), :],
                          start=True, stop=True).then_inc(s["kt_done"], 1)

            def soft(prev, a, part):
                if part == 0:
                    pe.wait_ge(s["max_done"], prev + 1)
                    for b in range(2):
                        mm = pe.transpose(ps_x[0:N, 128 * b:128 * b + 128], top[:, N * b:N * b + N], k["ident"][:])
                    mm.then_inc(s["max_turned"], 1)
                if part == 1:
                    pe.wait_ge(s["max_ready"], prev + 1)
                    for mi in range(2):
                        for b in range(2):
                            mm = pe.matmul(ps_b[64 * mi:64 * mi + 64, N * b:N * b + N], top_e[:, b].rearrange("p o m -> p (o m)"),
                                           k["ident"][0:N, 0:N], start=True, stop=True)
                    mm.then_inc(s["max_spread"], 1)
                if part == 2:
                    pe.wait_ge(s["exp_done"], prev + 1)
                    pe.wait_ge(s["v_ready"], prev + 1)
                    pe.wait_ge(s["out_done"], prev)
                    for t in range(NT):
                        for b in range(2):
                            pe.matmul(ps_o[64 * b:64 * b + 64, 0:N], v_blk[:, a, b, t, :], prob[:, t, N * b:N * b + N],
                                      start=(t == 0), stop=(t == NT - 1))
                    pe.wait_ge(s["sum_done"], prev + 1)
                    for n in range(2):
                        for b in range(2):
                            mm = pe.matmul(ps_o[64 * b:64 * b + 64, NP:NP + N], k["den_w"][:, n, :], sums[:, n, N * b:N * b + N],
                                           start=(n == 0), stop=(n == 1))
                    mm.then_inc(s["av_done"], 1)

            def step(i, a, has_prev, has_next):
                prev = i - 1
                pe.wait_ge(s["q_ready"], i + 1)
                pe.wait_ge(s["keys_ready"], 3 * i + 1)
                pe.wait_ge(s["turned_ready"], i + 1)
                for g in range(6):
                    j, mi = divmod(g, 2)
                    if has_prev or g >= 2:
                        pe.wait_ge(s["squared"], 6 * i + g - 1)
                    for t in (2 * j, 2 * j + 1):
                        mm = pe.matmul(ps_dot[:, g % 2, N2 * (t % 2):N2 * (t % 2) + N2],
                                       k_blk[:, a, mi * NT + t].rearrange("p k h m -> p (k h m)"), q_z[:, a, :], start=True, stop=True)
                    mm.then_inc(s["dots_done"], 1)
                    if has_prev and g == 0:
                        soft(prev, 1 - a, 0)
                    if has_prev and g == 2:
                        soft(prev, 1 - a, 1)
                    if has_next and g == 3:
                        turn_keys(i + 1, 1 - a)
                if has_prev:
                    pe.wait_ge(s["sub_done"], prev + 1)
                pe.wait_ge(s["keys_ready"], 3 * (i + 1))
                for j in range(3):
                    for t in (2 * j, 2 * j + 1):
                        mm = pe.matmul(ps_a[:, j, N2 * (t % 2):N2 * (t % 2) + N2], k_mix[:, a, t].rearrange("p q o m -> p (q o m)"),
                                       q_z[:, a, :], start=(t % 2 == 0), stop=False, skip_group_check=True)
                mm.then_inc(s["keys_used"], 1)
                for j in range(3):
                    for mi in range(2):
                        pe.wait_ge(s["squared"], 6 * i + 2 * j + mi + 1)
                        mm = pe.matmul(ps_a[64 * mi:64 * mi + 64, j, 0:2 * N2], k["mix_w"][:], sq[:, 2 * j + mi, :],
                                       start=False, stop=True, skip_group_check=True)
                mm.then_inc(s["mixed"], 1)
                if has_prev:
                    soft(prev, 1 - a, 2)

            turn_keys(0, 0)
            steps(pe, step)
            soft(PAIRS - 1, 1, 0)
            soft(PAIRS - 1, 1, 1)
            soft(PAIRS - 1, 1, 2)

        @block.scalar
        def _(act):
            def turned_out(i, a):
                act.wait_ge(s["kt_done"], i + 1)
                if not (isinstance(i, int) and i < 2):
                    act.wait_ge(s["turned_ready"], i - 1)
                act.activation(k_turn[:, a, :], ps_x[:, 256:256 + NP], ACT.Copy).then_inc(s["kt_out"], 1)

            def shift_out(prev):
                act.wait_ge(s["max_spread"], prev + 1)
                act.wait_ge(s["sub_done"], prev)
                act.activation(shift[:], ps_b[:, 0:N2], ACT.Identity, bias=k["conv_const"]).then_inc(s["max_out"], 1)

            def exps(prev):
                act.wait_ge(s["sub_done"], prev + 1)
                act.activation(prob[:], prob[:], ACT.Exp, bias=k["conv_const"]).then_inc(s["exp_done"], 1)

            def step(i, a, has_prev, has_next):
                for g in range(6):
                    if has_prev and g == 0:
                        act.wait_ge(s["mixed"], i)
                    act.wait_ge(s["dots_done"], 6 * i + g + 1)
                    act.activation(sq[:, g, :], ps_dot[:, g % 2, 0:2 * N2], ACT.Square).then_inc(s["squared"], 1)
                    if has_prev and g == 2:
                        shift_out(i - 1)
                    if has_next and g == 3:
                        turned_out(i + 1, 1 - a)
                if has_prev:
                    exps(i - 1)

            turned_out(0, 0)
            steps(act, step)
            shift_out(PAIRS - 1)
            exps(PAIRS - 1)

        @block.vector
        def _(dve):
            def queries(i, a):
                if not (isinstance(i, int) and i < 2):
                    dve.wait_ge(s["keys_used"], i - 1)
                for b in range(2):
                    q = slice(64 * b, 64 * b + 64)
                    cp = dve.tensor_copy(q_z[q, a, N * b:N * b + N], q_cm[q, span(i, 1), 0:N])
                cp.then_inc(s["q_ready"], 1)

            def maxima(prev):
                dve.wait_ge(s["mixed"], prev + 1)
                dve.wait_ge(s["max_turned"], prev)
                dve.tensor_reduce(top[:], ps_a[:, :, 0:2 * N2].rearrange("p j (t n) -> p n j t", t=2), AX.XY, ALU.max).then_inc(s["max_done"], 1)
                dve.wait_ge(s["max_turned"], prev + 1)
                dve.tensor_reduce(top16[:].rearrange("p b m o -> p (b m o)"), ps_x[0:N, 0:256].rearrange("p (q m) -> p q m", m=8),
                                  AX.X, ALU.max).then_inc(s["r_done"], 1)
                dve.wait_ge(s["r_done"], prev + 1)
                dve.wait_ge(s["max_spread"], prev)
                dve.tensor_tensor(top_e[:], top16[:, :, 0].unsqueeze(3).broadcast_to([N, 2, H, 8]),
                                  top16[:, :, 1].unsqueeze(3).broadcast_to([N, 2, H, 8]), ALU.max).then_inc(s["max_ready"], 1)

            def output(i):
                dve.wait_ge(s["av_done"], i + 1)
                dve.reciprocal(inv[:], ps_o[:, NP:NP + N]).then_inc(s["inv_done"], 1)
                dve.wait_ge(s["inv_done"], i + 1)
                dve.tensor_tensor(o_cm[:, span(i, 1), 0:N].rearrange("p i n -> p (i n)"), ps_o[:, 0:N], inv[:], ALU.mult).then_inc(s["out_done"], 1)

            def shifted(prev, first=False):
                dve.wait_ge(s["max_out"], prev + 1)
                dve.wait_ge(s["av_done"], prev)
                dve.tensor_tensor(prob[:].rearrange("p (j t) n -> p j t n", t=2), ps_a[:, :, 0:2 * N2].rearrange("p j (t n) -> p j t n", t=2),
                                  shift[:].unsqueeze(1).unsqueeze(1).broadcast_to([128, 3, 2, N2]), ALU.subtract).then_inc(s["sub_done"], 1)

            def sums_of(prev):
                dve.wait_ge(s["exp_done"], prev + 1)
                dve.tensor_reduce(sums[:, 0, :], prob[:, 0:4, :].rearrange("p t n -> p n t"), AX.X, ALU.add)
                dve.tensor_tensor(sums[:, 1, :], prob[:, 4, :], prob[:, 5, :], ALU.add).then_inc(s["sum_done"], 1)

            def step(i, a, has_prev, has_next):
                if has_prev:
                    maxima(i - 1)
                if has_next:
                    queries(i + 1, 1 - a)
                if has_prev:
                    shifted(i - 1)
                    if has_prev == "two":
                        output(i - 2)
                    sums_of(i - 1)

            dve.memset(q_z[:], 0.0).then_inc(s["q_zero"], 1)
            dve.wait_ge(s["q_zero"], 1)
            queries(0, 0)
            step(0, 0, False, True)
            step(1, 1, True, True)
            with dve.Fori(1, (PAIRS) // 2 - 1) as twice:
                i = twice * 2
                step(i, 0, "two", True)
                step(i + 1, 1, "two", True)
            step(PAIRS - 2, 0, "two", True)
            step(PAIRS - 1, 1, "two", False)
            maxima(PAIRS - 1)
            shifted(PAIRS - 1)
            output(PAIRS - 2)
            sums_of(PAIRS - 1)
            output(PAIRS - 1)


LAYER_BANKS = (4, 5, 1, 2)


def feed_forward(nc, h1, xc, rstd_t, out, k):
    sem = nc.semaphore
    with ExitStack() as ctx:
        names = ("masked rstd_done xn_done hid_done hid_out sel_done lay_done even_out odd_out "
                 "wo_done summed turned row_out")
        s = {n: ctx.enter_context(sem("f_" + n)) for n in names.split()}
        stored = [ctx.enter_context(sem(f"out_stored{a}")) for a in range(2)]

        def sb(name, shape):
            return ctx.enter_context(nc.sbuf_tensor(name, shape, F32))

        rstd_of = sb("f_rstd_of", [128, 2, CP, N])
        xn = sb("f_xn", [128, 2, CP, N])
        hid = sb("hid", [128, 3, 2, CP, N])
        w_sel = sb("w_sel", [128, 2, CP, LAYERS, HID + 1])
        final = sb("final", [128, CP, N])
        rows = sb("rows", [N, 2, CP, 2 * C])
        ps = ctx.enter_context(nc.psum_tensor("ps_f", [128, 8, 512], F32))
        block = ctx.enter_context(nc.Block())
        W = CP * N
        TURN_BANK, WO_BANK = 0, 6

        def flat(view):
            return view.rearrange("p r m -> p (r m)")

        @block.sync
        def _(sp):
            def store(c, a):
                sp.wait_ge(s["row_out"], c + 1)
                sp.dma_start(out[span(c, 2 * CP)].rearrange("b n f -> n b f"),
                             rows[:, a].rearrange("n r (b f) -> n (r b) f", b=2)).then_inc(stored[a], 16)

            staggered(sp, NCH, [(0, store)])
            for a in range(2):
                sp.wait_ge(stored[a], 16 * NCH // 2)

        @block.gpsimd
        def _(pool):
            def select(c, a):
                if later(c, 2):
                    pool.wait_ge(s["rstd_done"], c - 1)
                pool.tensor_tensor(rstd_of[:, a], rstd_t[:, 0:N].unsqueeze(1).broadcast_to([128, CP, N]),
                                   k["pair_mask"][:, span(c, CP)].unsqueeze(2).broadcast_to([128, CP, N]), ALU.mult).then_inc(s["masked"], 1)
                if later(c, 2):
                    for values in (s["even_out"], s["odd_out"]):
                        pool.wait_ge(values, CP * (c - 1))
                for r in range(CP):
                    e = pool.value_load(k["route"][0:1, span(c * CP + r, 1)], min_val=0, max_val=EXP)
                    pool.tensor_copy(w_sel[:, a, r].rearrange("p l f -> p (l f)"),
                                     k["ffn_w"][:, bass.ds(e, 1)].rearrange("p e l f -> p (e l f)")).then_inc(s["sel_done"], 1)

            staggered(pool, NCH, [(0, select)])

        @block.tensor
        def _(pe):
            def spread(c, a):
                pe.wait_ge(s["masked"], c + 1)
                if later(c, 3):
                    pe.wait_ge(s["row_out"], c - 2)
                if later(c, 1):
                    pe.wait_ge(s["xn_done"], c)
                pe.matmul(ps[:, TURN_BANK, 0:W], k["batch_sel"][:], flat(rstd_of[:, a]), start=True, stop=True).then_inc(s["rstd_done"], 1)

            def hidden(c, a):
                pe.wait_ge(s["xn_done"], c + 1)
                pe.wait_ge(s["hid_out"], 2 * c)
                for b in range(2):
                    pe.matmul(ps[:, (3, 7)[b], 0:W], k["wi_bd"][:, b, :], flat(xn[:, a]), start=True, stop=True).then_inc(s["hid_done"], 1)

            def layers(c, a):
                pe.wait_ge(s["hid_out"], 2 * c + 2)
                for u in range(2 * CP):
                    l, r = divmod(u, CP)
                    values = s["odd_out" if r % 2 else "even_out"]
                    if l == 0:
                        pe.wait_ge(s["sel_done"], CP * c + r + 1)
                        pe.wait_ge(values, CP * c)
                    else:
                        pe.wait_ge(values, CP * c + r // 2 + 1)
                    pe.matmul(ps[:, LAYER_BANKS[r], 0:2 * N], w_sel[:, a, r, l, 0:HID], hid[:, l, :, r, :],
                              start=True, stop=True).then_inc(s["lay_done"], 1)

            def project_out(c, a):
                for values in (s["even_out"], s["odd_out"]):
                    pe.wait_ge(values, CP * (c + 1))
                pe.wait_ge(s["summed"], c)
                for b in range(2):
                    mm = pe.matmul(ps[64 * b:64 * b + 64, WO_BANK, 0:W], k["wo_t"][:], flat(hid[:, 2, b]), start=True, stop=True)
                mm.then_inc(s["wo_done"], 1)

            def turn(c, a):
                pe.wait_ge(s["summed"], c + 1)
                pe.wait_ge(s["xn_done"], min(c + 3, NCH) if isinstance(c, int) else c + 3)
                pe.wait_ge(s["row_out"], c)
                for r in range(CP):
                    mm = pe.transpose(ps[0:N, TURN_BANK, 2 * C * r:2 * C * r + 2 * C], final[:, r, :], k["ident"][:])
                mm.then_inc(s["turned"], 1)

            staggered(pe, NCH, [(1, hidden), (2, project_out), (0, spread), (1, layers), (2, turn)])

        @block.scalar
        def _(act):
            def hidden_out(c, a):
                act.wait_ge(s["lay_done"], 2 * CP * c)
                act.wait_ge(s["hid_done"], 2 * c + 1)
                act.activation(flat(hid[:, 0, 0]), ps[:, 3, 0:W], ACT.Relu, bias=k["ffn_bias"][:, 34:35]).then_inc(s["hid_out"], 1)

            def even(c, a):
                for u in range(0, 2 * CP, 2):
                    l, r = divmod(u, CP)
                    act.wait_ge(s["lay_done"], 2 * CP * c + u + 1)
                    if l:
                        act.wait_ge(s["wo_done"], c)
                    act.activation(hid[:, l + 1, :, r, :], ps[:, LAYER_BANKS[r], 0:2 * N].rearrange("p (b n) -> p b n", b=2), ACT.Relu,
                                   bias=w_sel[:, a, r, l, HID:HID + 1]).then_inc(s["even_out"], 1)

            def rows_out(c, a):
                act.wait_ge(s["turned"], c + 1)
                if later(c, 2):
                    act.wait_ge(stored[a], 8 * (c - a))
                act.activation(rows[:, a].rearrange("p r f -> p (r f)"), ps[0:N, TURN_BANK, :], ACT.Copy).then_inc(s["row_out"], 1)

            staggered(act, NCH, [(1, hidden_out), (1, even), (2, rows_out)])

        @block.vector
        def _(dve):
            def hidden_out(c, a):
                dve.wait_ge(s["lay_done"], 2 * CP * c)
                dve.wait_ge(s["hid_done"], 2 * c + 2)
                dve.tensor_scalar(flat(hid[:, 0, 1]), ps[:, 7, 0:W], k["ffn_bias"][:, 34:35], 0.0, ALU.add, ALU.max).then_inc(s["hid_out"], 1)

            def residual(c, a):
                dve.wait_ge(s["wo_done"], c + 1)
                dve.wait_ge(s["turned"], c)
                dve.scalar_tensor_tensor(out=final[:], in0=ps[:, WO_BANK, 0:W].rearrange("p (r n) -> p r n", r=CP), scalar=k["out_bias"],
                                         in1=h1[:, span(c, CP), 0:N], op0=ALU.add, op1=ALU.add).then_inc(s["summed"], 1)

            def normed(c, a):
                dve.wait_ge(s["rstd_done"], c + 1)
                if later(c, 2):
                    dve.wait_ge(s["hid_done"], 2 * (c - 1))
                dve.tensor_tensor(xn[:, a], xc[:, span(c, CP), 0:N], ps[:, TURN_BANK, 0:W].rearrange("p (r n) -> p r n", r=CP),
                                  ALU.mult).then_inc(s["xn_done"], 1)

            def odd(c, a):
                for u in range(1, 2 * CP, 2):
                    l, r = divmod(u, CP)
                    dve.wait_ge(s["lay_done"], 2 * CP * c + u + 1)
                    if l:
                        dve.wait_ge(s["wo_done"], c)
                    dve.tensor_scalar(hid[:, l + 1, :, r, :], ps[:, LAYER_BANKS[r], 0:2 * N].rearrange("p (b n) -> p b n", b=2),
                                      w_sel[:, a, r, l, HID:HID + 1], 0.0, ALU.add, ALU.max).then_inc(s["odd_out"], 1)

            staggered(dve, NCH, [(1, hidden_out), (2, residual), (0, normed), (1, odd)])


def audio_layer(nc, p, out, debug=None):
    with ExitStack() as ctx:
        def sb(name, shape, dt=F32):
            return ctx.enter_context(nc.sbuf_tensor(name, shape, dt))

        cols = sb("cols", [128, 56])
        k = {
            "ident": sb("ident", [128, 128]), "mask4": sb("mask4", [128, 4]),
                        "mean_w": sb("mean_w", [128, 128]), "w_bd": sb("w_bd", [128, 4, 128]), "w_tok": sb("w_tok", [128, 2, 192]),
            "pair_mask": sb("pair_mask", [128, PAIRS]), "batch_sel": sb("batch_sel", [128, 128]),
            "wi_bd": sb("wi_bd", [128, 2, HID]), "wo_t": sb("wo_t", [128, C]), "mask16": sb("mask16", [128, 16]),
            "delta_q": sb("delta_q", [128, 16, 8]), "delta": sb("delta", [128, 8]), "hmask": sb("hmask", [128, 8]),
            "mix_w": sb("mix_w", [128, 64]), "cols": cols, "conv1": cols[:, 16:24], "conv_const": cols[:, 12:13],
            "vmask": sb("vmask", [128, NT, H]), "den_w": sb("den_w", [128, 2, 64]), "tok_bias": cols[:, 4:5],
            "qkv_bias": cols[:, 0:3], "proj_bias": cols[:, 3:4], "ln_eps": sb("ln_eps", [128, 1]),
            "bias_row": sb("bias_row", [96, 2, 192]), "out_bias": cols[:, 13:14],
            "ffn_w": sb("ffn_w", [128, EXP + 1, LAYERS, HID + 1]), "ffn_bias": sb("ffn_bias", [128, 35]),
            "route_in": sb("route_in", [1, PAIRS], I32), "route": sb("route", [1, PAIRS], I32),
        }
        tokens = sb("tokens", [128, PAIRS, NP])
        v_dram = nc.dram_tensor("v_rows", (B, NP, C), F32).ap()
        top_dram = nc.dram_tensor("top_rows", (B, D, 2 * C), F32).ap()

        with ExitStack() as first:
            x_g = first.enter_context(nc.sbuf_tensor("x_g", [128, 2, GP, TP], F32))
            k["score_w"] = first.enter_context(nc.sbuf_tensor("score_w", [128, GP, 32], F32))
            k["pair_sel"] = first.enter_context(nc.sbuf_tensor("pair_sel", [128, 2, GP, 128], BF16))
            ps_score = first.enter_context(nc.psum_tensor("ps_score", [128, 512], F32))
            x_in = [[first.enter_context(nc.semaphore(f"x_in{a}{q}")) for q in range(GROUP_LOADS)] for a in range(2)]
            constants(nc, p, x_g, x_in, ps_score, k)
            pool_windows(nc, p["x"], x_g, x_in, ps_score, tokens, k)
        with nc.sbuf_tensor("q_cm", [128, PAIRS, NP], F32) as q_cm, nc.sbuf_tensor("k_cm", [128, PAIRS, NP], F32) as k_cm, \
                nc.sbuf_tensor("m_t", [128, PAIRS, D], F32) as m_t, nc.sbuf_tensor("rstd_t", [128, NP], F32) as rstd_t:
            with nc.sbuf_tensor("gram", [128, B, D], F32) as gram:
                with nc.sbuf_tensor("xc", [128, PAIRS, NP], F32) as xc:
                    centre(nc, tokens, xc, rstd_t, NP, k)
                    project(nc, xc, rstd_t, gram, v_dram, top_dram, k)
                    orthogonalise(nc, p, gram, m_t, top_dram, xc, q_cm, k_cm, k)
            attend(nc, q_cm, k_cm, m_t, q_cm, v_dram, k)
            centre(nc, tokens, k_cm, rstd_t, N, k, q_cm)
            feed_forward(nc, tokens, k_cm, rstd_t, out, k)


def laid_out(given):
    g = {name.replace("L0_", "").replace("attn_", "").replace("ffn_", ""): np.asarray(a) for name, a in given.items()}

    def col(a):
        return np.asarray(a).reshape(-1, 1)

    def by_head(a):
        return np.tile(np.repeat(a, 8, axis=0), (2, 1))

    wide = np.repeat(np.asarray(g["conv_w"]).T[H:3 * H], 8, axis=0)
    columns = [
        np.tile(g["b_qkv"].reshape(3, C).T, (2, 1)),
        np.tile(col(g["b_proj"]), (2, 1)),
        np.repeat(col(g["tok_b"]), 128, axis=0),
        np.tile(col(g["tok_w"]), (2, 1)),
        np.repeat(col(g["scale"]), 128, axis=0),
        np.repeat(np.concatenate([col(g["riem_scale"]), col(g["grassman_scale"])]), 64, axis=0),
        by_head(col(g["bn_gamma"][0:H])), by_head(col(g["bn_var"][0:H])),
        np.repeat(col(g["bn_gamma"][H:3 * H]), 8, axis=0), np.repeat(col(g["bn_var"][H:3 * H]), 8, axis=0),
        by_head(col(g["conv_b"])),
        np.tile(col(g["bo"]), (2, 1)),
        np.zeros((128, 2), np.float32),
        by_head(g["conv_w"].T[0:H]),
        wide,
        by_head(g["conv_w"]),
    ]
    square = np.concatenate([g["w_qkv"].reshape(3, C, C), g["w_proj"][None]]).transpose(1, 0, 2)
    rows = [np.tile(g["b_qkv"], 2), g["bn_gamma"], g["bn_beta"], g["bn_mean"], g["bn_var"]]
    return {
        "x": g["x"], "columns": np.concatenate(columns, axis=1), "square": np.tile(square, (2, 1, 1)),
        "rows": np.concatenate(rows).reshape(1, -1), "Wi": g["Wi"], "Wo": g["Wo"], "Wr": g["Wr"], "Ws": g["Ws"],
        "biases": np.concatenate([g["br"].reshape(-1, HID), g["bs"].reshape(-1, HID), g["bi"].reshape(1, HID)]),
        "route_id": g["route_id"].reshape(1, PAIRS),
    }


def kernel(**inputs):
    import numpy as _np
    import concourse.bacc as _bacc
    from concourse import mybir as _mybir
    from concourse.bass_utils import run_bass_kernel_spmd as _run

    nc = _bacc.Bacc("TRN2", target_bir_lowering=False, num_devices=1)
    arrays, p = {}, {}
    for name, a in laid_out(inputs).items():
        a = _np.ascontiguousarray(a)
        arrays[f"in_{name}_dram"] = a
        p[name] = nc.dram_tensor(f"in_{name}_dram", a.shape, _mybir.dt.from_np(a.dtype), kind="ExternalInput").ap()
    out = nc.dram_tensor("out_0_dram", (B, N, C), F32, kind="ExternalOutput").ap()
    audio_layer(nc, p, out)
    r = _run(nc, [arrays], core_ids=[0])
    return r.results[0]["out_0_dram"]
```
